# Optimizing a Trainium2 kernel written in Bass

```python
import numpy as np
import jax
import jax.numpy as jnp

def _softmax(x, axis=-1):
    return jax.nn.softmax(x, axis=axis)

def _gelu(x):
    return jax.nn.gelu(x, approximate=True)

def _silu(x):
    return jax.nn.silu(x)

def _sigmoid(x):
    return jax.nn.sigmoid(x)

def _layernorm(x, axis=-1, eps=1e-05):
    m = jnp.mean(x, axis=axis, keepdims=True)
    v = jnp.var(x, axis=axis, keepdims=True)
    return (x - m) / jnp.sqrt(v + eps)

def _scatter_add(tgt, idx, src, axis=0):
    return tgt.at[idx].add(src)

def _segment_sum(src, seg, n):
    return jax.ops.segment_sum(src, seg, n)
kernel_name = 'mk_gps_d1_gnn_r8_f2d083'

def setup_inputs(seed: int=0):
    np.random.seed(seed)
    _w = jnp.asarray

    def _rec_inputs():
        import jax
        import jax.numpy as jnp
        _gk = jax.random.key(seed)
        x = -0.0003713 + 1 * jax.random.normal(jax.random.fold_in(_gk, 1), (6250, 256), jnp.float32)
        src = jax.random.randint(jax.random.fold_in(_gk, 2), (100000,), 0, 6250, jnp.int32)
        dst = jnp.minimum((6250 * jax.random.uniform(jax.random.fold_in(_gk, 3), (100000,)) ** 2.0).astype(jnp.int32), 49999)
        _o = jnp.argsort(dst, stable=True)
        src = src[_o]
        dst = dst[_o]
        edge_type_4 = jax.random.randint(jax.random.fold_in(_gk, 12), (100000,), 0, 4, jnp.int32)
        return (x, src, dst, edge_type_4)
    x, src, dst, edge_type_4 = _rec_inputs()

    def _L0_gnn_setup():
        import jax, jax.numpy as jnp
        import numpy as np
        N = 6250
        E = 100000
        IN = 256
        H = 4
        C = 64
        NUM_EDGE_TYPES = 4
        key = jax.random.key(seed)
        ks = jax.random.split(key, 12)
        s = 1.0 / np.sqrt(IN)
        return {'x': jax.random.normal(ks[0], (N, IN), jnp.float32), 'edge_index': jax.random.randint(ks[1], (2, E), 0, N, jnp.int64), 'edge_type_ids': jax.random.randint(ks[2], (E,), 0, NUM_EDGE_TYPES, jnp.int64), 'edge_emb': jax.random.normal(ks[3], (NUM_EDGE_TYPES, IN), jnp.float32), 'Wq': jax.random.uniform(ks[4], (IN, H * C), jnp.float32, -s, s), 'bq': jnp.zeros((H * C,), jnp.float32), 'Wk': jax.random.uniform(ks[5], (IN, H * C), jnp.float32, -s, s), 'bk': jnp.zeros((H * C,), jnp.float32), 'Wv': jax.random.uniform(ks[6], (IN, H * C), jnp.float32, -s, s), 'bv': jnp.zeros((H * C,), jnp.float32), 'Ws': jax.random.uniform(ks[7], (IN, H * C), jnp.float32, -s, s), 'bs': jnp.zeros((H * C,), jnp.float32)}
    _L0_gnn_all = _L0_gnn_setup()
    _L0_gnn_in = {k: v for k, v in _L0_gnn_all.items() if k in ('edge_emb', 'Wq', 'bq', 'Wk', 'bk', 'Wv', 'bv', 'Ws', 'bs')}
    del _L0_gnn_all

    def _L0_mix_setup():
        import jax, jax.numpy as jnp
        import numpy as np
        DIM = 256
        HEADS = 4
        HEAD_DIM = DIM // HEADS
        MLP_HIDDEN = DIM * 3
        B, N = (8, 512)
        EPS = 1e-05

        def _layernorm(x, g, b):
            mu = jnp.mean(x, axis=-1, keepdims=True)
            var = jnp.mean(jnp.square(x - mu), axis=-1, keepdims=True)
            return (x - mu) * jax.lax.rsqrt(var + EPS) * g + b
        key = jax.random.key(seed)
        ks = jax.random.split(key, 8)
        s = 0.02
        return {'x': jax.random.normal(ks[0], (B, N, DIM), dtype=jnp.float32), 'w_qkv': jax.random.normal(ks[1], (DIM, 3 * DIM), dtype=jnp.float32) * s, 'b_qkv': jnp.zeros((3 * DIM,), dtype=jnp.float32), 'norm_g': jnp.ones((DIM,), dtype=jnp.float32), 'norm_b': jnp.zeros((DIM,), dtype=jnp.float32), 'w_fc1': jax.random.normal(ks[2], (DIM, MLP_HIDDEN), dtype=jnp.float32) * s, 'b_fc1': jnp.zeros((MLP_HIDDEN,), dtype=jnp.float32), 'w_fc2': jax.random.normal(ks[3], (MLP_HIDDEN, DIM), dtype=jnp.float32) * s, 'b_fc2': jnp.zeros((DIM,), dtype=jnp.float32)}
    _L0_mix_all = _L0_mix_setup()
    _L0_mix_in = {k: v for k, v in _L0_mix_all.items() if k in ('w_qkv', 'b_qkv', 'norm_g', 'norm_b', 'w_fc1', 'b_fc1', 'w_fc2', 'b_fc2')}
    del _L0_mix_all

    def _L0_ffn_setup():
        import jax, jax.numpy as jnp
        import numpy as np
        BN_EPS = 0.001

        def _bn(h, g, b, m, v):
            return g * (h - m) * jax.lax.rsqrt(v + BN_EPS) + b
        key = jax.random.key(seed)
        ks = jax.random.split(key, 8)
        B, F, Df = (256, 64, 256)
        E, H, D = (8, 256, 256)
        s1 = 1.0 / np.sqrt(Df)
        s2 = 1.0 / np.sqrt(H)
        return {'x': jax.random.normal(ks[0], (B, F, Df), jnp.float32), 'Wr': jax.random.normal(ks[1], (Df, E), jnp.float32) * s1, 'br': jnp.zeros((E,), jnp.float32), 'W1': jax.random.normal(ks[2], (E, Df, H), jnp.float32) * s1, 'b1': jnp.zeros((E, H), jnp.float32), 'g1': jnp.ones((E, H), jnp.float32), 'be1': jnp.zeros((E, H), jnp.float32), 'm1': jnp.zeros((E, H), jnp.float32), 'v1': jnp.ones((E, H), jnp.float32), 'W2': jax.random.normal(ks[3], (E, H, H), jnp.float32) * s2, 'b2': jnp.zeros((E, H), jnp.float32), 'g2': jnp.ones((E, H), jnp.float32), 'be2': jnp.zeros((E, H), jnp.float32), 'm2': jnp.zeros((E, H), jnp.float32), 'v2': jnp.ones((E, H), jnp.float32), 'Wo': jax.random.normal(ks[4], (E, H, D), jnp.float32) * s2, 'bo': jnp.zeros((E, D), jnp.float32)}
    _L0_ffn_all = _L0_ffn_setup()
    _L0_ffn_in = {k: v for k, v in _L0_ffn_all.items() if k in ('Wr', 'br', 'W1', 'b1', 'g1', 'be1', 'm1', 'v1', 'W2', 'b2', 'g2', 'be2', 'm2', 'v2', 'Wo', 'bo')}
    del _L0_ffn_all
    return {'x': x, 'src': src, 'dst': dst, 'edge_type_4': edge_type_4, 'L0_gnn_edge_emb': _L0_gnn_in['edge_emb'], 'L0_gnn_Wq': _L0_gnn_in['Wq'], 'L0_gnn_bq': _L0_gnn_in['bq'], 'L0_gnn_Wk': _L0_gnn_in['Wk'], 'L0_gnn_bk': _L0_gnn_in['bk'], 'L0_gnn_Wv': _L0_gnn_in['Wv'], 'L0_gnn_bv': _L0_gnn_in['bv'], 'L0_gnn_Ws': _L0_gnn_in['Ws'], 'L0_gnn_bs': _L0_gnn_in['bs'], 'L0_mix_w_qkv': _L0_mix_in['w_qkv'], 'L0_mix_b_qkv': _L0_mix_in['b_qkv'], 'L0_mix_norm_g': _L0_mix_in['norm_g'], 'L0_mix_norm_b': _L0_mix_in['norm_b'], 'L0_mix_w_fc1': _L0_mix_in['w_fc1'], 'L0_mix_b_fc1': _L0_mix_in['b_fc1'], 'L0_mix_w_fc2': _L0_mix_in['w_fc2'], 'L0_mix_b_fc2': _L0_mix_in['b_fc2'], 'L0_ffn_Wr': _L0_ffn_in['Wr'], 'L0_ffn_br': _L0_ffn_in['br'], 'L0_ffn_W1': _L0_ffn_in['W1'], 'L0_ffn_b1': _L0_ffn_in['b1'], 'L0_ffn_g1': _L0_ffn_in['g1'], 'L0_ffn_be1': _L0_ffn_in['be1'], 'L0_ffn_m1': _L0_ffn_in['m1'], 'L0_ffn_v1': _L0_ffn_in['v1'], 'L0_ffn_W2': _L0_ffn_in['W2'], 'L0_ffn_b2': _L0_ffn_in['b2'], 'L0_ffn_g2': _L0_ffn_in['g2'], 'L0_ffn_be2': _L0_ffn_in['be2'], 'L0_ffn_m2': _L0_ffn_in['m2'], 'L0_ffn_v2': _L0_ffn_in['v2'], 'L0_ffn_Wo': _L0_ffn_in['Wo'], 'L0_ffn_bo': _L0_ffn_in['bo']}

def reference(x, src, dst, edge_type_4, L0_gnn_edge_emb, L0_gnn_Wq, L0_gnn_bq, L0_gnn_Wk, L0_gnn_bk, L0_gnn_Wv, L0_gnn_bv, L0_gnn_Ws, L0_gnn_bs, L0_mix_w_qkv, L0_mix_b_qkv, L0_mix_norm_g, L0_mix_norm_b, L0_mix_w_fc1, L0_mix_b_fc1, L0_mix_w_fc2, L0_mix_b_fc2, L0_ffn_Wr, L0_ffn_br, L0_ffn_W1, L0_ffn_b1, L0_ffn_g1, L0_ffn_be1, L0_ffn_m1, L0_ffn_v1, L0_ffn_W2, L0_ffn_b2, L0_ffn_g2, L0_ffn_be2, L0_ffn_m2, L0_ffn_v2, L0_ffn_Wo, L0_ffn_bo):
    import jax
    import jax.numpy as jnp

    def _L0_gnn_ref(x, edge_index, edge_type_ids, edge_emb, Wq, bq, Wk, bk, Wv, bv, Ws, bs):
        import jax, jax.numpy as jnp
        import numpy as np
        N = 6250
        E = 100000
        IN = 256
        H = 4
        C = 64
        NUM_EDGE_TYPES = 4
        src, dst = (edge_index[0], edge_index[1])
        ef = edge_emb[edge_type_ids]
        esum = jax.ops.segment_sum(ef, src, num_segments=N)
        cnt = jax.ops.segment_sum(jnp.ones((ef.shape[0], 1), ef.dtype), src, num_segments=N)
        x = x + esum / jnp.maximum(cnt, 1.0)
        q = (x @ Wq + bq).reshape(N, H, C)
        k = (x @ Wk + bk).reshape(N, H, C)
        v = (x @ Wv + bv).reshape(N, H, C)
        alpha = jnp.sum(q[dst] * k[src], axis=-1) / jnp.sqrt(jnp.float32(C))
        amax = jax.ops.segment_max(alpha, dst, num_segments=N)
        amax = jnp.where(jnp.isfinite(amax), amax, 0.0)
        a = jnp.exp(alpha - amax[dst])
        denom = jax.ops.segment_sum(a, dst, num_segments=N) + 1e-16
        wv = jax.ops.segment_sum(a[:, :, None] * v[src], dst, num_segments=N)
        out = wv / denom[:, :, None]
        return out.reshape(N, H * C) + (x @ Ws + bs)

    def _L0_mix_ref(x, w_qkv, b_qkv, norm_g, norm_b, w_fc1, b_fc1, w_fc2, b_fc2):
        import jax, jax.numpy as jnp
        import numpy as np
        DIM = 256
        HEADS = 4
        HEAD_DIM = DIM // HEADS
        MLP_HIDDEN = DIM * 3
        B, N = (8, 512)
        EPS = 1e-05

        def _layernorm(x, g, b):
            mu = jnp.mean(x, axis=-1, keepdims=True)
            var = jnp.mean(jnp.square(x - mu), axis=-1, keepdims=True)
            return (x - mu) * jax.lax.rsqrt(var + EPS) * g + b
        Bx, Nx, C = x.shape
        scale = HEAD_DIM ** (-0.5)
        qkv = (x @ w_qkv + b_qkv).reshape(Bx, Nx, 3, HEADS, HEAD_DIM)
        qkv = jnp.transpose(qkv, (2, 0, 3, 1, 4))
        q, k, v = (qkv[0], qkv[1], qkv[2])
        k = k * scale
        attn = jnp.einsum('bhnd,bhne->bhde', k, v)
        attn = jax.nn.softmax(attn, axis=-1)
        xf = jnp.einsum('bhde,bhne->bhnd', attn, q)
        xf = jnp.transpose(xf, (0, 2, 1, 3)).reshape(Bx, Nx, C)
        x = x + xf
        h = _layernorm(x, norm_g, norm_b)
        h = jax.nn.gelu(h @ w_fc1 + b_fc1, approximate=False) @ w_fc2 + b_fc2
        return x + h

    def _L0_ffn_ref(x, Wr, br, W1, b1, g1, be1, m1, v1, W2, b2, g2, be2, m2, v2, Wo, bo):
        import jax, jax.numpy as jnp
        import numpy as np
        BN_EPS = 0.001

        def _bn(h, g, b, m, v):
            return g * (h - m) * jax.lax.rsqrt(v + BN_EPS) + b
        feat = jnp.mean(x, axis=0)
        w = jax.nn.softmax(feat @ Wr + br, axis=-1)
        h = jnp.einsum('bfd,edh->bfeh', x, W1) + b1
        h = jax.nn.relu(_bn(h, g1, be1, m1, v1))
        h = jnp.einsum('bfeh,ehk->bfek', h, W2) + b2
        h = jax.nn.relu(_bn(h, g2, be2, m2, v2))
        y = jnp.einsum('bfeh,ehd->bfed', h, Wo) + bo
        return jnp.einsum('bfed,fe->bfd', y, w)
    edge_index = jnp.stack([src, dst])
    xn = _layernorm(x, axis=-1)
    x = x + _L0_gnn_ref(xn, edge_index, edge_type_4, L0_gnn_edge_emb, L0_gnn_Wq, L0_gnn_bq, L0_gnn_Wk, L0_gnn_bk, L0_gnn_Wv, L0_gnn_bv, L0_gnn_Ws, L0_gnn_bs) + _L0_mix_ref(xn[None], L0_mix_w_qkv, L0_mix_b_qkv, L0_mix_norm_g, L0_mix_norm_b, L0_mix_w_fc1, L0_mix_b_fc1, L0_mix_w_fc2, L0_mix_b_fc2)[0]
    x = x + _L0_ffn_ref(_layernorm(x, axis=-1)[None], L0_ffn_Wr, L0_ffn_br, L0_ffn_W1, L0_ffn_b1, L0_ffn_g1, L0_ffn_be1, L0_ffn_m1, L0_ffn_v1, L0_ffn_W2, L0_ffn_b2, L0_ffn_g2, L0_ffn_be2, L0_ffn_m2, L0_ffn_v2, L0_ffn_Wo, L0_ffn_bo)[0]
    return x

_drawn_inputs = setup_inputs


def setup_inputs(seed=0):
    import zlib

    import numpy as np

    out = dict(_drawn_inputs(seed))
    spreads = {'L0_gnn_bq': (0.0, 0.8),
     'L0_gnn_bk': (0.0, 0.8),
     'L0_gnn_bv': (0.0, 0.1),
     'L0_gnn_bs': (0.0, 0.1),
     'L0_mix_b_qkv': (0.0, 0.1),
     'L0_mix_norm_g': (1.0, 0.6),
     'L0_mix_norm_b': (0.0, 0.8),
     'L0_mix_b_fc1': (0.0, 0.593),
     'L0_mix_b_fc2': (0.0, 0.1),
     'L0_ffn_br': (0.0, 0.504),
     'L0_ffn_b1': (0.0, 0.678),
     'L0_ffn_g1': (1.0, 0.6),
     'L0_ffn_be1': (0.0, 0.688),
     'L0_ffn_m1': (0.0, 0.67),
     'L0_ffn_v1': (1.0, 0.6),
     'L0_ffn_b2': (0.0, 0.486),
     'L0_ffn_g2': (1.0, 0.6),
     'L0_ffn_be2': (0.0, 0.509),
     'L0_ffn_m2': (0.0, 0.497),
     'L0_ffn_v2': (1.0, 0.6),
     'L0_ffn_bo': (0.0, 0.36)}
    factors = {}
    for name, (base, spread) in spreads.items():
        noise = np.random.default_rng([zlib.crc32(name.encode()), seed]).standard_normal(out[name].shape)
        drawn = base * np.exp(spread * noise) if base else spread * noise
        out[name] = jnp.asarray(drawn.astype(out[name].dtype))
    for name, factor in factors.items():
        out[name] = (out[name] * factor).astype(out[name].dtype)
    return out
```

```python
from contextlib import ExitStack

import concourse.bass as bass
from concourse import mybir

ALU = mybir.AluOpType
ACT = mybir.ActivationFunctionType
AX_X = mybir.AxisListType.X
F32 = mybir.dt.float32
BF16 = mybir.dt.bfloat16
I32 = mybir.dt.int32
U32 = mybir.dt.uint32

P = 128
BIG_NEG = -1.0e30
FAR = 1 << 20


def ds(start, size):
    return bass.ds(start, size)


def gps_layer_kernel(nc, x, src, dst, etype, edge_emb, Wq, bq, Wk, bk, Wv, bv, Ws, bs,
                     w_qkv, b_qkv, norm_g, norm_b, w_fc1, b_fc1, w_fc2, b_fc2,
                     Wr, br, W1, b1, g1, be1, m1, v1, W2, b2, g2, be2, m2, v2, Wo, bo, out):
    N, D = x.shape
    E = src.shape[0]
    NTYPE = edge_emb.shape[0]
    H, C = 4, 64
    NW = -(-N // P)
    TAIL = N - (NW - 1) * P
    ET = -(-E // P)
    G = 8
    NS = -(-(ET + NW) // G) * G
    NB = -(-NS // P)
    NSP = NB * P
    NGR = NS // G
    AC = D + H
    HT = -(-ET // (2 * G)) * 2 * G
    NK = NW * NTYPE
    EPS = 1e-5
    MH = w_fc1.shape[1]
    NE = W1.shape[0]
    FE = E // P
    FB = FE // P
    FR = FE - FB * P
    EREST = E - FE * P
    TG = 4
    NG = (NW - 1) // TG
    NM = MH // P
    NF = D // P
    PIECES = NGR // (NG + 1)
    assert NW == NG * TG + 1 and NG % 2 == 0 and PIECES * (NG + 1) == NGR and PIECES == 8 and NE == 8
    CREDIT = 2

    def done(g):
        return g + (1 + CREDIT)

    def reuse(g, ring):
        return g + (1 + CREDIT - ring)

    srcS = nc.dram_tensor("edges_src", [(ET + 1) * P], I32, kind="Internal").ap()
    dstS = nc.dram_tensor("edges_dst", [(ET + 1) * P], I32, kind="Internal").ap()
    relD = nc.dram_tensor("rel_rows", [NSP, P], BF16, kind="Internal").ap()
    xnD = nc.dram_tensor("xn_rows", [NW * P, D], F32, kind="Internal").ap()
    kD = nc.dram_tensor("k_rows", [NW * P, D], F32, kind="Internal").ap()
    vD = nc.dram_tensor("v_rows", [NW * P, D], F32, kind="Internal").ap()
    resD = nc.dram_tensor("res_rows", [NW * P, D], F32, kind="Internal").ap()
    sD = nc.dram_tensor("s_rows", [NW * P, D], F32, kind="Internal").ap()

    with ExitStack() as ctx:
        def sb(name, shape, dt):
            return ctx.enter_context(nc.sbuf_tensor(name, shape, dt))

        sems = {}

        def sem(name):
            if name not in sems:
                sems[name] = ctx.enter_context(nc.semaphore(name))
            return sems[name]

        nodes = sb("nodes", [P, NW * AC], F32)
        rows = sb("rows", [P, 16 * NSP + 8], F32)
        alpha = sb("alpha", [P, NSP * H], F32)
        srcC = sb("srcC", [P, NSP], U32)
        relC = sb("relC", [P, NSP], F32)
        relR = sb("relR", [P, NSP], F32)
        absR = sb("absR", [P, NSP], F32)
        work = sb("work", [P, 9280], F32)
        wrow = sb("wrow", [1, NSP], U32)
        w_gnn = sb("w_gnn", [P, 2, 4 * D], F32)
        w_mix = sb("w_mix", [P, 2, 3 * D], F32)
        w_f1 = w_gnn[:, :, 0:MH]
        w_f2 = sb("w_f2", [P, MH // P, D], F32)
        w_qf = w_mix[:, :, 0:D]
        b_gnn = sb("b_gnn", [P, 4 * D], F32)
        b_mix = sb("b_mix", [P, 3 * D], F32)
        emb = sb("emb", [NTYPE, D], F32)
        ident = sb("ident", [P, P], F32)
        iota_f = sb("iota_f", [P, P], F32)
        iota_p = sb("iota_p", [P, 1], F32)
        ones = sb("ones", [P, 1], F32)
        r4 = sb("r4", [P, NK], F32)
        stats = sb("stats", [P, NW * 6], F32)
        mv = sb("mv", [P, NW * 2], F32)
        rstd = sb("rstd", [P, NW], F32)
        tiny = sb("tiny", [P, 160], F32)

        gramK = sb("gramK", [P, 2 * P], F32)
        ends_all = sb("ends_all", [P, 6 * NB * H], F32)

        ps = ctx.enter_context(nc.psum_tensor("ps", [P, 8 * 512], F32))

        def bank(i, a=0, b=512):
            return ps[:, 512 * i + a:512 * i + b]

        def slot(i, n=1):
            return rows[:, i * NSP:(i + n) * NSP]

        iota_s = slot(0)
        cmp = slot(1)
        hs_i = slot(2).bitcast(I32)
        hy_i = slot(3).bitcast(I32)
        lo_i = slot(4).bitcast(I32)
        hi_i = slot(5).bitcast(I32)
        key_f = slot(6)
        lo_f = slot(7)
        sg_i = slot(8).bitcast(I32)
        dg_i = slot(9).bitcast(I32)
        sg_f = slot(10)
        iota8_i = rows[:, 11 * NSP:11 * NSP + NK * G].bitcast(I32)
        loh = [rows[:, 11 * NSP + 512 * b:11 * NSP + 512 * (b + 1)].bitcast(BF16) for b in range(2)]
        iota8 = rows[:, 13 * NSP:13 * NSP + NK * G // 2].bitcast(BF16)
        koh = [rows[:, 14 * NSP + NK * G // 2 * b:14 * NSP + NK * G // 2 * (b + 1)].bitcast(BF16) for b in range(2)]
        loC = slot(8)[:, 0:HT // 2].bitcast(BF16)
        keyC = slot(9)[:, 0:HT // 2].bitcast(BF16)
        relB = slot(10)[:, 0:NSP // 2].bitcast(BF16)
        assert NK * G <= 2 * NSP and NK * G // 2 <= NSP
        last_i = tiny[:, 0:8].bitcast(I32)
        last_w = tiny[:, 8:16].bitcast(I32)
        stepkey = tiny[:, 16:24]
        tcol = tiny[:, 24:32]
        icol = tiny[:, 32:40]
        wcol = tiny[:, 40:48]
        tcol_u = tiny[:, 48:56].bitcast(U32)
        padS = tiny[0:1, 56:57].bitcast(I32)
        count = tiny[:, 64:64 + NW]

        xs = [work[:, 256 * k:256 * (k + 1)] for k in range(2)]
        xp = [work[:, 512 + 256 * k:512 + 256 * (k + 1)] for k in range(2)]
        xT = [work[:, 1024 + 512 * k:1024 + 512 * (k + 1)] for k in range(2)]
        kS = [work[:, 2048 + 256 * k:2048 + 256 * (k + 1)] for k in range(2)]
        vsS = [work[:, 2560 + 512 * k:2560 + 512 * (k + 1)] for k in range(2)]
        mkv = [work[:, 3584 + 512 * k:3584 + 512 * (k + 1)] for k in range(2)]
        r4s = [work[:, 4608 + 4 * k:4608 + 4 * (k + 1)] for k in range(2)]
        r4T = [work[0:NTYPE, 4616 + 128 * k:4616 + 128 * (k + 1)] for k in range(2)]
        gramS = work[:, 4900:4900 + 256]

        kv = [work[:, G * AC * b:G * AC * (b + 1)] for b in range(2)]
        oh = [work[:, 2 * G * AC + G * P * b:2 * G * AC + G * P * (b + 1)] for b in range(2)]
        prod = work[:, 2 * G * AC + 2 * G * P:2 * G * AC + 2 * G * P + G * D]
        relq = [work[:, 2 * G * AC + 2 * G * P + G * D + G * P // 2 * b:
                     2 * G * AC + 2 * G * P + G * D + G * P // 2 * (b + 1)].bitcast(BF16) for b in range(2)]
        idx = [tiny[:, 128 + G * b:128 + G * (b + 1)].bitcast(U32) for b in range(2)]
        assert 2 * G * AC + 2 * G * P + G * D + G * P <= 9280

        RW = H * NSP
        atR = rows[:, 0:RW]
        fwR = rows[:, RW:2 * RW]
        bwR = rows[:, 2 * RW:3 * RW]
        penR = rows[:, 3 * RW:4 * RW]
        penN = rows[:, 3 * RW + 1:4 * RW + 1]
        ends = [ends_all[:, i * NB * H:(i + 1) * NB * H] for i in range(4)]
        saved = [ends_all[:, (4 + i) * NB * H:(5 + i) * NB * H] for i in range(2)]

        def line(i):
            return nodes[0:H, i * NSP:(i + 1) * NSP]
        carry = [line(8), line(9)]

        def slot_n(i):
            return nodes[:, i * NSP:(i + 1) * NSP]

        def cut(t, at, n):
            return t[:, at:at + n]
        W4 = TG * D
        m_xn = [cut(rows, W4 * b, W4) for b in range(2)]
        m_x = [cut(rows, W4 * (2 + b), W4) for b in range(2)]
        m_s = [cut(rows, W4 * (4 + b), W4) for b in range(2)]
        m_x1 = cut(rows, W4 * 6, W4)
        m_T = cut(rows, W4 * 7, W4)
        m_hT = cut(rows, W4 * 8, W4)
        m_gT = cut(rows, W4 * 9, NM * TG * P)
        assert W4 * 9 + NM * TG * P <= 16 * NSP
        m_col = sb("m_col", [P, 16], F32)
        spare = sb("spare", [P, 2], F32)
        m_st = sb("m_st", [P, TG * 6], F32)
        m_mv = sb("m_mv", [P, TG * 2], F32)
        m_rs = sb("m_rs", [P, TG], F32)
        a_sm = cut(work, 0, 2 * C)
        a_bd = cut(work, 128, 2 * P)
        a_T = cut(work, 384, 2 * P)
        a_wT = cut(work, 640, 4 * P)
        a_bT = cut(work, 1152, 2 * P)
        a_row = cut(work, 1408, P)
        a_v = [cut(work, 1536 + 2 * i, 2) for i in range(4)]

        e_w = [rows[:, NE * NF * D * i:NE * NF * D * (i + 1)].rearrange("p (e k n) -> p e k n", e=NE, k=NF) for i in range(3)]
        at = 3 * NE * NF * D
        e_bo = rows[0:NE, at:at + D]
        e_wr = rows[:, at + D:at + D + NF * NE].rearrange("p (k n) -> p k n", k=NF)
        e_br = cut(rows, at + D + 16, NE)
        e_prow = [cut(rows, at + D + 32 + P * i, P) for i in range(2)]
        e_par = [cut(rows, at + D + 32 + 2 * P + 80 * i, 80) for i in range(2)]
        e_sc = [cut(rows, at + D + 448 + 16 * i, 16) for i in range(2)]
        e_sh = [cut(rows, at + D + 480 + 16 * i, 16) for i in range(2)]
        assert at + D + 512 <= 16 * NSP
        f_T = [cut(work, W4 * b, W4) for b in range(2)]
        f_h1 = [cut(work, W4 * (2 + b), W4) for b in range(2)]
        f_h2 = [cut(work, W4 * (4 + b), W4) for b in range(2)]
        f_y = [cut(work, W4 * (6 + b), W4) for b in range(2)]
        f_z = cut(work, W4 * 8, W4)
        f_res = [cut(alpha, W4 * b, W4) for b in range(2)]
        f_wT = alpha[0:NE, W4 * 2:W4 * 2 + TG * P]
        f_lg = cut(ends_all, 0, TG * NE)
        f_w = [cut(ends_all, 32 + 32 * b, TG * NE) for b in range(2)]
        f_rc = cut(ends_all, 96, TG * H)
        f_m = cut(ends_all, 112, TG)
        f_st, f_mv, f_rs = m_st, m_mv, m_rs

        def on_rows(eng, e, name):
            state = [0]

            def link(ins):
                state[0] += 1
                ins.then_inc(sem(name), 1)
                eng.wait_ge(sem(name), state[0])
            return link

        block = ctx.enter_context(nc.Block())

        @block.sync
        def _(sp):
            sp.dma_start(srcS[0:E].rearrange("(a b) -> a b", a=160), src.rearrange("(a b) -> a b", a=160)).then_inc(sem("edges"), 16)
            sp.dma_start(dstS[0:E].rearrange("(a b) -> a b", a=160), dst.rearrange("(a b) -> a b", a=160)).then_inc(sem("edges"), 16)
            sp.wait_ge(sem("pads_set"), 1)
            one = lambda t, a, b: t[a:b].rearrange("(a b) -> a b", a=1)
            sp.dma_start(one(srcS, E, (ET + 1) * P), iota8_i[0:1, 0:(ET + 1) * P - E]).then_inc(sem("edges"), 16)
            sp.dma_start(one(dstS, E, ET * P), iota8_i[0:1, 256:256 + ET * P - E]).then_inc(sem("edges"), 16)
            sp.dma_start(one(dstS, ET * P, (ET + 1) * P), iota8_i[0:1, 384:384 + P]).then_inc(sem("edges"), 16)
            sp.wait_ge(sem("x_pad_set"), 1)
            for c in range(4):
                n = (NW - 1) // 4
                sp.dma_start(nodes[:, c * n * D:(c + 1) * n * D].rearrange("p (t d) -> p t d", d=D),
                             x[c * n * P:(c + 1) * n * P, :].rearrange("(t p) d -> p t d", p=P)).then_inc(sem("x_in"), 16)
            sp.dma_start(nodes[0:TAIL, (NW - 1) * D:NW * D], x[(NW - 1) * P:N, :]).then_inc(sem("x_in"), 16)
            sp.wait_ge(sem("hist_pad"), 1)
            for t, o in ((src, hs_i), (etype, hy_i)):
                sp.dma_start(o[:, 0:FB * P].rearrange("p (b e) -> p b e", b=FB),
                             t[0:FB * P * P].rearrange("(b p e) -> p b e", b=FB, p=P)).then_inc(sem("hist_in"), 16)
                sp.dma_start(o[0:FR, FB * P:(FB + 1) * P],
                             t[FB * P * P:FE * P].rearrange("(p e) -> p e", p=FR)).then_inc(sem("hist_in"), 16)
                sp.dma_start(o[FR:FR + 1, FB * P:FB * P + EREST],
                             t[FE * P:E].rearrange("(p e) -> p e", p=1)).then_inc(sem("hist_in"), 16)
            sp.wait_ge(sem("edges"), 80)
            sp.wait_ge(sem("last_pad"), 1)
            lastd = dstS[0:ET * P].rearrange("(t e) -> t e", e=P)
            for b in range(NB):
                n = min(P, ET - b * P)
                sp.dma_start(last_i[0:n, b:b + 1], lastd[b * P:b * P + n, P - 1:P], allow_slow_non_contiguous=True).then_inc(sem("last_in"), 16)
            for i, w in enumerate((Wq, Wk, Wv, Ws)):
                sp.dma_start(w_gnn[:, :, i * D:(i + 1) * D], w.rearrange("(k p) n -> p k n", p=P)).then_inc(sem("w_in"), 16)
            sp.dma_start(w_mix[:, :, :], w_qkv.rearrange("(k p) n -> p k n", p=P)).then_inc(sem("w_in"), 16)
            for i, w in enumerate((bq, bk, bv, bs)):
                sp.dma_start(b_gnn[:, i * D:(i + 1) * D], w.rearrange("(a n) -> a n", a=1).partition_broadcast(P)).then_inc(sem("w_in"), 16)
            sp.dma_start(b_mix[:, :], b_qkv.rearrange("(a n) -> a n", a=1).partition_broadcast(P)).then_inc(sem("w_in"), 16)
            sp.dma_start(emb[:, :], edge_emb).then_inc(sem("w_in"), 16)
            sp.wait_ge(sem("relB_made"), 1)
            sp.dma_start(relD.rearrange("(b p) e -> p b e", p=P), relB.rearrange("p (b e) -> p b e", b=NB)).then_inc(sem("rel_out"), 16)
            sp.wait_ge(sem("xn_made"), NW)
            sp.dma_start(xnD.rearrange("(t p) d -> p t d", p=P), nodes[:, 0:NW * D].rearrange("p (t d) -> p t d", d=D)).then_inc(sem("xn_out"), 16)
            sp.wait_ge(sem("xn_out"), 16)
            sp.sem_inc(sem("xn_stored"), 1)
            sp.sem_inc(sem("stored"), CREDIT)

            def store(t, k):
                sp.wait_ge(sem("qk_sb"), done(t))
                sp.dma_start(kD[ds(t * P, P), :], kS[k]).then_inc(sem("proj_out"), 16)
                sp.wait_ge(sem("vs_sb"), done(t))
                sp.dma_start(vD[ds(t * P, P), :], vsS[k][:, 0:D]).then_inc(sem("proj_out"), 16)
                sp.dma_start(sD[ds(t * P, P), :], vsS[k][:, D:2 * D]).then_inc(sem("proj_out"), 16)
                sp.wait_ge(sem("proj_out"), t * 48 + 48)
                sp.sem_inc(sem("stored"), 1)
            with sp.Fori(0, NW // 2) as it:
                for k in range(2):
                    store(it * 2 + k, k)
            store(NW - 1, 0)
            sp.wait_ge(sem("gram_sb"), 1)
            for i, (w, n) in enumerate(((norm_g, NF), (norm_b, NF), (b_fc1, NM))):
                sp.dma_start(a_row[NF * i:NF * i + n, :], w.rearrange("(k p) -> k p", p=P)).then_inc(sem("mix_in"), 16)
            sp.dma_start(b_mix[:, D:2 * D], b_fc2.rearrange("(a n) -> a n", a=1).partition_broadcast(P)).then_inc(sem("mix_in"), 16)
            sp.dma_start(w_f1, w_fc1.rearrange("(k p) n -> p k n", p=P)).then_inc(sem("mix_in"), 16)
            sp.dma_start(w_f2[:, :, :], w_fc2.rearrange("(k p) n -> p k n", p=P)).then_inc(sem("mix_in"), 16)

            def rel_load(j, b):
                sp.wait_ge(sem("oh_made"), reuse(j, 2))
                sp.dma_start(relq[b], relD[ds(j * G, G), :].rearrange("(a g) e -> a (g e)", a=1).partition_broadcast(P)).then_inc(sem(f"relq_in{b}"), 16)

            def tiles(t, g, n):
                return t[ds(g * (TG * P), n * P), :].rearrange("(t p) d -> p t d", p=P)

            def mix_load(g, b, n):
                for t, o in ((xnD, m_xn[b]), (sD, m_s[b])):
                    sp.dma_start(o[:, 0:n * D].rearrange("p (t d) -> p t d", d=D), tiles(t, g, n)).then_inc(sem(f"mix_rows{b}"), 16)
                if n == TG:
                    sp.dma_start(m_x[b].rearrange("p (t d) -> p t d", d=D), tiles(x, g, n)).then_inc(sem(f"mix_rows{b}"), 16)
                else:
                    sp.dma_start(m_x[b][0:TAIL, 0:D], x[(NW - 1) * P:N, :]).then_inc(sem(f"mix_rows{b}"), 16)

            def mix_store(g, n):
                sp.wait_ge(sem("m_out"), done(g))
                sp.dma_start(tiles(resD, g, n), m_x1[:, 0:n * D].rearrange("p (t d) -> p t d", d=D)).then_inc(sem("res_out"), 16)
                sp.wait_ge(sem("res_out"), g * 16 + 16)
                sp.sem_inc(sem("res_stored"), 1)

            def pass1(g, b, n, nxt):
                for p in range(PIECES):
                    rel_load(g * PIECES + p, p % 2)
                    if p == 0 and nxt:
                        if nxt == 1:
                            sp.wait_ge(sem("m_x_zero"), 1)
                        sp.wait_ge(sem("m_out"), reuse(g + 1, 2))
                        mix_load(g + 1, 1 - b, nxt)
                mix_store(g, n)
            sp.sem_inc(sem("res_stored"), CREDIT)
            sp.wait_ge(sem("rel_out"), 16)
            sp.wait_ge(sem("att_used"), 1)
            mix_load(0, 0, TG)
            with sp.Fori(0, NG // 2 - 1) as it:
                for b in range(2):
                    pass1(it * 2 + b, b, TG, TG)
            pass1(NG - 2, 0, TG, TG)
            pass1(NG - 1, 1, TG, 1)
            pass1(NG, 0, 1, 0)

            sp.wait_ge(sem("ex_cols"), 1)
            for i, w in enumerate((W1, W2, Wo)):
                sp.dma_start(rows[:, NE * NF * D * i:NE * NF * D * (i + 1)].rearrange("p (e n) -> p e n", n=D), w.rearrange("e (k p) n -> p (e k) n", p=P)).then_inc(sem("exp_in"), 16)
            sp.dma_start(e_bo, bo).then_inc(sem("exp_in"), 16)
            sp.dma_start(e_wr, Wr.rearrange("(k p) n -> p k n", p=P)).then_inc(sem("exp_in"), 16)
            sp.dma_start(e_br, br.rearrange("(a n) -> a n", a=1).partition_broadcast(P)).then_inc(sem("exp_in"), 16)
            for l, ws in enumerate(((g1, b1, be1, m1, v1), (g2, b2, be2, m2, v2))):
                for i, w in enumerate(ws):
                    sp.dma_start(e_prow[l][16 * i:16 * (i + 1), :], w.rearrange("e (k p) -> (e k) p", p=P)).then_inc(sem("exp_in"), 16)

            def res_load(g, b, n):
                sp.dma_start(f_res[b][:, 0:n * D].rearrange("p (t d) -> p t d", d=D), tiles(resD, g, n)).then_inc(sem(f"res_in{b}"), 16)

            def out_store(g, b, n):
                sp.wait_ge(sem("y_made"), done(g * NE + (NE - 1)))
                if n == TG:
                    sp.dma_start(tiles(out, g, n), f_y[b].rearrange("p (t d) -> p t d", d=D)).then_inc(sem("out_sent"), 16)
                else:
                    sp.dma_start(out[(NW - 1) * P:N, :], f_y[b][0:TAIL, 0:D]).then_inc(sem("out_sent"), 16)
                sp.wait_ge(sem("out_sent"), g * 16 + 16)
                sp.sem_inc(sem("y_stored"), 1)
            sp.sem_inc(sem("y_stored"), CREDIT)
            sp.wait_ge(sem("acc_made"), done(NGR * G - 1))
            res_load(0, 0, TG)
            res_load(1, 1, TG)

            def experts(g, b, n, later):
                if later:
                    sp.wait_ge(sem("y_init"), done(g))
                    res_load(g + 2, b, later)
                out_store(g, b, n)
            with sp.Fori(0, NG // 2 - 1) as it:
                for b in range(2):
                    experts(it * 2 + b, b, TG, TG)
            experts(NG - 2, 0, TG, 1)
            experts(NG - 1, 1, TG, 0)
            experts(NG, 0, 1, 0)
            sp.wait_ge(sem("out_sent"), 16 * (NG + 1))

        @block.gpsimd
        def _(pool):
            pool.iota(iota_s, pattern=[[1, NSP]], base=0, channel_multiplier=0, allow_small_or_imprecise_dtypes=True).then_inc(sem("iotas"), 1)
            pool.iota(iota_f[:, :], pattern=[[1, P]], base=0, channel_multiplier=0, allow_small_or_imprecise_dtypes=True).then_inc(sem("iotas"), 1)
            pool.iota(iota_p[:, :], pattern=[[0, 1]], base=0, channel_multiplier=1, allow_small_or_imprecise_dtypes=True).then_inc(sem("iotas"), 1)
            pool.iota(icol[:, 0:NB], pattern=[[P, NB]], base=0, channel_multiplier=1, allow_small_or_imprecise_dtypes=True).then_inc(sem("iotas"), 1)
            pool.memset(ident[:, :], 0.0).then_inc(sem("ident"), 1)
            pool.wait_ge(sem("ident"), 1)
            pool.affine_select(out=ident[:, :], in_=ident[:, :], compare_op=ALU.not_equal, fill=1.0,
                               base=0, pattern=[[-1, P]], channel_multiplier=1).then_inc(sem("ident"), 1)
            pool.memset(ones[:, :], 1.0).then_inc(sem("iotas"), 1)
            pool.wait_ge(sem("edges"), 80)
            pool.iota(iota8_i, pattern=[[1, NK], [0, G]], base=0, channel_multiplier=0).then_inc(sem("iotas"), 1)
            pool.wait_ge(sem("steps"), 1)
            for b in range(NB):
                for t, o in ((srcS, sg_i), (dstS, dg_i)):
                    pool.indirect_dma_start(out=o[:, b * P:(b + 1) * P], out_offset=None, in_=t.rearrange("(t e) -> t e", e=P),
                                            in_offset=bass.IndirectOffsetOnAxis(ap=tcol_u[:, b:b + 1], axis=0)).then_inc(sem("rows_in"), 16)

            def gather(j, b, m, table):
                pool.tensor_copy(idx[b], srcC[:, ds(m * G, G)]).then_inc(sem("idx_made"), 1)
                pool.wait_ge(sem("idx_made"), j + 1)
                pool.sem_inc(sem("gathers_begun"), 1)
                for g in range(G):
                    pool.indirect_dma_start(out=kv[b][:, g * AC:g * AC + D], out_offset=None, in_=table,
                                            in_offset=bass.IndirectOffsetOnAxis(ap=idx[b][:, g:g + 1], axis=0)).then_inc(sem(f"kv_in{b}"), 16)

            pool.wait_ge(sem("proj_out"), NW * 48)
            pool.wait_ge(sem("srcC_made"), 1)
            pool.wait_ge(sem("att_used"), 1)
            with pool.Fori(0, NGR // 2) as it:
                for b in range(2):
                    pool.wait_ge(sem("kv_used"), reuse(it * 2 + b, 2))
                    gather(it * 2 + b, b, it * 2 + b, kD)
            with pool.Fori(0, NGR // 2) as it:
                for b in range(2):
                    pool.wait_ge(sem("kv_used"), reuse(it * 2 + (b + NGR), 2))
                    gather(it * 2 + (b + NGR), b, it * 2 + b, vD)

        @block.scalar
        def _(act):
            act.sem_inc(sem("a_in"), CREDIT)
            act.sem_inc(sem("r4T_sb"), CREDIT)
            act.sem_inc(sem("xT_sb"), CREDIT)
            act.wait_ge(sem("var_eps"), 1)
            act.activation(rstd[:, :], rstd[:, :], ACT.Sqrt).then_inc(sem("std"), 1)
            act.wait_ge(sem("xn_made"), NW)
            act.wait_ge(sem("r4_made"), 1)

            def front(t, k):
                act.wait_ge(sem("xT_ps"), reuse(t, 2))
                act.activation(xs[k], nodes[:, ds(t * D, D)], ACT.Copy)
                act.activation(r4s[k], r4[:, ds(t * NTYPE, NTYPE)], ACT.Copy).then_inc(sem("a_in"), 1)
                act.wait_ge(sem("r4T_ps"), done(t))
                act.activation(r4T[k], bank(k, 0, P)[0:NTYPE, :], ACT.Copy).then_inc(sem("r4T_sb"), 1)
                act.wait_ge(sem("xT_ps"), done(t))
                act.wait_ge(sem("gram_ps"), reuse(t, 2))
                act.activation(xT[k], bank(2 + k), ACT.Copy).then_inc(sem("xT_sb"), 1)
            front(0, 0)
            with act.Fori(0, NW // 2) as it:
                front(it * 2 + 1, 1)
                front(it * 2 + 2, 0)
            act.sem_inc(sem("m_T_sb"), CREDIT)
            act.sem_inc(sem("m_std"), CREDIT)
            act.sem_inc(sem("gelu"), CREDIT)
            act.wait_ge(sem("a_neg"), 1)
            for i in range(2):
                act.activation(a_sm[:, i * C:(i + 1) * C], a_sm[:, i * C:(i + 1) * C], ACT.Exp, bias=a_v[1][:, i:i + 1],
                               scale=1.0 / C ** 0.5, accum_out=a_v[2][:, i:i + 1]).then_inc(sem("a_exp"), 1)

            def mix(g, p, n):
                if p == 0:
                    act.wait_ge(sem("m_T_ps"), done(g))
                    for i in range(NF):
                        ins = act.activation(m_T[:, i * TG * P:i * TG * P + n * P], bank(4 + i, 0, n * P), ACT.Copy)
                    ins.then_inc(sem("m_T_sb"), 1)
                if p == 1:
                    act.wait_ge(sem("m_var"), done(g))
                    act.activation(m_rs[:, 0:n], m_rs[:, 0:n], ACT.Sqrt).then_inc(sem("m_std"), 1)
                if p in (4, 5):
                    for i in range(NM // 2):
                        m = NM // 2 * (p - 4) + i
                        act.wait_ge(sem("fc1_ps"), done(g * NM + m))
                        act.activation(m_gT[:, m * TG * P:m * TG * P + n * P], bank(4 + m % 2, 0, n * P), ACT.Gelu,
                                       bias=m_col[:, 2 * NF + m:2 * NF + m + 1]).then_inc(sem("gelu"), 1)

            def pass1(g, n):
                for p in range(PIECES):
                    mix(g, p, n)
            with act.Fori(0, NG // 2) as it:
                for b in range(2):
                    pass1(it * 2 + b, TG)
            pass1(NG, 1)

            act.wait_ge(sem("shifted"), 1)
            act.activation(atR, atR, ACT.Exp).then_inc(sem("ex_made"), 1)
            act.sem_inc(sem("ex_in"), CREDIT)
            act.wait_ge(sem("ex_cols"), 1)
            with act.Fori(0, NGR // 2) as it:
                for b in range(2):
                    j = it * 2 + b
                    act.wait_ge(sem("agg_used"), reuse(j, 2))
                    act.activation(kv[b].rearrange("p (g a) -> p g a", g=G)[:, :, D:AC],
                                   alpha[:, ds(j * (G * H), G * H)].rearrange("p (g h) -> p g h", g=G), ACT.Copy).then_inc(sem("ex_in"), 1)

            for q in ("f_std", "f_T_sb", "f_exp", "f_wT_sb", "h1_sb", "h2_sb"):
                act.sem_inc(sem(q), CREDIT)
            act.wait_ge(sem("e_var"), 1)
            for l in range(2):
                ins = act.activation(e_sc[l], e_sc[l], ACT.Sqrt)
            ins.then_inc(sem("e_std"), 1)

            def first_part(g, b, n, q):
                if q == 0:
                    act.wait_ge(sem("f_var"), done(g))
                    act.activation(f_rs[:, 0:n], f_rs[:, 0:n], ACT.Sqrt).then_inc(sem("f_std"), 1)
                if q == 2:
                    act.wait_ge(sem("f_T_ps"), done(g))
                    for i in range(NF):
                        ins = act.activation(f_T[b][:, i * TG * P:i * TG * P + n * P], bank(6 + i, 0, n * P), ACT.Copy)
                    ins.then_inc(sem("f_T_sb"), 1)
                if q == 4:
                    act.wait_ge(sem("f_sub"), done(g))
                    act.activation(f_lg[:, 0:n * NE], f_lg[:, 0:n * NE], ACT.Exp).then_inc(sem("f_exp"), 1)
                if q == 5:
                    act.wait_ge(sem("f_wT_ps"), done(g))
                    act.activation(f_wT[:, 0:n * P], bank(6, 0, n * P)[0:NE, :], ACT.Copy).then_inc(sem("f_wT_sb"), 1)

            def layer(l, u, e, n):
                s_ps, s_sb, o = (("l1_ps", "h1_sb", f_h1), ("l2_ps", "h2_sb", f_h2))[l]
                for m in range(NF):
                    act.wait_ge(sem(s_ps), done(u * NF + m))
                    if m == 0 and l == 0:
                        act.wait_ge(sem("l2_ps"), u * NF + 1)
                    if m == 0 and l == 1:
                        act.wait_ge(sem("l3_ps"), reuse(u, 2))
                    act.activation(o[e % 2][:, m * TG * P:m * TG * P + n * P], bank(2 * l + m, 0, n * P), ACT.Relu,
                                   bias=e_sh[l][:, e * NF + m:e * NF + m + 1], scale=e_sc[l][:, e * NF + m:e * NF + m + 1]).then_inc(sem(s_sb), 1)

            def experts(g, b, n, nxt):
                for e in range(NE):
                    layer(1, g * NE + e, e, n)
                    if e < NE - 1 or nxt:
                        layer(0, g * NE + (e + 1), (e + 1) % NE, n if e < NE - 1 else nxt)
                    if nxt:
                        first_part(g + 1, 1 - b, nxt, e)
            for q in range(NE):
                first_part(0, 0, TG, q)
            layer(0, 0, 0, TG)
            with act.Fori(0, NG // 2 - 1) as it:
                for b in range(2):
                    experts(it * 2 + b, b, TG, TG)
            experts(NG - 2, 0, TG, TG)
            experts(NG - 1, 1, TG, 1)
            experts(NG, 0, 1, 0)

        @block.tensor
        def _(pe):
            for s in ("r4T_ps", "es_ps", "xT_ps", "qk_ps", "vs_ps", "mkv_ps", "gram_ps", "hist_ps", "qg_ps", "agg_ps", "m_T_ps", "x1_ps", "m_hT_ps", "fc1_ps",
                      "fc2_ps", "f_T_ps", "lg_ps", "f_wT_ps", "bo_ps", "l1_ps", "l2_ps", "l3_ps"):
                pe.sem_inc(sem(s), CREDIT)
            pe.wait_ge(sem("cmp_made"), 1)
            pe.wait_ge(sem("iotas"), 5)
            for b in range(NB):
                pe.matmul(bank(0, b, b + 1), cmp[:, b * P:(b + 1) * P], ones[:, :], start=True, stop=True)
            for h in range(2):
                w = NSP // 2
                last = pe.matmul(bank(1 + h, 0, w)[0:1, :], ones[:, :], cmp[:, h * w:(h + 1) * w], start=True, stop=True)
            last.then_inc(sem("tcol_ps"), 1)
            pe.wait_ge(sem("ident"), 2)

            def turn(rowsrc, first):
                for b in range(NB):
                    last = pe.transpose(bank(first + b // 4, (b % 4) * P, (b % 4 + 1) * P), rowsrc[:, b * P:(b + 1) * P], ident[:, :])
                return last
            pe.wait_ge(sem("hist_rows"), 1)
            turn(lo_f, 4).then_inc(sem("lo_ps"), 1)
            turn(key_f, 6).then_inc(sem("key_ps"), 1)
            pe.wait_ge(sem("rows_made"), 1)
            pe.wait_ge(sem("tcol_sb"), 1)
            turn(relR, 0).then_inc(sem("rel_ps"), 1)
            turn(sg_f, 2).then_inc(sem("src_ps"), 1)
            pe.wait_ge(sem("hist_z"), 1)
            pe.matmul(bank(4, 0, NK), loh[0][:, 0:P], koh[0][:, 0:NK], start=True, stop=False, skip_group_check=True)
            pe.matmul(bank(4, 0, NK), loh[0][:, 0:P], koh[0][:, 0:NK], start=False, stop=False, skip_group_check=True).then_inc(sem("hist_zero"), 1)
            with pe.Fori(0, HT // (2 * G)) as it:
                for b in range(2):
                    c = it * 2 + b
                    pe.wait_ge(sem("oneh"), done(c))
                    lo = loh[b].rearrange("p (n g) -> p g n", g=G)
                    ky = koh[b].rearrange("p (n g) -> p g n", g=G)
                    for g in range(G):
                        last = pe.matmul(bank(4, 0, NK), lo[:, g, :], ky[:, g, :], start=False, stop=False, skip_group_check=True)
                    last.then_inc(sem("hist_ps"), 1)

            pe.wait_ge(sem("w_in"), 176)
            pe.wait_ge(sem("xn_made"), NW)
            pe.wait_ge(sem("r4_made"), 1)
            pe.wait_ge(sem("srcC_made"), 1)
            pe.wait_ge(sem("gram0"), 1)
            pe.matmul(bank(7, 0, 256), gramS[:, 0:P], gramS[:, 0:256], start=True, stop=False, skip_group_check=True)

            def front(t, k):
                pe.wait_ge(sem("a_in"), done(t))
                pe.wait_ge(sem("xp_made"), reuse(t, 2))
                pe.transpose(bank(k, 0, P)[0:NTYPE, :], r4s[k], ident[:, :]).then_inc(sem("r4T_ps"), 1)
                pe.wait_ge(sem("r4T_sb"), done(t))
                pe.matmul(bank(k, P, P + D), r4T[k], emb[:, :], start=True, stop=True).then_inc(sem("es_ps"), 1)
                pe.wait_ge(sem("xp_made"), done(t))
                pe.wait_ge(sem("xT_sb"), reuse(t, 2))
                for i, s in enumerate((xs[k][:, 0:P], xs[k][:, P:D], xp[k][:, 0:P], xp[k][:, P:D])):
                    last = pe.transpose(bank(2 + k, i * P, (i + 1) * P), s, ident[:, :])
                last.then_inc(sem("xT_ps"), 1)

            def project(t, k, n):
                pe.wait_ge(sem("xT_sb"), done(t))
                for s_ps, s_sb, bk_, lhs, w in (("mkv_ps", "mkv_sb", 6, 0, w_mix[:, :, D:3 * D]),
                                                ("qk_ps", "qk_sb", 4, 2, w_gnn[:, :, 0:2 * D]),
                                                ("vs_ps", "vs_sb", 5, 2, w_gnn[:, :, 2 * D:4 * D])):
                    pe.wait_ge(sem(s_sb), reuse(t, 1))
                    for i in range(2):
                        last = pe.matmul(bank(bk_), xT[k][:, (lhs + i) * P:(lhs + i + 1) * P], w[:, i, :], start=(i == 0), stop=(i == 1))
                    last.then_inc(sem(s_ps), 1)
                pe.wait_ge(sem("mkv_sb"), done(t))
                for i in range(2):
                    last = pe.matmul(bank(7, i * P, (i + 1) * P), mkv[k][0:n, i * P:(i + 1) * P], mkv[k][0:n, D + i * P:D + (i + 1) * P],
                                     start=False, stop=False, skip_group_check=True)
                last.then_inc(sem("gram_ps"), 1)
            front(0, 0)
            with pe.Fori(0, NW // 2) as it:
                front(it * 2 + 1, 1)
                project(it * 2, 0, P)
                front(it * 2 + 2, 0)
                project(it * 2 + 1, 1, P)
            project(NW - 1, 0, TAIL)

            pe.wait_ge(sem("gram_sb"), 1)
            for a in range(2):
                for i in range(2):
                    last = pe.transpose(bank(2, (2 * i + a) * P, (2 * i + a + 1) * P), w_mix[:, a, i * P:(i + 1) * P], ident[:, :])
            for i in range(2):
                last = pe.transpose(bank(3, i * P, (i + 1) * P), b_mix[:, i * P:(i + 1) * P], ident[:, :])
            pe.wait_ge(sem("mix_in"), 96)
            n_ = 2 * NF + NM
            pe.transpose(bank(3, 2 * P, 2 * P + n_), a_row[0:n_, :], ident[0:n_, 0:n_]).then_inc(sem("a_turn"), 1)
            pe.wait_ge(sem("a_made"), 1)
            for i in range(2):
                last = pe.transpose(bank(0, i * P, (i + 1) * P), a_bd[:, i * P:(i + 1) * P], ident[:, :])
            last.then_inc(sem("aT_ps"), 1)
            pe.wait_ge(sem("aT_sb"), 1)
            for i in range(2):
                for a in range(2):
                    pe.matmul(bank(1, a * D + i * P, a * D + (i + 1) * P), a_wT[:, (2 * i + a) * P:(2 * i + a + 1) * P], a_T[:, i * P:(i + 1) * P], start=True, stop=True)
                last = pe.matmul(bank(0, D + i * P, D + (i + 1) * P), a_bT[:, i * P:(i + 1) * P], a_T[:, i * P:(i + 1) * P], start=True, stop=True)
            last.then_inc(sem("fold_ps"), 1)
            pe.wait_ge(sem("fold_sb"), 1)
            pe.wait_ge(sem("qk_sb"), done(NW - 1))
            pe.wait_ge(sem("vs_sb"), done(NW - 1))

            def mix(g, b, p, n):
                if p == 0:
                    pe.wait_ge(sem(f"mix_rows{b}"), (g - b) * 24 + 48)
                    pe.wait_ge(sem("gelu"), done(g * NM - 1))
                    for t in range(n):
                        for i in range(NF):
                            last = pe.transpose(bank(4 + i, t * P, (t + 1) * P), m_xn[b][:, t * D + i * P:t * D + (i + 1) * P], ident[:, :])
                    last.then_inc(sem("m_T_ps"), 1)
                if p == 1:
                    pe.wait_ge(sem("m_T_sb"), done(g))
                    pe.wait_ge(sem("m_out"), reuse(g, 1))
                    for t in range(n):
                        for i in range(NF):
                            last = pe.matmul(bank(6 + t // 2, t % 2 * D, (t % 2 + 1) * D), m_T[:, i * TG * P + t * P:i * TG * P + (t + 1) * P], w_qf[:, i, :], start=(i == 0), stop=(i == 1))
                    last.then_inc(sem("x1_ps"), 1)
                if p == 3:
                    pe.wait_ge(sem("m_z"), done(g))
                    for t in range(n):
                        for i in range(NF):
                            last = pe.transpose(bank(4 + i, t * P, (t + 1) * P), m_xn[b][:, t * D + i * P:t * D + (i + 1) * P], ident[:, :])
                    last.then_inc(sem("m_hT_ps"), 1)
                if p in (4, 5):
                    pe.wait_ge(sem("m_hT_sb"), done(g))
                    for k in range(NM // 2):
                        m = NM // 2 * (p - 4) + k
                        if m >= 2:
                            pe.wait_ge(sem("gelu"), done(g * NM + (m - 2)))
                        for i in range(NF):
                            last = pe.matmul(bank(4 + m % 2, 0, n * P), w_f1[:, i, m * P:(m + 1) * P], m_hT[:, i * TG * P:i * TG * P + n * P], start=(i == 0), stop=(i == 1))
                        last.then_inc(sem("fc1_ps"), 1)
                if p in (6, 7):
                    pe.wait_ge(sem("gelu"), done(g * NM + (NM - 1)))
                    last = None
                    for t in range(2 * (p - 6), min(n, 2 * (p - 6) + 2)):
                        for m in range(NM):
                            last = pe.matmul(bank(6 + t // 2, t % 2 * D, (t % 2 + 1) * D), m_gT[:, m * TG * P + t * P:m * TG * P + (t + 1) * P], w_f2[:, m, :], start=(m == 0), stop=(m == NM - 1))
                    if p == 7 and last is not None or n == 1 and p == 6:
                        last.then_inc(sem("fc2_ps"), 1)

            def edges(j, b):
                _, win = nc.values_load_multi_w_load_instructions(wrow[0:1, ds(j * G, G)], engines=(pe.engine,), min_val=0, max_val=NW - 1)
                pe.wait_ge(sem("oh_made"), done(j))
                for h in range(2):
                    pe.wait_ge(sem("prod_made"), reuse(j * 2 + h, 2))
                    for g in range(4):
                        s = 4 * h + g
                        last = pe.matmul(ps[:, 1024 * h + 256 * g:1024 * h + 256 * (g + 1)], oh[b][:, s * P:(s + 1) * P],
                                         nodes[:, ds(win[s] * D, D)], start=True, stop=True)
                    last.then_inc(sem("qg_ps"), 1)

            def pass1(g, b, n):
                for p in range(PIECES):
                    mix(g, b, p, n)
                    edges(g * PIECES + p, p % 2)
            with pe.Fori(0, NG // 2) as it:
                for b in range(2):
                    pass1(it * 2 + b, b, TG)
            pass1(NG, 0, 1)

            pe.wait_ge(sem("alpha_made"), done(2 * NGR - 1))
            pe.wait_ge(sem("alpha_pad"), 1)
            al = alpha[:, :].rearrange("p (s h) -> p h s", h=H)
            for h in range(H):
                for b in range(NB):
                    last = pe.transpose(ps[:, 1024 * h + b * P:1024 * h + (b + 1) * P], al[:, h, b * P:(b + 1) * P], ident[:, :])
                last.then_inc(sem("row_turn"), 1)
            pe.wait_ge(sem("ends_made"), 1)
            for i in range(4):
                for b in range(NB):
                    last = pe.transpose(ps[0:H, 1024 * i + b * P:1024 * i + (b + 1) * P], ends[i][:, b * H:(b + 1) * H], ident[:, :])
            last.then_inc(sem("ends_turn"), 1)
            pe.wait_ge(sem("carry_made"), 1)
            for i in range(2):
                for b in range(NB):
                    last = pe.transpose(bank(i, b * H, (b + 1) * H), carry[i][:, b * P:(b + 1) * P], ident[0:H, 0:H])
            last.then_inc(sem("carry_turn"), 1)
            pe.wait_ge(sem("ex_made"), 1)
            pe.wait_ge(sem("carry_in"), 1)
            for h in range(H):
                for b in range(NB):
                    n = h * NB + b
                    last = pe.transpose(ps[:, 1024 * h + b * P:1024 * h + (b + 1) * P], atR[:, n * P:(n + 1) * P], ident[:, :])
                last.then_inc(sem("col_turn"), 1)

            pe.wait_ge(sem("ex_cols"), 1)
            with pe.Fori(0, NGR // 2) as it:
                for b in range(2):
                    j = it * 2 + b
                    pe.wait_ge(sem("oh2_made"), done(j))
                    pe.wait_ge(sem("ex_in"), done(j))
                    for g in range(G):
                        pe.wait_ge(sem("acc_made"), reuse(j * G + g, 2))
                        pe.matmul(bank(g % 2, 0, AC), oh[b][:, g * P:(g + 1) * P], kv[b][:, g * AC:(g + 1) * AC],
                                  start=True, stop=True).then_inc(sem("agg_ps"), 1)


            pe.wait_ge(sem("exp_in"), 256)
            for l in range(2):
                last = pe.transpose(bank(2, l * 80, (l + 1) * 80), e_prow[l][0:80, :], ident[0:80, 0:80])
            last.then_inc(sem("par_turn"), 1)

            def first_part(g, b, n, q):
                if q == 2:
                    pe.wait_ge(sem("f_z_made"), done(g))
                    pe.wait_ge(sem("y_init"), reuse(g, 1))
                    for t in range(n):
                        for i in range(NF):
                            last = pe.transpose(bank(6 + i, t * P, (t + 1) * P), f_z[:, t * D + i * P:t * D + (i + 1) * P], ident[:, :])
                    last.then_inc(sem("f_T_ps"), 1)
                if q == 3:
                    pe.wait_ge(sem("f_T_sb"), done(g))
                    for t in range(n):
                        for i in range(NF):
                            last = pe.matmul(bank(6, t * NE, (t + 1) * NE), f_T[b][:, i * TG * P + t * P:i * TG * P + (t + 1) * P], e_wr[:, i, :], start=(i == 0), stop=(i == 1))
                    last.then_inc(sem("lg_ps"), 1)
                if q == 5:
                    pe.wait_ge(sem("f_w_made"), done(g))
                    for t in range(n):
                        last = pe.transpose(bank(6, t * P, (t + 1) * P)[0:NE, :], f_w[b][:, t * NE:(t + 1) * NE], ident[:, :])
                    last.then_inc(sem("f_wT_ps"), 1)
                if q == 6:
                    pe.wait_ge(sem("f_wT_sb"), done(g))
                    for t in range(n):
                        last = pe.matmul(bank(6 + t // 2, t % 2 * D, (t % 2 + 1) * D), f_wT[:, t * P:(t + 1) * P], e_bo, start=True, stop=True)
                    last.then_inc(sem("bo_ps"), 1)

            def layer(l, u, e, b, n):
                s_ps, s_sb, src_ = (("l1_ps", "h1_sb", f_T[b]), ("l2_ps", "h2_sb", f_h1[e % 2]))[l]
                if l == 1:
                    pe.wait_ge(sem("h1_sb"), done(u * NF + (NF - 1)))
                for m in range(NF):
                    pe.wait_ge(sem(s_sb), reuse(u * NF + m, 2))
                    for i in range(NF):
                        last = pe.matmul(bank(2 * l + m, 0, n * P), e_w[l][:, e, i, m * P:(m + 1) * P], src_[:, i * TG * P:i * TG * P + n * P], start=(i == 0), stop=(i == 1))
                    last.then_inc(sem(s_ps), 1)

            def last_layer(u, e, n):
                pe.wait_ge(sem("h2_sb"), done(u * NF + (NF - 1)))
                pe.wait_ge(sem("y_made"), reuse(u, 1))
                for t in range(n):
                    for i in range(NF):
                        last = pe.matmul(bank(4 + t // 2, t % 2 * D, (t % 2 + 1) * D), f_h2[e % 2][:, i * TG * P + t * P:i * TG * P + (t + 1) * P], e_w[2][:, e, i, :], start=(i == 0), stop=(i == 1))
                last.then_inc(sem("l3_ps"), 1)

            def experts(g, b, n, nxt):
                for e in range(NE):
                    layer(1, g * NE + e, e, b, n)
                    if e < NE - 1:
                        layer(0, g * NE + (e + 1), e + 1, b, n)
                    elif nxt:
                        layer(0, g * NE + (e + 1), 0, 1 - b, nxt)
                    last_layer(g * NE + e, e, n)
                    if nxt:
                        first_part(g + 1, 1 - b, nxt, e)
            for q in range(NE):
                first_part(0, 0, TG, q)
            pe.wait_ge(sem("e_ready"), 1)
            layer(0, 0, 0, 0, TG)
            with pe.Fori(0, NG // 2 - 1) as it:
                for b in range(2):
                    experts(it * 2 + b, b, TG, TG)
            experts(NG - 2, 0, TG, TG)
            experts(NG - 1, 1, TG, 1)
            experts(NG, 0, 1, 0)

        @block.vector
        def _(dve):
            for s in ("oneh", "xp_made", "mkv_sb", "qk_sb", "vs_sb", "oh_made", "prod_made", "alpha_made", "kv_used", "oh2_made", "agg_used", "acc_made",
                      "m_var", "m_z", "m_hT_sb", "m_out", "f_var", "f_z_made", "f_sub", "f_w_made", "y_init", "y_made"):
                dve.sem_inc(sem(s), CREDIT)
            link_n = [0]

            def link(ins):
                link_n[0] += 1
                ins.then_inc(sem("link"), 1)
                dve.wait_ge(sem("link"), link_n[0])

            dve.memset(iota8_i[0:1, 0:256], 0)
            dve.memset(iota8_i[0:1, 256:384], NW * P - 1)
            dve.memset(iota8_i[0:1, 384:512], FAR).then_inc(sem("pads_set"), 1)
            dve.memset(nodes[:, (NW - 1) * D:NW * D], 0.0).then_inc(sem("x_pad_set"), 1)
            dve.memset(hs_i, P * 63)
            dve.memset(hy_i, 0).then_inc(sem("hist_pad"), 1)
            dve.memset(last_i, FAR).then_inc(sem("last_pad"), 1)

            dve.wait_ge(sem("last_in"), 16 * NB)
            dve.wait_ge(sem("iotas"), 5)
            link(dve.tensor_scalar(last_w[:, 0:NB], last_i[:, 0:NB], 7, None, ALU.logical_shift_right))
            link(dve.tensor_copy(stepkey[:, 0:NB], last_w[:, 0:NB]))
            link(dve.tensor_tensor(stepkey[:, 0:NB], stepkey[:, 0:NB], icol[:, 0:NB], ALU.add))
            link(dve.tensor_scalar(cmp, iota_s, stepkey[:, 0:1], None, ALU.is_gt))
            for b in range(1, NB):
                ins = dve.scalar_tensor_tensor(out=cmp, in0=iota_s, scalar=stepkey[:, b:b + 1], in1=cmp, op0=ALU.is_gt, op1=ALU.add)
                if b < NB - 1:
                    link(ins)
            ins.then_inc(sem("cmp_made"), 1)
            dve.wait_ge(sem("tcol_ps"), 1)
            link(dve.tensor_copy(tcol[:, 0:NB], bank(0, 0, NB)))
            dve.tensor_copy(tcol_u[:, 0:NB], tcol[:, 0:NB]).then_inc(sem("steps"), 1)
            link(dve.tensor_tensor(wcol[:, 0:NB], icol[:, 0:NB], tcol[:, 0:NB], ALU.subtract))
            link(dve.tensor_scalar(wcol[:, 0:NB], wcol[:, 0:NB], float(NW - 1), float(P), ALU.min, ALU.mult))
            w2 = NSP // 2
            for h in range(2):
                dve.tensor_tensor(cmp[0:1, h * w2:(h + 1) * w2], iota_s[0:1, h * w2:(h + 1) * w2], bank(1 + h, 0, w2)[0:1, :], ALU.subtract).then_inc(sem("t_row"), 1)
            dve.wait_ge(sem("t_row"), 2)
            link(dve.tensor_scalar(wrow[:, :], cmp[0:1, :], float(NW - 1), None, ALU.min))
            dve.sem_inc(sem("tcol_sb"), 1)

            dve.wait_ge(sem("hist_in"), 96)
            link(dve.tensor_scalar(hi_i, hs_i, 7, None, ALU.logical_shift_right))
            link(dve.tensor_scalar(lo_i, hs_i, P - 1, None, ALU.bitwise_and))
            link(dve.tensor_copy(lo_f, lo_i))
            link(dve.tensor_copy(key_f, hi_i))
            dve.scalar_tensor_tensor(out=key_f, in0=key_f, scalar=float(NTYPE), in1=hy_i, op0=ALU.mult, op1=ALU.add).then_inc(sem("hist_rows"), 1)

            dve.wait_ge(sem("rows_in"), 32 * NB)
            link(dve.tensor_copy(absR[:, :], dg_i))
            link(dve.tensor_copy(sg_f, sg_i))
            for b in range(NB):
                ins = dve.tensor_scalar(relR[:, b * P:(b + 1) * P], absR[:, b * P:(b + 1) * P], wcol[:, b:b + 1], None, ALU.subtract)
            ins.then_inc(sem("rows_made"), 1)
            dve.wait_ge(sem("lo_ps"), 1)
            dve.tensor_copy(loC, ps[:, 4 * 512:4 * 512 + HT])
            dve.wait_ge(sem("key_ps"), 1)
            dve.tensor_copy(keyC, ps[:, 6 * 512:6 * 512 + HT]).then_inc(sem("hist_cols"), 1)
            dve.wait_ge(sem("rel_ps"), 1)
            link(dve.tensor_copy(relC[:, :], ps[:, 0:NSP]))
            dve.wait_ge(sem("src_ps"), 1)
            dve.tensor_copy(srcC[:, :], ps[:, 1024:1024 + NSP]).then_inc(sem("srcC_made"), 1)
            dve.wait_ge(sem("srcC_made"), 1)
            dve.tensor_copy(relB, relR[:, :]).then_inc(sem("relB_made"), 1)

            dve.wait_ge(sem("iotas"), 6)
            dve.wait_ge(sem("hist_cols"), 1)
            link(dve.tensor_copy(iota8, iota8_i))
            link(dve.memset(rows[:, 11 * NSP:11 * NSP + 512], 0.0))
            link(dve.memset(koh[0], 0.0))
            dve.sem_inc(sem("hist_z"), 1)
            dve.wait_ge(sem("hist_zero"), 1)
            with dve.Fori(0, HT // (2 * G)) as it:
                for b in range(2):
                    c = it * 2 + b
                    dve.wait_ge(sem("hist_ps"), reuse(c, 2))
                    for o, k, n in ((loh[b], loC, P), (koh[b], keyC, NK)):
                        ins = dve.tensor_tensor(o.rearrange("p (n g) -> p n g", g=G), k[:, ds(c * G, G)].unsqueeze(1).broadcast_to([P, n, G]),
                                                iota8[:, 0:n * G].rearrange("p (n g) -> p n g", g=G), ALU.is_equal)
                    ins.then_inc(sem("oneh"), 1)

            dve.wait_ge(sem("x_in"), 80)
            with dve.Fori(0, NW) as t:
                dve.bn_stats(stats[:, ds(t * 6, 6)], nodes[:, ds(t * D, D)]).then_inc(sem("bn"), 1)
            dve.wait_ge(sem("bn"), NW)
            for t in range(NW):
                dve.bn_aggr(mv[:, t * 2:(t + 1) * 2], stats[:, t * 6:(t + 1) * 6]).then_inc(sem("bn"), 1)
            dve.wait_ge(sem("bn"), 2 * NW)
            dve.tensor_scalar(rstd[:, :], mv[:, :].rearrange("p (t c) -> p c t", c=2)[:, 1, :], EPS, None, ALU.add).then_inc(sem("var_eps"), 1)
            dve.wait_ge(sem("std"), 1)
            link(dve.reciprocal(rstd[:, :], rstd[:, :]))
            with dve.Fori(0, NW) as t:
                dve.tensor_scalar(nodes[:, ds(t * D, D)], nodes[:, ds(t * D, D)], mv[:, ds(t * 2, 1)], rstd[:, ds(t, 1)],
                                  ALU.subtract, ALU.mult).then_inc(sem("xn_made"), 1)

            dve.wait_ge(sem("hist_ps"), done(HT // G - 1))
            link(dve.tensor_copy(r4[:, :], bank(4, 0, NK)))
            r4v = r4[:, :].rearrange("p (w k) -> p w k", k=NTYPE)
            link(dve.tensor_reduce(count, r4v, AX_X, ALU.add))
            link(dve.tensor_scalar(count, count, 1.0, None, ALU.max))
            link(dve.reciprocal(count, count))
            dve.tensor_tensor(r4v, r4v, count.unsqueeze(2).broadcast_to([P, NW, NTYPE]), ALU.mult).then_inc(sem("r4_made"), 1)
            dve.memset(gramS, 0.0).then_inc(sem("gram0"), 1)

            dve.wait_ge(sem("w_in"), 176)
            dve.wait_ge(sem("xn_stored"), 1)

            def front(t, k):
                dve.wait_ge(sem("es_ps"), done(t))
                dve.tensor_tensor(xp[k], bank(k, P, P + D), xs[k], ALU.add).then_inc(sem("xp_made"), 1)

            def evacuate(t, k):
                dve.wait_ge(sem("mkv_ps"), done(t))
                dve.wait_ge(sem("gram_ps"), reuse(t, 2))
                dve.tensor_tensor(mkv[k], bank(6), b_mix[:, D:3 * D], ALU.add).then_inc(sem("mkv_sb"), 1)
                dve.wait_ge(sem("qk_ps"), done(t))
                dve.tensor_tensor(nodes[:, ds(t * D, D)], bank(4, 0, D), b_gnn[:, 0:D], ALU.add)
                dve.wait_ge(sem("stored"), reuse(t, 2))
                dve.tensor_tensor(kS[k], bank(4, D, 2 * D), b_gnn[:, D:2 * D], ALU.add).then_inc(sem("qk_sb"), 1)
                dve.wait_ge(sem("vs_ps"), done(t))
                dve.tensor_tensor(vsS[k], bank(5), b_gnn[:, 2 * D:4 * D], ALU.add).then_inc(sem("vs_sb"), 1)
            front(0, 0)
            with dve.Fori(0, NW // 2) as it:
                front(it * 2 + 1, 1)
                evacuate(it * 2, 0)
                front(it * 2 + 2, 0)
                evacuate(it * 2 + 1, 1)
            evacuate(NW - 1, 0)
            dve.wait_ge(sem("gram_ps"), done(NW - 1))
            dve.tensor_copy(gramK[:, :], bank(7, 0, 2 * P)).then_inc(sem("gram_sb"), 1)
            dve.wait_ge(sem("stored"), done(NW - 1))

            dve.wait_ge(sem("gram_sb"), 1)
            for i in range(2):
                for h in range(2):
                    r = slice(C * h, C * (h + 1))
                    ins = dve.tensor_copy(a_sm[r, i * C:(i + 1) * C], gramK[r, i * P + C * h:i * P + C * (h + 1)])
            link(ins)
            a3 = a_sm.rearrange("p (i c) -> p i c", i=2)
            link(dve.tensor_reduce(a_v[0], a3, AX_X, ALU.max))
            dve.tensor_scalar(a_v[1], a_v[0], -1.0 / C ** 0.5, None, ALU.mult).then_inc(sem("a_neg"), 1)
            link(dve.memset(a_bd, 0.0))
            dve.wait_ge(sem("a_exp"), 2)
            link(dve.reciprocal(a_v[3], a_v[2]))
            for i in range(2):
                for h in range(2):
                    r = slice(C * h, C * (h + 1))
                    ins = dve.tensor_scalar(a_bd[r, i * P + C * h:i * P + C * (h + 1)], a_sm[r, i * C:(i + 1) * C], a_v[3][r, i:i + 1], None, ALU.mult)
            ins.then_inc(sem("a_made"), 1)
            dve.wait_ge(sem("a_turn"), 1)
            dve.tensor_copy(a_wT, bank(2))
            dve.tensor_copy(a_bT, bank(3, 0, 2 * P))
            dve.tensor_copy(m_col[:, 0:2 * NF + NM], bank(3, 2 * P, 2 * P + 2 * NF + NM))
            dve.wait_ge(sem("aT_ps"), 1)
            dve.tensor_copy(a_T, bank(0, 0, 2 * P)).then_inc(sem("aT_sb"), 1)
            dve.wait_ge(sem("fold_ps"), 1)
            dve.tensor_copy(w_qf, bank(1).rearrange("p (a d) -> p a d", a=2))
            dve.tensor_copy(b_mix[:, 0:D], bank(0, D, 2 * D)).then_inc(sem("fold_sb"), 1)
            dve.wait_ge(sem("fold_sb"), 1)
            dve.sem_inc(sem("att_used"), 1)

            def chained(name, base):
                state = [0]

                def add(ins):
                    state[0] += 1
                    ins.then_inc(sem(name), 1)
                    dve.wait_ge(sem(name), base + state[0])
                return add, state

            def halves(t, n):
                return [(t[:, c * 2 * D:min(n, 2 * c + 2) * D], c, (min(n, 2 * c + 2) - 2 * c) * D) for c in range(-(-n // 2))]

            def mix(g, b, p, n, go):
                three = lambda t: t[:, 0:n * D].rearrange("p (t d) -> p t d", d=D)
                brow = lambda a: b_mix[:, a * D:(a + 1) * D].unsqueeze(1).broadcast_to([P, n, D])
                if p == 1:
                    dve.wait_ge(sem("x1_ps"), done(g))
                    dve.wait_ge(sem("res_stored"), reuse(g, 1))
                    go(dve.tensor_tensor(m_x1[:, 0:n * D], ps[:, 6 * 512:6 * 512 + n * D], m_xn[b][:, 0:n * D], ALU.add))
                    go(dve.tensor_tensor(three(m_x1), three(m_x1), brow(0), ALU.add))
                    for t in range(n):
                        ins = dve.bn_stats(m_st[:, t * 6:(t + 1) * 6], m_x1[:, t * D:(t + 1) * D])
                    go(ins)
                    dve.memset(spare[:, 1:2], 0.0)
                    for t in range(n):
                        ins = dve.bn_aggr(m_mv[:, t * 2:(t + 1) * 2], m_st[:, t * 6:(t + 1) * 6])
                    go(ins)
                    dve.tensor_scalar(m_rs[:, 0:n], m_mv[:, 0:2 * n].rearrange("p (t c) -> p c t", c=2)[:, 1, :], EPS, None, ALU.add).then_inc(sem("m_var"), 1)
                if p == 2:
                    dve.wait_ge(sem("m_std"), done(g))
                    go(dve.reciprocal(m_rs[:, 0:n], m_rs[:, 0:n]))
                    for t in range(n):
                        ins = dve.tensor_scalar(m_xn[b][:, t * D:(t + 1) * D], m_x1[:, t * D:(t + 1) * D], m_mv[:, 2 * t:2 * t + 1], m_rs[:, t:t + 1], ALU.subtract, ALU.mult)
                    ins.then_inc(sem("m_z"), 1)
                    dve.wait_ge(sem(f"mix_rows{b}"), (g - b) * 24 + 48)
                    go(dve.tensor_tensor(m_s[b][:, 0:n * D], m_s[b][:, 0:n * D], m_x[b][:, 0:n * D], ALU.add))
                if p == 3:
                    dve.wait_ge(sem("m_hT_ps"), done(g))
                    for i in range(NF):
                        ins = dve.tensor_scalar(m_hT[:, i * TG * P:i * TG * P + n * P], bank(4 + i, 0, n * P), m_col[:, i:i + 1], m_col[:, NF + i:NF + i + 1], ALU.mult, ALU.add)
                    ins.then_inc(sem("m_hT_sb"), 1)
                if p == 4:
                    go(dve.tensor_tensor(m_s[b][:, 0:n * D], m_s[b][:, 0:n * D], m_x1[:, 0:n * D], ALU.add))
                if p == 5:
                    go(dve.tensor_tensor(three(m_s[b]), three(m_s[b]), brow(1), ALU.add))
                if p == 7:
                    dve.wait_ge(sem("fc2_ps"), done(g))
                    dve.tensor_tensor(m_x1[:, 0:n * D], ps[:, 6 * 512:6 * 512 + n * D], m_s[b][:, 0:n * D], ALU.add).then_inc(sem("m_out"), 1)

            def scores(j, b, m):
                dve.wait_ge(sem(f"relq_in{b}"), m * 16 + 16)
                dve.tensor_scalar(oh[b], relq[b], iota_p[:, 0:1], None, ALU.is_equal).then_inc(sem("oh_made"), 1)
                dve.wait_ge(sem(f"kv_in{b}"), m * (16 * G) + 16 * G)
                for h in range(2):
                    dve.wait_ge(sem("qg_ps"), done(j * 2 + h))
                    dve.wait_ge(sem("alpha_made"), reuse(j * 2 + h, 2))
                    dve.tensor_tensor(prod[:, 1024 * h:1024 * (h + 1)].rearrange("p (g d) -> p g d", g=4),
                                      kv[b][:, 4 * h * AC:4 * (h + 1) * AC].rearrange("p (g a) -> p g a", g=4)[:, :, 0:D],
                                      ps[:, 1024 * h:1024 * (h + 1)].rearrange("p (g d) -> p g d", g=4), ALU.mult).then_inc(sem("prod_made"), 1)
                for h in range(2):
                    dve.wait_ge(sem("prod_made"), done(j * 2 + h))
                    dve.tensor_reduce(alpha[:, ds((j * 2 + h) * (4 * H), 4 * H)], prod[:, 1024 * h:1024 * (h + 1)].rearrange("p (s c) -> p s c", c=C),
                                      AX_X, ALU.add).then_inc(sem("alpha_made"), 1)
                dve.sem_inc(sem("kv_used"), 1)

            def pass1(g, b, n):
                go, state = chained("mchain", g * 8)
                for p in range(PIECES):
                    scores(g * PIECES + p, p % 2, g * (PIECES // 2) + p // 2)
                    mix(g, b, p, n, go)
                assert state[0] == 8
            with dve.Fori(0, NG // 2 - 1) as it:
                for b in range(2):
                    pass1(it * 2 + b, b, TG)
            pass1(NG - 2, 0, TG)
            dve.memset(m_x[0][:, 0:D], 0.0).then_inc(sem("m_x_zero"), 1)
            pass1(NG - 1, 1, TG)
            pass1(NG, 0, 1)
            dve.memset(alpha[:, NGR * G * H:NSP * H], 0.0).then_inc(sem("alpha_pad"), 1)

            dve.wait_ge(sem("res_out"), 16 * (NG + 1))
            link(dve.tensor_scalar(slot_n(10), relR[:, :], 0.0, None, ALU.is_lt))
            link(dve.scalar_tensor_tensor(out=slot_n(10), in0=relR[:, :], scalar=float(P - 1), in1=slot_n(10), op0=ALU.is_gt, op1=ALU.add))
            link(dve.tensor_scalar(slot_n(10), slot_n(10), BIG_NEG, None, ALU.mult))
            inv = slot_n(10)
            fresh = slot_n(11)
            ab = absR[:, :].rearrange("p (b e) -> p b e", b=NB)
            fr = fresh.rearrange("p (b e) -> p b e", b=NB)
            link(dve.tensor_tensor(fr[:, :, 1:P], ab[:, :, 1:P], ab[:, :, 0:P - 1], ALU.not_equal))
            link(dve.memset(fr[:, :, 0:1], 1.0))
            link(dve.tensor_scalar(penR.rearrange("p (h x) -> p h x", h=H), fresh.unsqueeze(1).broadcast_to([P, H, NSP]), BIG_NEG, None, ALU.mult))
            link(dve.memset(rows[:, 4 * RW:4 * RW + 1], BIG_NEG))
            for h in range(H):
                dve.wait_ge(sem("row_turn"), h + 1)
                link(dve.scalar_tensor_tensor(out=atR[:, h * NSP:(h + 1) * NSP], in0=ps[:, 1024 * h:1024 * h + NSP], scalar=1.0 / C ** 0.5,
                                              in1=inv, op0=ALU.mult, op1=ALU.add))

            def scans():
                dve.tensor_tensor_scan(fwR, penR, atR, BIG_NEG, ALU.add, ALU.max).then_inc(sem("scan"), 1)
                link(dve.tensor_tensor_scan(bwR[:, ::-1], penN[:, ::-1], atR[:, ::-1], BIG_NEG, ALU.add, ALU.max))
            scans()
            av = atR.rearrange("p (h b e) -> p b h e", h=H, b=NB)
            fv = fwR.rearrange("p (h b e) -> p b h e", h=H, b=NB)
            bv_ = bwR.rearrange("p (h b e) -> p b h e", h=H, b=NB)
            ev = [e.rearrange("p (b h) -> p b h", b=NB) for e in ends]
            sv = [e.rearrange("p (b h) -> p b h", b=NB) for e in saved]
            dve.tensor_copy(ev[0], fv[:, :, :, P - 1])
            dve.tensor_copy(ev[1], bv_[:, :, :, 0])
            dve.tensor_copy(sv[0], av[:, :, :, 0])
            dve.tensor_copy(sv[1], av[:, :, :, P - 1])
            dve.tensor_copy(ev[2], ab[:, :, 0:1].broadcast_to([P, NB, H]))
            dve.tensor_copy(ev[3], ab[:, :, P - 1:P].broadcast_to([P, NB, H])).then_inc(sem("ends_made"), 1)
            dve.wait_ge(sem("ends_turn"), 1)
            lm, fm, d0, de, cont, chain, fsc, bsc = [line(i) for i in range(8)]
            for i in range(4):
                link(dve.tensor_copy(line(i), ps[0:H, 1024 * i:1024 * i + NSP]))
            Z = NSP - 1
            link(dve.memset(cont, 0.0))
            link(dve.tensor_tensor(cont[:, 1:NSP], d0[:, 1:NSP], de[:, 0:Z], ALU.is_equal))
            link(dve.tensor_tensor(d0, d0, de, ALU.is_equal))
            link(dve.tensor_tensor(chain, d0, cont, ALU.mult))
            link(dve.tensor_scalar(chain, chain, -BIG_NEG, BIG_NEG, ALU.mult, ALU.add))
            link(dve.tensor_tensor_scan(fsc, chain, lm, BIG_NEG, ALU.add, ALU.max))
            link(dve.memset(chain, 0.0))
            link(dve.tensor_tensor(chain[:, 0:Z], d0[:, 0:Z], cont[:, 1:NSP], ALU.mult))
            link(dve.tensor_scalar(chain, chain, -BIG_NEG, BIG_NEG, ALU.mult, ALU.add))
            link(dve.tensor_tensor_scan(bsc[:, ::-1], chain[:, ::-1], fm[:, ::-1], BIG_NEG, ALU.add, ALU.max))
            link(dve.tensor_scalar(cont, cont, -BIG_NEG, BIG_NEG, ALU.mult, ALU.add))
            dve.memset(carry[0], BIG_NEG)
            link(dve.memset(carry[1], BIG_NEG))
            dve.tensor_tensor(carry[0][:, 1:NSP], fsc[:, 0:Z], cont[:, 1:NSP], ALU.add)
            dve.tensor_tensor(carry[1][:, 0:Z], bsc[:, 1:NSP], cont[:, 1:NSP], ALU.add).then_inc(sem("carry_made"), 1)
            dve.wait_ge(sem("carry_turn"), 1)
            for i, e in ((0, 0), (1, P - 1)):
                link(dve.tensor_tensor(av[:, :, :, e], sv[i], bank(i, 0, NB * H).rearrange("p (b h) -> p b h", b=NB), ALU.max))
            dve.sem_inc(sem("carry_in"), 1)
            scans()
            link(dve.tensor_tensor(fwR, fwR, bwR, ALU.max))
            for i, e in ((0, 0), (1, P - 1)):
                link(dve.tensor_copy(av[:, :, :, e], sv[i]))
            dve.tensor_tensor(atR, atR, fwR, ALU.subtract).then_inc(sem("shifted"), 1)
            dve.memset(nodes[:, :], 0.0).then_inc(sem("acc_zero"), 1)
            for h in range(H):
                dve.wait_ge(sem("col_turn"), h + 1)
                ins = dve.tensor_copy(alpha[:, :].rearrange("p (s h) -> p h s", h=H)[:, h, :], ps[:, 1024 * h:1024 * h + NSP])
            ins.then_inc(sem("ex_cols"), 1)
            dve.wait_ge(sem("ex_cols"), 1)
            dve.wait_ge(sem("acc_zero"), 1)

            with dve.Fori(0, NGR // 2) as it:
                for b in range(2):
                    j = it * 2 + b
                    _, win = nc.values_load_multi_w_load_instructions(wrow[0:1, ds(j * G, G)], engines=(dve.engine,), min_val=0, max_val=NW - 1)
                    dve.tensor_tensor(oh[b].rearrange("p (g n) -> p g n", g=G), relC[:, ds(j * G, G)].unsqueeze(2).broadcast_to([P, G, P]),
                                      iota_f[:, :].unsqueeze(1).broadcast_to([P, G, P]), ALU.is_equal)
                    dve.wait_ge(sem(f"kv_in{b}"), it * (16 * G) + (NGR // 2 * 16 * G + 16 * G))
                    v4 = kv[b].rearrange("p (g a) -> p g a", g=G)[:, :, 0:D]
                    for g in range(G):
                        vg = kv[b][:, g * AC:g * AC + D].rearrange("p (h c) -> p h c", h=H)
                        ins = dve.tensor_tensor(vg, vg, alpha[:, ds((j * G + g) * H, H)].unsqueeze(2).broadcast_to([P, H, C]), ALU.mult)
                    ins.then_inc(sem("oh2_made"), 1)
                    for g in range(G):
                        i = j * G + g
                        dve.wait_ge(sem("agg_ps"), done(i))
                        dve.wait_ge(sem("acc_made"), done(i - 1))
                        acc = nodes[:, ds(win[g] * AC, AC)]
                        dve.tensor_tensor(acc, acc, bank(g % 2, 0, AC), ALU.add).then_inc(sem("acc_made"), 1)
                    dve.sem_inc(sem("agg_used"), 1)
                    dve.sem_inc(sem("kv_used"), 1)
            dve.wait_ge(sem("acc_made"), done(NGR * G - 1))

            dve.wait_ge(sem("par_turn"), 1)
            for l in range(2):
                link(dve.tensor_copy(e_par[l], bank(2, l * 80, (l + 1) * 80)))
                ins = dve.tensor_scalar(e_sc[l], e_par[l][:, 64:80], 0.001, None, ALU.add)
            ins.then_inc(sem("e_var"), 1)
            dve.wait_ge(sem("e_std"), 1)
            for l in range(2):
                pg, pb, pbe, pm = [e_par[l][:, 16 * i:16 * (i + 1)] for i in range(4)]
                link(dve.reciprocal(e_sc[l], e_sc[l]))
                link(dve.tensor_tensor(e_sc[l], e_sc[l], pg, ALU.mult))
                link(dve.tensor_tensor(e_sh[l], pb, pm, ALU.subtract))
                link(dve.tensor_tensor(e_sh[l], e_sh[l], e_sc[l], ALU.mult))
                link(dve.tensor_tensor(e_sh[l], e_sh[l], pbe, ALU.add))
            dve.sem_inc(sem("e_ready"), 1)

            def first_part(g, b, m, n, q, go):
                y = f_y[b]
                av = nodes[:, ds(g * (TG * AC), n * AC)].rearrange("p (t a) -> p t a", a=AC)
                l3 = f_lg[:, 0:n * NE].rearrange("p (t e) -> p t e", e=NE)
                if q == 0:
                    go(dve.tensor_scalar(f_rc[:, 0:n * H].rearrange("p (t h) -> p t h", h=H), av[:, :, D:AC], 1e-16, None, ALU.add))
                    go(dve.reciprocal(f_rc[:, 0:n * H], f_rc[:, 0:n * H]))
                    dve.wait_ge(sem("y_stored"), reuse(g, 2))
                    go(dve.tensor_tensor(y[:, 0:n * D].rearrange("p (t h c) -> p t h c", t=n, h=H), av[:, :, 0:D].rearrange("p t (h c) -> p t h c", h=H),
                                         f_rc[:, 0:n * H].rearrange("p (t h) -> p t h", h=H).unsqueeze(3).broadcast_to([P, n, H, C]), ALU.mult))
                    dve.wait_ge(sem(f"res_in{b}"), m * 16 + 16)
                    go(dve.tensor_tensor(y[:, 0:n * D], y[:, 0:n * D], f_res[b][:, 0:n * D], ALU.add))
                    for t in range(n):
                        ins = dve.bn_stats(f_st[:, t * 6:(t + 1) * 6], y[:, t * D:(t + 1) * D])
                    go(ins)
                    dve.memset(spare[:, 1:2], 0.0)
                    for t in range(n):
                        ins = dve.bn_aggr(f_mv[:, t * 2:(t + 1) * 2], f_st[:, t * 6:(t + 1) * 6])
                    go(ins)
                    dve.tensor_scalar(f_rs[:, 0:n], f_mv[:, 0:2 * n].rearrange("p (t c) -> p c t", c=2)[:, 1, :], EPS, None, ALU.add).then_inc(sem("f_var"), 1)
                if q == 1:
                    dve.wait_ge(sem("f_std"), done(g))
                    go(dve.reciprocal(f_rs[:, 0:n], f_rs[:, 0:n]))
                    for t in range(n):
                        ins = dve.tensor_scalar(f_z[:, t * D:(t + 1) * D], y[:, t * D:(t + 1) * D], f_mv[:, 2 * t:2 * t + 1], f_rs[:, t:t + 1], ALU.subtract, ALU.mult)
                    ins.then_inc(sem("f_z_made"), 1)
                if q == 3:
                    dve.wait_ge(sem("lg_ps"), done(g))
                    go(dve.tensor_tensor(l3, bank(6, 0, n * NE).rearrange("p (t e) -> p t e", e=NE), e_br.unsqueeze(1).broadcast_to([P, n, NE]), ALU.add))
                    go(dve.tensor_reduce(f_m[:, 0:n], l3, AX_X, ALU.max))
                    dve.tensor_tensor(l3, l3, f_m[:, 0:n].unsqueeze(2).broadcast_to([P, n, NE]), ALU.subtract).then_inc(sem("f_sub"), 1)
                if q == 4:
                    dve.wait_ge(sem("f_exp"), done(g))
                    go(dve.tensor_reduce(f_m[:, 0:n], l3, AX_X, ALU.add))
                    go(dve.reciprocal(f_m[:, 0:n], f_m[:, 0:n]))
                    dve.tensor_tensor(f_w[b][:, 0:n * NE].rearrange("p (t e) -> p t e", e=NE), l3, f_m[:, 0:n].unsqueeze(2).broadcast_to([P, n, NE]), ALU.mult).then_inc(sem("f_w_made"), 1)
                if q == 6:
                    dve.wait_ge(sem("bo_ps"), done(g))
                    dve.tensor_tensor(y[:, 0:n * D], ps[:, 6 * 512:6 * 512 + n * D], y[:, 0:n * D], ALU.add).then_inc(sem("y_init"), 1)

            def experts(g, b, m, n, nxt):
                go, state = chained("fchain", (g + 1) * 11)
                dve.wait_ge(sem("y_init"), done(g))
                for e in range(NE):
                    dve.wait_ge(sem("l3_ps"), done(g * NE + e))
                    dve.wait_ge(sem("y_made"), done(g * NE + (e - 1)))
                    for t in range(n):
                        yt = f_y[b][:, t * D:(t + 1) * D]
                        ins = dve.scalar_tensor_tensor(out=yt, in0=bank(4 + t // 2, t % 2 * D, (t % 2 + 1) * D), scalar=f_w[b][:, t * NE + e:t * NE + e + 1],
                                                       in1=yt, op0=ALU.mult, op1=ALU.add)
                    ins.then_inc(sem("y_made"), 1)
                    if nxt:
                        first_part(g + 1, 1 - b, m + b, nxt, e, go)
                assert state[0] in (0, 11)
            go, _ = chained("fchain", 0)
            for q in range(NE):
                first_part(0, 0, 0, TG, q, go)
            with dve.Fori(0, NG // 2 - 1) as it:
                for b in range(2):
                    experts(it * 2 + b, b, it, TG, TG)
            experts(NG - 2, 0, NG // 2 - 1, TG, TG)
            experts(NG - 1, 1, NG // 2 - 1, TG, 1)
            experts(NG, 0, NG // 2, 1, 0)


_INS = ['x', 'src', 'dst', 'edge_type_4', 'L0_gnn_edge_emb', 'L0_gnn_Wq', 'L0_gnn_bq', 'L0_gnn_Wk', 'L0_gnn_bk', 'L0_gnn_Wv',
        'L0_gnn_bv', 'L0_gnn_Ws', 'L0_gnn_bs', 'L0_mix_w_qkv', 'L0_mix_b_qkv', 'L0_mix_norm_g', 'L0_mix_norm_b', 'L0_mix_w_fc1',
        'L0_mix_b_fc1', 'L0_mix_w_fc2', 'L0_mix_b_fc2', 'L0_ffn_Wr', 'L0_ffn_br', 'L0_ffn_W1', 'L0_ffn_b1', 'L0_ffn_g1',
        'L0_ffn_be1', 'L0_ffn_m1', 'L0_ffn_v1', 'L0_ffn_W2', 'L0_ffn_b2', 'L0_ffn_g2', 'L0_ffn_be2', 'L0_ffn_m2', 'L0_ffn_v2',
        'L0_ffn_Wo', 'L0_ffn_bo']
_OUTS = [((6250, 256), 'float32')]


def kernel(**inputs):
    import numpy as _np
    import concourse.bacc as _bacc
    from concourse import mybir as _mybir
    from concourse.bass_utils import run_bass_kernel_spmd as _run

    nc = _bacc.Bacc("TRN2", target_bir_lowering=False, num_devices=1)
    arrays, args = {}, []
    for name in _INS:
        a = _np.ascontiguousarray(inputs[name])
        arrays[f"in_{name}_dram"] = a
        args.append(nc.dram_tensor(f"in_{name}_dram", a.shape, _mybir.dt.from_np(a.dtype), kind="ExternalInput").ap())
    for i, (shape, dtype) in enumerate(_OUTS):
        dt = _mybir.dt.from_np(_np.dtype(dtype))
        args.append(nc.dram_tensor(f"out_{i}_dram", shape, dt, kind="ExternalOutput").ap())
    gps_layer_kernel(nc, *args)
    r = _run(nc, [arrays], core_ids=[0])
    got = tuple(r.results[0][f"out_{i}_dram"] for i in range(len(_OUTS)))
    return got[0]
```

```python
from contextlib import ExitStack

import concourse.bass as bass
from concourse import mybir

ALU = mybir.AluOpType
ACT = mybir.ActivationFunctionType
AX_X = mybir.AxisListType.X
F32 = mybir.dt.float32
BF16 = mybir.dt.bfloat16
I32 = mybir.dt.int32
U32 = mybir.dt.uint32

P = 128
BIG_NEG = -1.0e30
FAR = 1 << 20


def ds(start, size):
    return bass.ds(start, size)


def gps_layer_kernel(nc, x, src, dst, etype, edge_emb, Wq, bq, Wk, bk, Wv, bv, Ws, bs,
                     w_qkv, b_qkv, norm_g, norm_b, w_fc1, b_fc1, w_fc2, b_fc2,
                     Wr, br, W1, b1, g1, be1, m1, v1, W2, b2, g2, be2, m2, v2, Wo, bo, out):
    N, D = x.shape
    E = src.shape[0]
    NTYPE = edge_emb.shape[0]
    H, C = 4, 64
    NW = -(-N // P)
    TAIL = N - (NW - 1) * P
    ET = -(-E // P)
    G = 8
    NS = -(-(ET + NW) // G) * G
    NB = -(-NS // P)
    NSP = NB * P
    NGR = NS // G
    AC = D + H
    HT = -(-ET // (2 * G)) * 2 * G
    NK = NW * NTYPE
    EPS = 1e-5
    MH = w_fc1.shape[1]
    NE = W1.shape[0]
    FE = E // P
    FB = FE // P
    FR = FE - FB * P
    EREST = E - FE * P
    TG = 4
    NG = (NW - 1) // TG
    NM = MH // P
    NF = D // P
    PIECES = NGR // (NG + 1)
    assert NW == NG * TG + 1 and NG % 2 == 0 and PIECES * (NG + 1) == NGR and PIECES == 8 and NE == 8
    HG = G // 2
    NHF = 2 * NGR
    KV = 4
    CREDIT = 2

    def done(g):
        return g + (1 + CREDIT)

    def reuse(g, ring):
        return g + (1 + CREDIT - ring)

    srcS = nc.dram_tensor("edges_src", [(ET + 1) * P], I32, kind="Internal").ap()
    dstS = nc.dram_tensor("edges_dst", [(ET + 1) * P], I32, kind="Internal").ap()
    srcT = nc.dram_tensor("sorted_src", [ET * P], I32, kind="Internal").ap()
    dstT = nc.dram_tensor("sorted_dst", [ET * P], I32, kind="Internal").ap()
    nextD = nc.dram_tensor("next_place", [NW * P], F32, kind="Internal").ap()
    downD = nc.dram_tensor("descents", [P], F32, kind="Internal").ap()
    relD = nc.dram_tensor("rel_rows", [NSP, P], BF16, kind="Internal").ap()
    xnD = nc.dram_tensor("xn_rows", [NW * P, D], F32, kind="Internal").ap()
    kD = nc.dram_tensor("k_rows", [NW * P, D], F32, kind="Internal").ap()
    vD = nc.dram_tensor("v_rows", [NW * P, D], F32, kind="Internal").ap()
    resD = nc.dram_tensor("res_rows", [NW * P, D], F32, kind="Internal").ap()
    sD = nc.dram_tensor("s_rows", [NW * P, D], F32, kind="Internal").ap()

    with ExitStack() as ctx:
        def sb(name, shape, dt):
            return ctx.enter_context(nc.sbuf_tensor(name, shape, dt))

        sems = {}

        def sem(name):
            if name not in sems:
                sems[name] = ctx.enter_context(nc.semaphore(name))
            return sems[name]

        nodes = sb("nodes", [P, NW * AC], F32)
        rows = sb("rows", [P, 16 * NSP + 8], F32)
        alpha = sb("alpha", [P, NSP * H], F32)
        srcC = sb("srcC", [P, NSP], U32)
        relC = sb("relC", [P, NSP], F32)
        relR = sb("relR", [P, NSP], F32)
        absR = sb("absR", [P, NSP], F32)
        work = sb("work", [P, 9280], F32)
        wrow = sb("wrow", [1, NSP], U32)
        w_gnn = sb("w_gnn", [P, 2, 4 * D], F32)
        w_mix = sb("w_mix", [P, 2, 3 * D], F32)
        w_f1 = w_gnn[:, :, 0:MH]
        w_f2 = sb("w_f2", [P, MH // P, D], F32)
        w_qf = w_mix[:, :, 0:D]
        b_gnn = sb("b_gnn", [P, 4 * D], F32)
        b_mix = sb("b_mix", [P, 3 * D], F32)
        emb = sb("emb", [NTYPE, D], F32)
        ident = sb("ident", [P, P], F32)
        iota_f = sb("iota_f", [P, P], F32)
        iota_p = sb("iota_p", [P, 1], F32)
        ones = sb("ones", [P, 1], F32)
        r4 = sb("r4", [P, NK], F32)
        stats = sb("stats", [P, NW * 6], F32)
        mv = sb("mv", [P, NW * 2], F32)
        rstd = sb("rstd", [P, NW], F32)
        tiny = sb("tiny", [P, 160], F32)

        gramK = sb("gramK", [P, 2 * P], F32)
        ends_all = sb("ends_all", [P, 6 * NB * H], F32)

        ps = ctx.enter_context(nc.psum_tensor("ps", [P, 8 * 512], F32))

        def bank(i, a=0, b=512):
            return ps[:, 512 * i + a:512 * i + b]

        def slot(i, n=1):
            return rows[:, i * NSP:(i + n) * NSP]

        iota_s = slot(0)
        cmp = slot(1)
        hs_i = slot(2).bitcast(I32)
        hy_i = slot(3).bitcast(I32)
        lo_i = slot(4).bitcast(I32)
        hi_i = slot(5).bitcast(I32)
        key_f = slot(6)
        lo_f = slot(7)
        sg_i = slot(8).bitcast(I32)
        dg_i = slot(9).bitcast(I32)
        sg_f = slot(10)
        iota8_i = rows[:, 11 * NSP:11 * NSP + NK * G].bitcast(I32)
        loh = [rows[:, 11 * NSP + 512 * b:11 * NSP + 512 * (b + 1)].bitcast(BF16) for b in range(2)]
        iota8 = rows[:, 13 * NSP:13 * NSP + NK * G // 2].bitcast(BF16)
        koh = [rows[:, 14 * NSP + NK * G // 2 * b:14 * NSP + NK * G // 2 * (b + 1)].bitcast(BF16) for b in range(2)]
        loC = slot(8)[:, 0:HT // 2].bitcast(BF16)
        keyC = slot(9)[:, 0:HT // 2].bitcast(BF16)
        relB = slot(10)[:, 0:NSP // 2].bitcast(BF16)
        assert NK * G <= 2 * NSP and NK * G // 2 <= NSP
        OC = next(c for c in range(1000, 1, -1) if (E - 1) % c == 0)
        OR = (E - 1) // OC
        assert OR < P and 3 * OC + P <= 9280
        o_this = work[0:OR, 0:OC].bitcast(I32)
        o_next = work[0:OR, OC:2 * OC].bitcast(I32)
        o_gt = work[0:OR, 2 * OC:3 * OC]
        o_row = work[0:1, 3 * OC:3 * OC + P]
        o_sum = tiny[:, 57:58]
        o_flag = tiny[0:1, 58:59].bitcast(U32)
        t_row = work[:, 0:P].bitcast(I32)
        t_rowf = work[:, P:2 * P]
        t_col = work[:, 2 * P:2 * P + 2].bitcast(I32)
        t_colf = work[:, 2 * P + 2:2 * P + 3]
        t_next = work[:, 2 * P + 3:2 * P + 4]
        t_place = work[:, 2 * P + 4:2 * P + 5]
        t_place_u = work[:, 2 * P + 5:2 * P + 6].bitcast(U32)
        t_dst_u = work[:, 2 * P + 6:2 * P + 7].bitcast(U32)
        t_cnt = work[:, 3 * P:5 * P].rearrange("p (q e) -> p q e", q=2)
        t_low = work[:, 5 * P:6 * P]
        t_table = work[0:NW, 6 * P:7 * P]
        t_base = [work[0:NW, 7 * P + P * i:8 * P + P * i] for i in range(2)]
        last_i = tiny[:, 0:8].bitcast(I32)
        last_w = tiny[:, 8:16].bitcast(I32)
        stepkey = tiny[:, 16:24]
        tcol = tiny[:, 24:32]
        icol = tiny[:, 32:40]
        wcol = tiny[:, 40:48]
        tcol_u = tiny[:, 48:56].bitcast(U32)
        padS = tiny[0:1, 56:57].bitcast(I32)
        count = tiny[:, 64:64 + NW]

        xs = [work[:, 256 * k:256 * (k + 1)] for k in range(2)]
        xp = [work[:, 512 + 256 * k:512 + 256 * (k + 1)] for k in range(2)]
        xT = [work[:, 1024 + 512 * k:1024 + 512 * (k + 1)] for k in range(2)]
        kS = [work[:, 2048 + 256 * k:2048 + 256 * (k + 1)] for k in range(2)]
        vsS = [work[:, 2560 + 512 * k:2560 + 512 * (k + 1)] for k in range(2)]
        mkv = [work[:, 3584 + 512 * k:3584 + 512 * (k + 1)] for k in range(2)]
        r4s = [work[:, 4608 + 4 * k:4608 + 4 * (k + 1)] for k in range(2)]
        r4T = [work[0:NTYPE, 4616 + 128 * k:4616 + 128 * (k + 1)] for k in range(2)]
        gramS = work[:, 4900:4900 + 256]

        kv = [work[:, HG * AC * b:HG * AC * (b + 1)].rearrange("p (g a) -> p g a", a=AC) for b in range(KV)]
        oh = [work[:, 2 * G * AC + G * P * b:2 * G * AC + G * P * (b + 1)] for b in range(2)]
        relq = [work[:, 2 * G * AC + 2 * G * P + G * P // 2 * b:2 * G * AC + 2 * G * P + G * P // 2 * (b + 1)].bitcast(BF16) for b in range(2)]
        ohh = [work[:, 2 * G * AC + HG * P * b:2 * G * AC + HG * P * (b + 1)] for b in range(4)]
        idx = [tiny[:, 128 + G * b:128 + G * (b + 1)].bitcast(U32) for b in range(2)]
        assert 2 * G * AC + 3 * G * P <= 9280

        RW = H * NSP
        atR = rows[:, 0:RW]
        fwR = rows[:, RW:2 * RW]
        bwR = rows[:, 2 * RW:3 * RW]
        penR = rows[:, 3 * RW:4 * RW]
        penN = rows[:, 3 * RW + 1:4 * RW + 1]
        ends = [ends_all[:, i * NB * H:(i + 1) * NB * H] for i in range(4)]
        saved = [ends_all[:, (4 + i) * NB * H:(5 + i) * NB * H] for i in range(2)]

        base_w = absR[0:1, 0:NSP // HG].bitcast(U32)
        base_f = absR[0:1, NSP // 2:NSP // 2 + NSP // HG]
        slot_w = relR[0:1, :].bitcast(U32)
        zeros = absR[:, NSP - AC // 2:NSP].bitcast(BF16)
        assert NSP // 2 + NSP // HG <= NSP - AC // 2

        def line(i):
            return nodes[0:H, i * NSP:(i + 1) * NSP]
        carry = [line(8), line(9)]

        def slot_n(i):
            return nodes[:, i * NSP:(i + 1) * NSP]

        def cut(t, at, n):
            return t[:, at:at + n]
        W4 = TG * D
        m_xn = [cut(rows, W4 * b, W4) for b in range(2)]
        m_x = [cut(rows, W4 * (2 + b), W4) for b in range(2)]
        m_s = [cut(rows, W4 * (4 + b), W4) for b in range(2)]
        m_x1 = cut(rows, W4 * 6, W4)
        m_T = cut(rows, W4 * 7, W4)
        m_hT = cut(rows, W4 * 8, W4)
        m_gT = cut(rows, W4 * 9, NM * TG * P)
        assert W4 * 9 + NM * TG * P <= 16 * NSP
        m_col = sb("m_col", [P, 16], F32)
        spare = sb("spare", [P, 2], F32)
        m_st = sb("m_st", [P, TG * 6], F32)
        m_mv = sb("m_mv", [P, TG * 2], F32)
        m_rs = sb("m_rs", [P, TG], F32)
        a_sm = cut(work, 0, 2 * C)
        a_bd = cut(work, 128, 2 * P)
        a_T = cut(work, 384, 2 * P)
        a_wT = cut(work, 640, 4 * P)
        a_bT = cut(work, 1152, 2 * P)
        a_row = cut(work, 1408, P)
        a_v = [cut(work, 1536 + 2 * i, 2) for i in range(4)]

        e_w = [rows[:, NE * NF * D * i:NE * NF * D * (i + 1)].rearrange("p (e k n) -> p e k n", e=NE, k=NF) for i in range(3)]
        at = 3 * NE * NF * D
        e_bo = rows[0:NE, at:at + D]
        e_wr = rows[:, at + D:at + D + NF * NE].rearrange("p (k n) -> p k n", k=NF)
        e_br = cut(rows, at + D + 16, NE)
        e_prow = [cut(rows, at + D + 32 + P * i, P) for i in range(2)]
        e_par = [cut(rows, at + D + 32 + 2 * P + 80 * i, 80) for i in range(2)]
        e_sc = [cut(rows, at + D + 448 + 16 * i, 16) for i in range(2)]
        e_sh = [cut(rows, at + D + 480 + 16 * i, 16) for i in range(2)]
        assert at + D + 512 <= 16 * NSP
        f_T = [cut(work, W4 * b, W4) for b in range(2)]
        f_h1 = [cut(work, W4 * (2 + b), W4) for b in range(2)]
        f_h2 = [cut(work, W4 * (4 + b), W4) for b in range(2)]
        f_y = [cut(work, W4 * (6 + b), W4) for b in range(2)]
        f_z = cut(work, W4 * 8, W4)
        f_res = [cut(alpha, W4 * b, W4) for b in range(2)]
        f_wT = alpha[0:NE, W4 * 2:W4 * 2 + TG * P]
        f_lg = cut(ends_all, 0, TG * NE)
        f_w = [cut(ends_all, 32 + 32 * b, TG * NE) for b in range(2)]
        f_rc = cut(ends_all, 96, TG * H)
        f_m = cut(ends_all, 112, TG)
        f_st, f_mv, f_rs = m_st, m_mv, m_rs

        def on_rows(eng, e, name):
            state = [0]

            def link(ins):
                state[0] += 1
                ins.then_inc(sem(name), 1)
                eng.wait_ge(sem(name), state[0])
            return link

        block = ctx.enter_context(nc.Block())

        @block.sync
        def _(sp):
            sp.dma_start(o_this, dst[0:E - 1].rearrange("(a b) -> a b", b=OC)).then_inc(sem("order_in"), 16)
            sp.dma_start(o_next, dst[1:E].rearrange("(a b) -> a b", b=OC)).then_inc(sem("order_in"), 16)
            sp.dma_start(srcS[0:E].rearrange("(a b) -> a b", a=160), src.rearrange("(a b) -> a b", a=160)).then_inc(sem("edges"), 16)
            sp.dma_start(dstS[0:E].rearrange("(a b) -> a b", a=160), dst.rearrange("(a b) -> a b", a=160)).then_inc(sem("edges"), 16)
            sp.wait_ge(sem("pads_set"), 1)
            one = lambda t, a, b: t[a:b].rearrange("(a b) -> a b", a=1)
            sp.dma_start(one(srcS, E, (ET + 1) * P), iota8_i[0:1, 0:(ET + 1) * P - E]).then_inc(sem("edges"), 16)
            sp.dma_start(one(dstS, E, ET * P), iota8_i[0:1, 256:256 + ET * P - E]).then_inc(sem("edges"), 16)
            sp.dma_start(one(dstS, ET * P, (ET + 1) * P), iota8_i[0:1, 384:384 + P]).then_inc(sem("edges"), 16)
            sp.wait_ge(sem("order_seen"), 1)
            sp.dma_start(downD[0:OR].rearrange("(a b) -> a b", b=1), o_sum[0:OR, :]).then_inc(sem("order_out"), 16)
            sp.wait_ge(sem("order_out"), 16)
            sp.dma_start(o_row[:, 0:OR], downD[0:OR].rearrange("(a b) -> a b", a=1)).then_inc(sem("order_row"), 16)
            sp.wait_ge(sem("x_pad_set"), 1)
            for c in range(4):
                n = (NW - 1) // 4
                sp.dma_start(nodes[:, c * n * D:(c + 1) * n * D].rearrange("p (t d) -> p t d", d=D),
                             x[c * n * P:(c + 1) * n * P, :].rearrange("(t p) d -> p t d", p=P)).then_inc(sem("x_in"), 16)
            sp.dma_start(nodes[0:TAIL, (NW - 1) * D:NW * D], x[(NW - 1) * P:N, :]).then_inc(sem("x_in"), 16)
            sp.wait_ge(sem("hist_pad"), 1)
            for t, o in ((src, hs_i), (etype, hy_i)):
                sp.dma_start(o[:, 0:FB * P].rearrange("p (b e) -> p b e", b=FB),
                             t[0:FB * P * P].rearrange("(b p e) -> p b e", b=FB, p=P)).then_inc(sem("hist_in"), 16)
                sp.dma_start(o[0:FR, FB * P:(FB + 1) * P],
                             t[FB * P * P:FE * P].rearrange("(p e) -> p e", p=FR)).then_inc(sem("hist_in"), 16)
                sp.dma_start(o[FR:FR + 1, FB * P:FB * P + EREST],
                             t[FE * P:E].rearrange("(p e) -> p e", p=1)).then_inc(sem("hist_in"), 16)
            sp.wait_ge(sem("edges_sorted"), 1)
            sp.wait_ge(sem("last_pad"), 1)
            lastd = dstS[0:ET * P].rearrange("(t e) -> t e", e=P)
            for b in range(NB):
                n = min(P, ET - b * P)
                sp.dma_start(last_i[0:n, b:b + 1], lastd[b * P:b * P + n, P - 1:P], allow_slow_non_contiguous=True).then_inc(sem("last_in"), 16)
            for i, w in enumerate((Wq, Wk, Wv, Ws)):
                sp.dma_start(w_gnn[:, :, i * D:(i + 1) * D], w.rearrange("(k p) n -> p k n", p=P)).then_inc(sem("w_in"), 16)
            sp.dma_start(w_mix[:, :, :], w_qkv.rearrange("(k p) n -> p k n", p=P)).then_inc(sem("w_in"), 16)
            for i, w in enumerate((bq, bk, bv, bs)):
                sp.dma_start(b_gnn[:, i * D:(i + 1) * D], w.rearrange("(a n) -> a n", a=1).partition_broadcast(P)).then_inc(sem("w_in"), 16)
            sp.dma_start(b_mix[:, :], b_qkv.rearrange("(a n) -> a n", a=1).partition_broadcast(P)).then_inc(sem("w_in"), 16)
            sp.dma_start(emb[:, :], edge_emb).then_inc(sem("w_in"), 16)
            sp.wait_ge(sem("relB_made"), 1)
            sp.dma_start(relD.rearrange("(b p) e -> p b e", p=P), relB.rearrange("p (b e) -> p b e", b=NB)).then_inc(sem("rel_out"), 16)
            sp.wait_ge(sem("xn_made"), NW)
            sp.dma_start(xnD.rearrange("(t p) d -> p t d", p=P), nodes[:, 0:NW * D].rearrange("p (t d) -> p t d", d=D)).then_inc(sem("xn_out"), 16)
            sp.wait_ge(sem("xn_out"), 16)
            sp.sem_inc(sem("xn_stored"), 1)
            sp.sem_inc(sem("stored"), CREDIT)

            def store(t, k):
                sp.wait_ge(sem("qk_sb"), done(t))
                sp.dma_start(kD[ds(t * P, P), :], kS[k]).then_inc(sem("proj_out"), 16)
                sp.wait_ge(sem("vs_sb"), done(t))
                sp.dma_start(vD[ds(t * P, P), :], vsS[k][:, 0:D]).then_inc(sem("proj_out"), 16)
                sp.dma_start(sD[ds(t * P, P), :], vsS[k][:, D:2 * D]).then_inc(sem("proj_out"), 16)
                sp.wait_ge(sem("proj_out"), t * 48 + 48)
                sp.sem_inc(sem("stored"), 1)
            with sp.Fori(0, NW // 2) as it:
                for k in range(2):
                    store(it * 2 + k, k)
            store(NW - 1, 0)
            sp.wait_ge(sem("gram_sb"), 1)
            for i, (w, n) in enumerate(((norm_g, NF), (norm_b, NF), (b_fc1, NM))):
                sp.dma_start(a_row[NF * i:NF * i + n, :], w.rearrange("(k p) -> k p", p=P)).then_inc(sem("mix_in"), 16)
            sp.dma_start(b_mix[:, D:2 * D], b_fc2.rearrange("(a n) -> a n", a=1).partition_broadcast(P)).then_inc(sem("mix_in"), 16)
            sp.dma_start(w_f1, w_fc1.rearrange("(k p) n -> p k n", p=P)).then_inc(sem("mix_in"), 16)
            sp.dma_start(w_f2[:, :, :], w_fc2.rearrange("(k p) n -> p k n", p=P)).then_inc(sem("mix_in"), 16)

            def rel_load(j, b):
                sp.wait_ge(sem("oh_made"), reuse(j, 2))
                sp.dma_start(relq[b], relD[ds(j * G, G), :].rearrange("(a g) e -> a (g e)", a=1).partition_broadcast(P)).then_inc(sem(f"relq_in{b}"), 16)

            def tiles(t, g, n):
                return t[ds(g * (TG * P), n * P), :].rearrange("(t p) d -> p t d", p=P)

            def mix_load(g, b, n):
                for t, o in ((xnD, m_xn[b]), (sD, m_s[b])):
                    sp.dma_start(o[:, 0:n * D].rearrange("p (t d) -> p t d", d=D), tiles(t, g, n)).then_inc(sem(f"mix_rows{b}"), 16)
                if n == TG:
                    sp.dma_start(m_x[b].rearrange("p (t d) -> p t d", d=D), tiles(x, g, n)).then_inc(sem(f"mix_rows{b}"), 16)
                else:
                    sp.dma_start(m_x[b][0:TAIL, 0:D], x[(NW - 1) * P:N, :]).then_inc(sem(f"mix_rows{b}"), 16)

            def mix_store(g, n):
                sp.wait_ge(sem("m_out"), done(g))
                sp.dma_start(tiles(resD, g, n), m_x1[:, 0:n * D].rearrange("p (t d) -> p t d", d=D)).then_inc(sem("res_out"), 16)
                sp.wait_ge(sem("res_out"), g * 16 + 16)
                sp.sem_inc(sem("res_stored"), 1)

            def pass1(g, b, nxt, before):
                for p in range(PIECES):
                    if g is not NG or p < PIECES - 2:
                        rel_load(g * PIECES + (p + 2), p % 2)
                    if p == 0 and before:
                        mix_store(g - 1, before)
                    if p == 1 and nxt:
                        if nxt == 1:
                            sp.wait_ge(sem("m_x_zero"), 1)
                        sp.wait_ge(sem("m_out"), reuse(g + 1, 2))
                        mix_load(g + 1, 1 - b, nxt)
            sp.sem_inc(sem("res_stored"), CREDIT)
            sp.wait_ge(sem("rel_out"), 16)
            sp.wait_ge(sem("att_used"), 1)
            rel_load(0, 0)
            rel_load(1, 1)
            mix_load(0, 0, TG)
            pass1(0, 0, TG, 0)
            with sp.Fori(0, NG // 2 - 1) as it:
                for b in range(2):
                    pass1(it * 2 + (b + 1), 1 - b, TG, TG)
            pass1(NG - 1, 1, 1, TG)
            pass1(NG, 0, 0, TG)
            mix_store(NG, 1)

            sp.wait_ge(sem("ex_cols"), 1)
            for i, w in enumerate((W1, W2, Wo)):
                sp.dma_start(rows[:, NE * NF * D * i:NE * NF * D * (i + 1)].rearrange("p (e n) -> p e n", n=D), w.rearrange("e (k p) n -> p (e k) n", p=P)).then_inc(sem("exp_in"), 16)
            sp.dma_start(e_bo, bo).then_inc(sem("exp_in"), 16)
            sp.dma_start(e_wr, Wr.rearrange("(k p) n -> p k n", p=P)).then_inc(sem("exp_in"), 16)
            sp.dma_start(e_br, br.rearrange("(a n) -> a n", a=1).partition_broadcast(P)).then_inc(sem("exp_in"), 16)
            for l, ws in enumerate(((g1, b1, be1, m1, v1), (g2, b2, be2, m2, v2))):
                for i, w in enumerate(ws):
                    sp.dma_start(e_prow[l][16 * i:16 * (i + 1), :], w.rearrange("e (k p) -> (e k) p", p=P)).then_inc(sem("exp_in"), 16)

            def res_load(g, b, n):
                sp.dma_start(f_res[b][:, 0:n * D].rearrange("p (t d) -> p t d", d=D), tiles(resD, g, n)).then_inc(sem(f"res_in{b}"), 16)

            def out_store(g, b, n):
                sp.wait_ge(sem("y_made"), done(g * NE + (NE - 1)))
                if n == TG:
                    sp.dma_start(tiles(out, g, n), f_y[b].rearrange("p (t d) -> p t d", d=D)).then_inc(sem("out_sent"), 16)
                else:
                    sp.dma_start(out[(NW - 1) * P:N, :], f_y[b][0:TAIL, 0:D]).then_inc(sem("out_sent"), 16)
                sp.wait_ge(sem("out_sent"), g * 16 + 16)
                sp.sem_inc(sem("y_stored"), 1)
            sp.sem_inc(sem("y_stored"), CREDIT)
            sp.wait_ge(sem("acc_made"), done(NHF - 1))
            res_load(0, 0, TG)
            res_load(1, 1, TG)

            def experts(g, b, n, later):
                if later:
                    sp.wait_ge(sem("y_init"), done(g))
                    res_load(g + 2, b, later)
                out_store(g, b, n)
            with sp.Fori(0, NG // 2 - 1) as it:
                for b in range(2):
                    experts(it * 2 + b, b, TG, TG)
            experts(NG - 2, 0, TG, 1)
            experts(NG - 1, 1, TG, 0)
            experts(NG, 0, 1, 0)
            sp.wait_ge(sem("out_sent"), 16 * (NG + 1))

        @block.gpsimd
        def _(pool):
            pool.iota(iota_s, pattern=[[1, NSP]], base=0, channel_multiplier=0, allow_small_or_imprecise_dtypes=True).then_inc(sem("iotas"), 1)
            pool.iota(iota_f[:, :], pattern=[[1, P]], base=0, channel_multiplier=0, allow_small_or_imprecise_dtypes=True).then_inc(sem("iotas"), 1)
            pool.iota(iota_p[:, :], pattern=[[0, 1]], base=0, channel_multiplier=1, allow_small_or_imprecise_dtypes=True).then_inc(sem("iotas"), 1)
            pool.iota(icol[:, 0:NB], pattern=[[P, NB]], base=0, channel_multiplier=1, allow_small_or_imprecise_dtypes=True).then_inc(sem("iotas"), 1)
            pool.memset(ident[:, :], 0.0).then_inc(sem("ident"), 1)
            pool.wait_ge(sem("ident"), 1)
            pool.affine_select(out=ident[:, :], in_=ident[:, :], compare_op=ALU.not_equal, fill=1.0,
                               base=0, pattern=[[-1, P]], channel_multiplier=1).then_inc(sem("ident"), 1)
            pool.memset(ones[:, :], 1.0).then_inc(sem("iotas"), 1)
            pool.wait_ge(sem("edges"), 80)
            pool.iota(iota8_i, pattern=[[1, NK], [0, G]], base=0, channel_multiplier=0).then_inc(sem("iotas"), 1)

            def settled(ins):
                ins.then_inc(sem("sort_step"), 1)
                pool.wait_ge(sem("sort_step"), 1)
                pool.sem_clear(sem("sort_step"))

            sent = [0, "table_moves"]

            def moved(ins):
                sent[0] = sent[0] + 1
                ins.then_inc(sem(sent[1]), 16)
                pool.wait_ge(sem(sent[1]), sent[0] * 16)
                pool.sem_inc(sem("sort_seen"), 1)

            def offset(t):
                return bass.IndirectOffsetOnAxis(ap=t, axis=0)

            def tally(t):
                e = dstS[ds(t * P, P)]
                moved(pool.dma_start(t_row, e.rearrange("(a b) -> a b", a=1).partition_broadcast(P)))
                moved(pool.dma_start(t_col[:, 0:1], e.rearrange("(a b) -> a b", b=1)))
                pool.tensor_copy(t_rowf, t_row)
                pool.tensor_copy(t_dst_u, t_col[:, 0:1])
                settled(pool.tensor_copy(t_colf, t_col[:, 0:1]))
                settled(pool.tensor_scalar(t_cnt[:, 0, :], t_rowf, t_colf, None, ALU.is_equal))
                settled(pool.tensor_tensor(t_cnt[:, 1, :], t_cnt[:, 0, :], t_low, ALU.mult))
                n = P // 2
                while n:
                    settled(pool.tensor_tensor(t_cnt[:, :, 0:n], t_cnt[:, :, 0:n], t_cnt[:, :, n:2 * n], ALU.add))
                    n //= 2
                moved(pool.indirect_dma_start(out=t_next, out_offset=None, in_=table1, in_offset=offset(t_dst_u)))

            def advance():
                settled(pool.tensor_tensor(t_next, t_next, t_cnt[:, 0, 0:1], ALU.add))
                moved(pool.indirect_dma_start(out=table1, out_offset=offset(t_dst_u), in_=t_next, in_offset=None))

            table1 = nextD.rearrange("(a b) -> a b", b=1)
            table2 = nextD.rearrange("(a b) -> a b", b=P)
            pool.wait_ge(sem("order_flag"), 1)
            _, unsorted = nc.values_load_multi_w_load_instructions(o_flag, engines=(pool.engine,), min_val=0, max_val=1)
            with pool.If(unsorted[0]):
                settled(pool.tensor_scalar(t_low, iota_f[:, :], iota_p[:, 0:1], None, ALU.is_lt))
                settled(pool.memset(t_table, 0.0))
                moved(pool.dma_start(table2, t_table))
                base_moves = sent[:]
                with pool.Fori(0, ET) as t:
                    sent[:] = [t * 4, "count_moves"]
                    tally(t)
                    advance()
                sent[:] = base_moves
                moved(pool.dma_start(t_table, table2))
                settled(pool.tensor_copy(t_base[0], t_table))
                src_, n = 0, 1
                while n < P:
                    settled(pool.tensor_copy(t_base[1 - src_], t_base[src_]))
                    settled(pool.tensor_tensor(t_base[1 - src_][:, n:P], t_base[src_][:, n:P], t_base[src_][:, 0:P - n], ALU.add))
                    src_, n = 1 - src_, 2 * n
                incl = t_base[src_]
                settled(pool.tensor_tensor(t_base[1 - src_], incl, t_table, ALU.subtract))
                tot = [work[0:1, 9 * P + P * i:10 * P + P * i] for i in range(3)]
                settled(pool.memset(tot[0], 0.0))
                moved(pool.dma_start(srcT[0:NW].rearrange("(a b) -> a b", b=1).bitcast(F32), incl[:, P - 1:P]))
                moved(pool.dma_start(tot[0][:, 0:NW], srcT[0:NW].rearrange("(a b) -> a b", a=1).bitcast(F32)))
                settled(pool.tensor_copy(tot[1], tot[0]))
                q, n = 1, 1
                while n < NW:
                    settled(pool.tensor_copy(tot[3 - q], tot[q]))
                    settled(pool.tensor_tensor(tot[3 - q][:, n:P], tot[q][:, n:P], tot[q][:, 0:P - n], ALU.add))
                    q, n = 3 - q, 2 * n
                settled(pool.tensor_tensor(tot[q], tot[q], tot[0], ALU.subtract))
                moved(pool.dma_start(srcT[0:NW].rearrange("(a b) -> a b", a=1).bitcast(F32), tot[q][:, 0:NW]))
                moved(pool.dma_start(t_colf[0:NW, :], srcT[0:NW].rearrange("(a b) -> a b", b=1).bitcast(F32)))
                settled(pool.tensor_scalar(t_base[1 - src_], t_base[1 - src_], t_colf[0:NW, :], None, ALU.add))
                moved(pool.dma_start(table2, t_base[1 - src_]))
                base_moves = sent[:]
                with pool.Fori(0, ET) as t:
                    sent[:] = [t * 4, "place_moves"]
                    tally(t)
                    sent[:] = [t * 3, "edge_moves"]
                    moved(pool.dma_start(t_col[:, 1:2], srcS[ds(t * P, P)].rearrange("(a b) -> a b", b=1)))
                    settled(pool.tensor_tensor(t_place, t_next, t_cnt[:, 1, 0:1], ALU.add))
                    settled(pool.tensor_copy(t_place_u, t_place))
                    for i, o in ((0, dstT), (1, srcT)):
                        moved(pool.indirect_dma_start(out=o.rearrange("(a b) -> a b", b=1), out_offset=offset(t_place_u), in_=t_col[:, i:i + 1], in_offset=None))
                    sent[:] = [t * 4 + 3, "place_moves"]
                    advance()
                sent[:] = base_moves
                for a, o in ((dstT, dstS), (srcT, srcS)):
                    moved(pool.dma_start(o[0:ET * P].rearrange("(a b) -> a b", b=P), a.rearrange("(a b) -> a b", b=P)))
            pool.sem_inc(sem("edges_sorted"), 1)
            pool.wait_ge(sem("steps"), 1)
            for b in range(NB):
                for t, o in ((srcS, sg_i), (dstS, dg_i)):
                    pool.indirect_dma_start(out=o[:, b * P:(b + 1) * P], out_offset=None, in_=t.rearrange("(t e) -> t e", e=P),
                                            in_offset=bass.IndirectOffsetOnAxis(ap=tcol_u[:, b:b + 1], axis=0)).then_inc(sem("rows_in"), 16)

            def gather(j, b, m, table):
                pool.wait_ge(sem("kv_used"), j * 2 + 1)
                pool.tensor_copy(idx[b], srcC[:, ds(m * G, G)]).then_inc(sem("idx_made"), 1)
                pool.wait_ge(sem("idx_made"), j + 1)
                pool.sem_inc(sem("gathers_begun"), 1)
                for h in range(2):
                    if h:
                        pool.wait_ge(sem("kv_used"), j * 2 + (h + 1))
                        pool.sem_inc(sem("gathers_begun"), 1)
                    for g in range(HG):
                        pool.indirect_dma_start(out=kv[2 * b + h][:, g, 0:D], out_offset=None, in_=table,
                                                in_offset=bass.IndirectOffsetOnAxis(ap=idx[b][:, HG * h + g:HG * h + g + 1], axis=0)).then_inc(sem(f"kv_in{2 * b + h}"), 16)

            pool.sem_inc(sem("kv_used"), KV)
            pool.wait_ge(sem("proj_out"), NW * 48)
            pool.wait_ge(sem("srcC_made"), 1)
            pool.wait_ge(sem("att_used"), 1)
            with pool.Fori(0, NGR // 2) as it:
                for b in range(2):
                    gather(it * 2 + b, b, it * 2 + b, kD)
            with pool.Fori(0, NGR // 2) as it:
                for b in range(2):
                    gather(it * 2 + (b + NGR), b, it * 2 + b, vD)

        @block.scalar
        def _(act):
            act.sem_inc(sem("a_in"), CREDIT)
            act.sem_inc(sem("r4T_sb"), CREDIT)
            act.sem_inc(sem("xT_sb"), CREDIT)
            act.wait_ge(sem("var_eps"), 1)
            act.activation(rstd[:, :], rstd[:, :], ACT.Sqrt).then_inc(sem("std"), 1)
            act.wait_ge(sem("xn_made"), NW)
            act.wait_ge(sem("r4_made"), 1)

            def front(t, k):
                act.wait_ge(sem("xT_ps"), reuse(t, 2))
                act.activation(xs[k], nodes[:, ds(t * D, D)], ACT.Copy)
                act.activation(r4s[k], r4[:, ds(t * NTYPE, NTYPE)], ACT.Copy).then_inc(sem("a_in"), 1)
                act.wait_ge(sem("r4T_ps"), done(t))
                act.activation(r4T[k], bank(k, 0, P)[0:NTYPE, :], ACT.Copy).then_inc(sem("r4T_sb"), 1)
                act.wait_ge(sem("xT_ps"), done(t))
                act.wait_ge(sem("gram_ps"), reuse(t, 2))
                act.activation(xT[k], bank(2 + k), ACT.Copy).then_inc(sem("xT_sb"), 1)
            front(0, 0)
            with act.Fori(0, NW // 2) as it:
                front(it * 2 + 1, 1)
                front(it * 2 + 2, 0)
            act.sem_inc(sem("m_T_sb"), CREDIT)
            act.sem_inc(sem("m_std"), CREDIT)
            act.sem_inc(sem("gelu"), CREDIT)
            act.wait_ge(sem("a_neg"), 1)
            for i in range(2):
                act.activation(a_sm[:, i * C:(i + 1) * C], a_sm[:, i * C:(i + 1) * C], ACT.Exp, bias=a_v[1][:, i:i + 1],
                               scale=1.0 / C ** 0.5, accum_out=a_v[2][:, i:i + 1]).then_inc(sem("a_exp"), 1)

            def mix(g, p, n):
                if p == 0:
                    act.wait_ge(sem("m_T_ps"), done(g))
                    for i in range(NF):
                        ins = act.activation(m_T[:, i * TG * P:i * TG * P + n * P], bank(4 + i, 0, n * P), ACT.Copy)
                    ins.then_inc(sem("m_T_sb"), 1)
                if p == 1:
                    act.wait_ge(sem("m_var"), done(g))
                    act.activation(m_rs[:, 0:n], m_rs[:, 0:n], ACT.Sqrt).then_inc(sem("m_std"), 1)
                if p in (4, 5):
                    for i in range(NM // 2):
                        m = NM // 2 * (p - 4) + i
                        act.wait_ge(sem("fc1_ps"), done(g * NM + m))
                        act.activation(m_gT[:, m * TG * P:m * TG * P + n * P], bank(4 + m % 2, 0, n * P), ACT.Gelu,
                                       bias=m_col[:, 2 * NF + m:2 * NF + m + 1]).then_inc(sem("gelu"), 1)

            def pass1(g, n):
                for p in range(PIECES):
                    mix(g, p, n)
            with act.Fori(0, NG // 2) as it:
                for b in range(2):
                    pass1(it * 2 + b, TG)
            pass1(NG, 1)

            act.wait_ge(sem("shifted"), 1)
            act.activation(atR, atR, ACT.Exp).then_inc(sem("ex_made"), 1)
            act.sem_inc(sem("ex_in"), CREDIT)
            act.wait_ge(sem("ex_cols"), 1)
            with act.Fori(0, NHF // KV) as it:
                for b in range(KV):
                    i = it * KV + b
                    act.wait_ge(sem("kv_used"), i + (NHF + 1))
                    act.activation(kv[b][:, :, D:AC], alpha[:, ds(i * (HG * H), HG * H)].rearrange("p (g h) -> p g h", g=HG), ACT.Copy).then_inc(sem("ex_in"), 1)

            for q in ("f_std", "f_T_sb", "f_exp", "f_wT_sb", "h1_sb", "h2_sb"):
                act.sem_inc(sem(q), CREDIT)
            act.wait_ge(sem("e_var"), 1)
            for l in range(2):
                ins = act.activation(e_sc[l], e_sc[l], ACT.Sqrt)
            ins.then_inc(sem("e_std"), 1)

            def first_part(g, b, n, q):
                if q == 0:
                    act.wait_ge(sem("f_var"), done(g))
                    act.activation(f_rs[:, 0:n], f_rs[:, 0:n], ACT.Sqrt).then_inc(sem("f_std"), 1)
                if q == 2:
                    act.wait_ge(sem("f_T_ps"), done(g))
                    for i in range(NF):
                        ins = act.activation(f_T[b][:, i * TG * P:i * TG * P + n * P], bank(6 + i, 0, n * P), ACT.Copy)
                    ins.then_inc(sem("f_T_sb"), 1)
                if q == 4:
                    act.wait_ge(sem("f_sub"), done(g))
                    act.activation(f_lg[:, 0:n * NE], f_lg[:, 0:n * NE], ACT.Exp).then_inc(sem("f_exp"), 1)
                if q == 5:
                    act.wait_ge(sem("f_wT_ps"), done(g))
                    act.activation(f_wT[:, 0:n * P], bank(6, 0, n * P)[0:NE, :], ACT.Copy).then_inc(sem("f_wT_sb"), 1)

            def layer(l, u, e, n):
                s_ps, s_sb, o = (("l1_ps", "h1_sb", f_h1), ("l2_ps", "h2_sb", f_h2))[l]
                for m in range(NF):
                    act.wait_ge(sem(s_ps), done(u * NF + m))
                    if m == 0 and l == 0:
                        act.wait_ge(sem("l2_ps"), u * NF + 1)
                    if m == 0 and l == 1:
                        act.wait_ge(sem("l3_ps"), reuse(u, 2))
                    act.activation(o[e % 2][:, m * TG * P:m * TG * P + n * P], bank(2 * l + m, 0, n * P), ACT.Relu,
                                   bias=e_sh[l][:, e * NF + m:e * NF + m + 1], scale=e_sc[l][:, e * NF + m:e * NF + m + 1]).then_inc(sem(s_sb), 1)

            def experts(g, b, n, nxt):
                for e in range(NE):
                    layer(1, g * NE + e, e, n)
                    if e < NE - 1 or nxt:
                        layer(0, g * NE + (e + 1), (e + 1) % NE, n if e < NE - 1 else nxt)
                    if nxt:
                        first_part(g + 1, 1 - b, nxt, e)
            for q in range(NE):
                first_part(0, 0, TG, q)
            layer(0, 0, 0, TG)
            with act.Fori(0, NG // 2 - 1) as it:
                for b in range(2):
                    experts(it * 2 + b, b, TG, TG)
            experts(NG - 2, 0, TG, TG)
            experts(NG - 1, 1, TG, 1)
            experts(NG, 0, 1, 0)

        @block.tensor
        def _(pe):
            for s in ("r4T_ps", "es_ps", "xT_ps", "qk_ps", "vs_ps", "mkv_ps", "gram_ps", "hist_ps", "qg_ps", "agg_ps", "m_T_ps", "x1_ps", "m_hT_ps", "fc1_ps",
                      "fc2_ps", "f_T_ps", "lg_ps", "f_wT_ps", "bo_ps", "l1_ps", "l2_ps", "l3_ps"):
                pe.sem_inc(sem(s), CREDIT)
            pe.wait_ge(sem("cmp_made"), 1)
            pe.wait_ge(sem("iotas"), 5)
            for b in range(NB):
                pe.matmul(bank(0, b, b + 1), cmp[:, b * P:(b + 1) * P], ones[:, :], start=True, stop=True)
            for h in range(2):
                w = NSP // 2
                last = pe.matmul(bank(1 + h, 0, w)[0:1, :], ones[:, :], cmp[:, h * w:(h + 1) * w], start=True, stop=True)
            last.then_inc(sem("tcol_ps"), 1)
            pe.wait_ge(sem("ident"), 2)

            def turn(rowsrc, first):
                for b in range(NB):
                    last = pe.transpose(bank(first + b // 4, (b % 4) * P, (b % 4 + 1) * P), rowsrc[:, b * P:(b + 1) * P], ident[:, :])
                return last
            pe.wait_ge(sem("hist_rows"), 1)
            turn(lo_f, 4).then_inc(sem("lo_ps"), 1)
            turn(key_f, 6).then_inc(sem("key_ps"), 1)
            pe.wait_ge(sem("rows_made"), 1)
            pe.wait_ge(sem("tcol_sb"), 1)
            turn(relR, 0).then_inc(sem("rel_ps"), 1)
            turn(sg_f, 2).then_inc(sem("src_ps"), 1)
            pe.wait_ge(sem("hist_z"), 1)
            pe.matmul(bank(4, 0, NK), loh[0][:, 0:P], koh[0][:, 0:NK], start=True, stop=False, skip_group_check=True)
            pe.matmul(bank(4, 0, NK), loh[0][:, 0:P], koh[0][:, 0:NK], start=False, stop=False, skip_group_check=True).then_inc(sem("hist_zero"), 1)
            with pe.Fori(0, HT // (2 * G)) as it:
                for b in range(2):
                    c = it * 2 + b
                    pe.wait_ge(sem("oneh"), done(c))
                    lo = loh[b].rearrange("p (n g) -> p g n", g=G)
                    ky = koh[b].rearrange("p (n g) -> p g n", g=G)
                    for g in range(G):
                        last = pe.matmul(bank(4, 0, NK), lo[:, g, :], ky[:, g, :], start=False, stop=False, skip_group_check=True)
                    last.then_inc(sem("hist_ps"), 1)

            pe.wait_ge(sem("w_in"), 176)
            pe.wait_ge(sem("xn_made"), NW)
            pe.wait_ge(sem("r4_made"), 1)
            pe.wait_ge(sem("srcC_made"), 1)
            pe.wait_ge(sem("gram0"), 1)
            pe.matmul(bank(7, 0, 256), gramS[:, 0:P], gramS[:, 0:256], start=True, stop=False, skip_group_check=True)

            def front(t, k):
                pe.wait_ge(sem("a_in"), done(t))
                pe.wait_ge(sem("xp_made"), reuse(t, 2))
                pe.transpose(bank(k, 0, P)[0:NTYPE, :], r4s[k], ident[:, :]).then_inc(sem("r4T_ps"), 1)
                pe.wait_ge(sem("r4T_sb"), done(t))
                pe.matmul(bank(k, P, P + D), r4T[k], emb[:, :], start=True, stop=True).then_inc(sem("es_ps"), 1)
                pe.wait_ge(sem("xp_made"), done(t))
                pe.wait_ge(sem("xT_sb"), reuse(t, 2))
                for i, s in enumerate((xs[k][:, 0:P], xs[k][:, P:D], xp[k][:, 0:P], xp[k][:, P:D])):
                    last = pe.transpose(bank(2 + k, i * P, (i + 1) * P), s, ident[:, :])
                last.then_inc(sem("xT_ps"), 1)

            def project(t, k, n):
                pe.wait_ge(sem("xT_sb"), done(t))
                for s_ps, s_sb, bk_, lhs, w in (("mkv_ps", "mkv_sb", 6, 0, w_mix[:, :, D:3 * D]),
                                                ("qk_ps", "qk_sb", 4, 2, w_gnn[:, :, 0:2 * D]),
                                                ("vs_ps", "vs_sb", 5, 2, w_gnn[:, :, 2 * D:4 * D])):
                    pe.wait_ge(sem(s_sb), reuse(t, 1))
                    for i in range(2):
                        last = pe.matmul(bank(bk_), xT[k][:, (lhs + i) * P:(lhs + i + 1) * P], w[:, i, :], start=(i == 0), stop=(i == 1))
                    last.then_inc(sem(s_ps), 1)
                pe.wait_ge(sem("mkv_sb"), done(t))
                for i in range(2):
                    last = pe.matmul(bank(7, i * P, (i + 1) * P), mkv[k][0:n, i * P:(i + 1) * P], mkv[k][0:n, D + i * P:D + (i + 1) * P],
                                     start=False, stop=False, skip_group_check=True)
                last.then_inc(sem("gram_ps"), 1)
            front(0, 0)
            with pe.Fori(0, NW // 2) as it:
                front(it * 2 + 1, 1)
                project(it * 2, 0, P)
                front(it * 2 + 2, 0)
                project(it * 2 + 1, 1, P)
            project(NW - 1, 0, TAIL)

            pe.wait_ge(sem("gram_sb"), 1)
            for a in range(2):
                for i in range(2):
                    last = pe.transpose(bank(2, (2 * i + a) * P, (2 * i + a + 1) * P), w_mix[:, a, i * P:(i + 1) * P], ident[:, :])
            for i in range(2):
                last = pe.transpose(bank(3, i * P, (i + 1) * P), b_mix[:, i * P:(i + 1) * P], ident[:, :])
            pe.wait_ge(sem("mix_in"), 96)
            n_ = 2 * NF + NM
            pe.transpose(bank(3, 2 * P, 2 * P + n_), a_row[0:n_, :], ident[0:n_, 0:n_]).then_inc(sem("a_turn"), 1)
            pe.wait_ge(sem("a_made"), 1)
            for i in range(2):
                last = pe.transpose(bank(0, i * P, (i + 1) * P), a_bd[:, i * P:(i + 1) * P], ident[:, :])
            last.then_inc(sem("aT_ps"), 1)
            pe.wait_ge(sem("aT_sb"), 1)
            for i in range(2):
                for a in range(2):
                    pe.matmul(bank(1, a * D + i * P, a * D + (i + 1) * P), a_wT[:, (2 * i + a) * P:(2 * i + a + 1) * P], a_T[:, i * P:(i + 1) * P], start=True, stop=True)
                last = pe.matmul(bank(0, D + i * P, D + (i + 1) * P), a_bT[:, i * P:(i + 1) * P], a_T[:, i * P:(i + 1) * P], start=True, stop=True)
            last.then_inc(sem("fold_ps"), 1)
            pe.wait_ge(sem("fold_sb"), 1)
            pe.wait_ge(sem("qk_sb"), done(NW - 1))
            pe.wait_ge(sem("vs_sb"), done(NW - 1))

            def mix(g, b, p, n):
                if p == 0:
                    pe.wait_ge(sem(f"mix_rows{b}"), (g - b) * 24 + 48)
                    pe.wait_ge(sem("gelu"), done(g * NM - 1))
                    for t in range(n):
                        for i in range(NF):
                            last = pe.transpose(bank(4 + i, t * P, (t + 1) * P), m_xn[b][:, t * D + i * P:t * D + (i + 1) * P], ident[:, :])
                    last.then_inc(sem("m_T_ps"), 1)
                if p == 1:
                    pe.wait_ge(sem("m_T_sb"), done(g))
                    pe.wait_ge(sem("m_out"), reuse(g, 1))
                    for t in range(n):
                        for i in range(NF):
                            last = pe.matmul(bank(6 + t // 2, t % 2 * D, (t % 2 + 1) * D), m_T[:, i * TG * P + t * P:i * TG * P + (t + 1) * P], w_qf[:, i, :], start=(i == 0), stop=(i == 1))
                    last.then_inc(sem("x1_ps"), 1)
                if p == 3:
                    pe.wait_ge(sem("m_z"), done(g))
                    for t in range(n):
                        for i in range(NF):
                            last = pe.transpose(bank(4 + i, t * P, (t + 1) * P), m_xn[b][:, t * D + i * P:t * D + (i + 1) * P], ident[:, :])
                    last.then_inc(sem("m_hT_ps"), 1)
                if p in (4, 5):
                    pe.wait_ge(sem("m_hT_sb"), done(g))
                    for k in range(NM // 2):
                        m = NM // 2 * (p - 4) + k
                        if m >= 2:
                            pe.wait_ge(sem("gelu"), done(g * NM + (m - 2)))
                        for i in range(NF):
                            last = pe.matmul(bank(4 + m % 2, 0, n * P), w_f1[:, i, m * P:(m + 1) * P], m_hT[:, i * TG * P:i * TG * P + n * P], start=(i == 0), stop=(i == 1))
                        last.then_inc(sem("fc1_ps"), 1)
                if p in (6, 7):
                    pe.wait_ge(sem("gelu"), done(g * NM + (NM - 1)))
                    last = None
                    for t in range(2 * (p - 6), min(n, 2 * (p - 6) + 2)):
                        for m in range(NM):
                            last = pe.matmul(bank(6 + t // 2, t % 2 * D, (t % 2 + 1) * D), m_gT[:, m * TG * P + t * P:m * TG * P + (t + 1) * P], w_f2[:, m, :], start=(m == 0), stop=(m == NM - 1))
                    if p == 7 and last is not None or n == 1 and p == 6:
                        last.then_inc(sem("fc2_ps"), 1)

            def edges(j, b):
                _, win = nc.values_load_multi_w_load_instructions(wrow[0:1, ds(j * G, G)], engines=(pe.engine,), min_val=0, max_val=NW - 1)
                pe.wait_ge(sem("oh_made"), done(j))
                for h in range(2):
                    pe.wait_ge(sem("prod_made"), reuse(j * 2 + h, 2))
                    for g in range(4):
                        s = 4 * h + g
                        last = pe.matmul(ps[:, 1024 * h + 256 * g:1024 * h + 256 * (g + 1)], oh[b][:, s * P:(s + 1) * P],
                                         nodes[:, ds(win[s] * D, D)], start=True, stop=True)
                    last.then_inc(sem("qg_ps"), 1)

            def pass1(g, b, n):
                for p in range(PIECES):
                    mix(g, b, p, n)
                    if g is not NG or p < PIECES - 1:
                        edges(g * PIECES + (p + 1), (p + 1) % 2)
            edges(0, 0)
            with pe.Fori(0, NG // 2) as it:
                for b in range(2):
                    pass1(it * 2 + b, b, TG)
            pass1(NG, 0, 1)

            pe.wait_ge(sem("kv_used"), NHF + KV)
            pe.wait_ge(sem("alpha_pad"), 1)
            al = alpha[:, :].rearrange("p (s h) -> p h s", h=H)
            for h in range(H):
                for b in range(NB):
                    last = pe.transpose(ps[:, 1024 * h + b * P:1024 * h + (b + 1) * P], al[:, h, b * P:(b + 1) * P], ident[:, :])
                last.then_inc(sem("row_turn"), 1)
            pe.wait_ge(sem("ends_made"), 1)
            for i in range(4):
                for b in range(NB):
                    last = pe.transpose(ps[0:H, 1024 * i + b * P:1024 * i + (b + 1) * P], ends[i][:, b * H:(b + 1) * H], ident[:, :])
            last.then_inc(sem("ends_turn"), 1)
            pe.wait_ge(sem("carry_made"), 1)
            for i in range(2):
                for b in range(NB):
                    last = pe.transpose(bank(i, b * H, (b + 1) * H), carry[i][:, b * P:(b + 1) * P], ident[0:H, 0:H])
            last.then_inc(sem("carry_turn"), 1)
            pe.wait_ge(sem("ex_made"), 1)
            pe.wait_ge(sem("carry_in"), 1)
            for h in range(H):
                for b in range(NB):
                    n = h * NB + b
                    last = pe.transpose(ps[:, 1024 * h + b * P:1024 * h + (b + 1) * P], atR[:, n * P:(n + 1) * P], ident[:, :])
                last.then_inc(sem("col_turn"), 1)

            pe.wait_ge(sem("ex_cols"), 1)
            pe.wait_ge(sem("slots_made"), 1)
            with pe.Fori(0, NHF // KV) as it:
                for b in range(KV):
                    i = it * KV + b
                    _, place = nc.values_load_multi_w_load_instructions(slot_w[0:1, ds(i * HG, HG)], engines=(pe.engine,), min_val=0, max_val=HG - 1)
                    pe.wait_ge(sem("acc_made"), reuse(i, 2))
                    for g in range(HG):
                        pe.matmul(bank(4 * (b % 2) + g, 0, AC), zeros[:, 0:P], zeros, start=True, stop=False, skip_group_check=True)
                    pe.wait_ge(sem("oh2_made"), done(i))
                    pe.wait_ge(sem("ex_in"), done(i))
                    for g in range(HG):
                        last = pe.matmul(ps[:, ds(place[g] * 512 + 2048 * (b % 2), AC)], ohh[b][:, g * P:(g + 1) * P], kv[b][:, g, :],
                                         start=False, stop=False, skip_group_check=True)
                    last.then_inc(sem("agg_ps"), 1)

            pe.wait_ge(sem("exp_in"), 256)
            pe.wait_ge(sem("acc_made"), done(NHF - 1))
            for l in range(2):
                last = pe.transpose(bank(2, l * 80, (l + 1) * 80), e_prow[l][0:80, :], ident[0:80, 0:80])
            last.then_inc(sem("par_turn"), 1)

            def first_part(g, b, n, q):
                if q == 2:
                    pe.wait_ge(sem("f_z_made"), done(g))
                    pe.wait_ge(sem("y_init"), reuse(g, 1))
                    for t in range(n):
                        for i in range(NF):
                            last = pe.transpose(bank(6 + i, t * P, (t + 1) * P), f_z[:, t * D + i * P:t * D + (i + 1) * P], ident[:, :])
                    last.then_inc(sem("f_T_ps"), 1)
                if q == 3:
                    pe.wait_ge(sem("f_T_sb"), done(g))
                    for t in range(n):
                        for i in range(NF):
                            last = pe.matmul(bank(6, t * NE, (t + 1) * NE), f_T[b][:, i * TG * P + t * P:i * TG * P + (t + 1) * P], e_wr[:, i, :], start=(i == 0), stop=(i == 1))
                    last.then_inc(sem("lg_ps"), 1)
                if q == 5:
                    pe.wait_ge(sem("f_w_made"), done(g))
                    for t in range(n):
                        last = pe.transpose(bank(6, t * P, (t + 1) * P)[0:NE, :], f_w[b][:, t * NE:(t + 1) * NE], ident[:, :])
                    last.then_inc(sem("f_wT_ps"), 1)
                if q == 6:
                    pe.wait_ge(sem("f_wT_sb"), done(g))
                    for t in range(n):
                        last = pe.matmul(bank(6 + t // 2, t % 2 * D, (t % 2 + 1) * D), f_wT[:, t * P:(t + 1) * P], e_bo, start=True, stop=True)
                    last.then_inc(sem("bo_ps"), 1)

            def layer(l, u, e, b, n):
                s_ps, s_sb, src_ = (("l1_ps", "h1_sb", f_T[b]), ("l2_ps", "h2_sb", f_h1[e % 2]))[l]
                if l == 1:
                    pe.wait_ge(sem("h1_sb"), done(u * NF + (NF - 1)))
                for m in range(NF):
                    pe.wait_ge(sem(s_sb), reuse(u * NF + m, 2))
                    for i in range(NF):
                        last = pe.matmul(bank(2 * l + m, 0, n * P), e_w[l][:, e, i, m * P:(m + 1) * P], src_[:, i * TG * P:i * TG * P + n * P], start=(i == 0), stop=(i == 1))
                    last.then_inc(sem(s_ps), 1)

            def last_layer(u, e, n):
                pe.wait_ge(sem("h2_sb"), done(u * NF + (NF - 1)))
                pe.wait_ge(sem("y_made"), reuse(u, 1))
                for t in range(n):
                    for i in range(NF):
                        last = pe.matmul(bank(4 + t // 2, t % 2 * D, (t % 2 + 1) * D), f_h2[e % 2][:, i * TG * P + t * P:i * TG * P + (t + 1) * P], e_w[2][:, e, i, :], start=(i == 0), stop=(i == 1))
                last.then_inc(sem("l3_ps"), 1)

            def experts(g, b, n, nxt):
                for e in range(NE):
                    layer(1, g * NE + e, e, b, n)
                    if e < NE - 1:
                        layer(0, g * NE + (e + 1), e + 1, b, n)
                    elif nxt:
                        layer(0, g * NE + (e + 1), 0, 1 - b, nxt)
                    last_layer(g * NE + e, e, n)
                    if nxt:
                        first_part(g + 1, 1 - b, nxt, e)
            for q in range(NE):
                first_part(0, 0, TG, q)
            pe.wait_ge(sem("e_ready"), 1)
            layer(0, 0, 0, 0, TG)
            with pe.Fori(0, NG // 2 - 1) as it:
                for b in range(2):
                    experts(it * 2 + b, b, TG, TG)
            experts(NG - 2, 0, TG, TG)
            experts(NG - 1, 1, TG, 1)
            experts(NG, 0, 1, 0)

        @block.vector
        def _(dve):
            for s in ("oneh", "xp_made", "mkv_sb", "qk_sb", "vs_sb", "oh_made", "prod_made", "oh2_made", "acc_made",
                      "m_var", "m_z", "m_hT_sb", "m_out", "f_var", "f_z_made", "f_sub", "f_w_made", "y_init", "y_made"):
                dve.sem_inc(sem(s), CREDIT)
            link_n = [0]

            def link(ins):
                link_n[0] += 1
                ins.then_inc(sem("link"), 1)
                dve.wait_ge(sem("link"), link_n[0])

            dve.memset(iota8_i[0:1, 0:256], 0)
            dve.memset(iota8_i[0:1, 256:384], NW * P - 1)
            dve.memset(iota8_i[0:1, 384:512], FAR).then_inc(sem("pads_set"), 1)
            dve.memset(nodes[:, (NW - 1) * D:NW * D], 0.0).then_inc(sem("x_pad_set"), 1)
            dve.memset(hs_i, P * 63)
            dve.memset(hy_i, 0).then_inc(sem("hist_pad"), 1)
            dve.memset(last_i, FAR).then_inc(sem("last_pad"), 1)

            dve.wait_ge(sem("order_in"), 32)
            link(dve.tensor_tensor(o_gt, o_this, o_next, ALU.is_gt))
            dve.tensor_reduce(o_sum[0:OR, :], o_gt, AX_X, ALU.add).then_inc(sem("order_seen"), 1)
            dve.wait_ge(sem("order_row"), 16)
            link(dve.tensor_reduce(o_row[:, P - 1:P], o_row[:, 0:OR], AX_X, ALU.max))
            dve.tensor_scalar(o_flag, o_row[:, P - 1:P], 1.0, None, ALU.min).then_inc(sem("order_flag"), 1)

            dve.wait_ge(sem("last_in"), 16 * NB)
            dve.wait_ge(sem("iotas"), 5)
            link(dve.tensor_scalar(last_w[:, 0:NB], last_i[:, 0:NB], 7, None, ALU.logical_shift_right))
            link(dve.tensor_copy(stepkey[:, 0:NB], last_w[:, 0:NB]))
            link(dve.tensor_tensor(stepkey[:, 0:NB], stepkey[:, 0:NB], icol[:, 0:NB], ALU.add))
            link(dve.tensor_scalar(cmp, iota_s, stepkey[:, 0:1], None, ALU.is_gt))
            for b in range(1, NB):
                ins = dve.scalar_tensor_tensor(out=cmp, in0=iota_s, scalar=stepkey[:, b:b + 1], in1=cmp, op0=ALU.is_gt, op1=ALU.add)
                if b < NB - 1:
                    link(ins)
            ins.then_inc(sem("cmp_made"), 1)
            dve.wait_ge(sem("tcol_ps"), 1)
            link(dve.tensor_copy(tcol[:, 0:NB], bank(0, 0, NB)))
            dve.tensor_copy(tcol_u[:, 0:NB], tcol[:, 0:NB]).then_inc(sem("steps"), 1)
            link(dve.tensor_tensor(wcol[:, 0:NB], icol[:, 0:NB], tcol[:, 0:NB], ALU.subtract))
            link(dve.tensor_scalar(wcol[:, 0:NB], wcol[:, 0:NB], float(NW - 1), float(P), ALU.min, ALU.mult))
            w2 = NSP // 2
            for h in range(2):
                dve.tensor_tensor(cmp[0:1, h * w2:(h + 1) * w2], iota_s[0:1, h * w2:(h + 1) * w2], bank(1 + h, 0, w2)[0:1, :], ALU.subtract).then_inc(sem("t_row"), 1)
            dve.wait_ge(sem("t_row"), 2)
            link(dve.tensor_scalar(wrow[:, :], cmp[0:1, :], float(NW - 1), None, ALU.min))
            dve.sem_inc(sem("tcol_sb"), 1)

            dve.wait_ge(sem("hist_in"), 96)
            link(dve.tensor_scalar(hi_i, hs_i, 7, None, ALU.logical_shift_right))
            link(dve.tensor_scalar(lo_i, hs_i, P - 1, None, ALU.bitwise_and))
            link(dve.tensor_copy(lo_f, lo_i))
            link(dve.tensor_copy(key_f, hi_i))
            dve.scalar_tensor_tensor(out=key_f, in0=key_f, scalar=float(NTYPE), in1=hy_i, op0=ALU.mult, op1=ALU.add).then_inc(sem("hist_rows"), 1)

            dve.wait_ge(sem("rows_in"), 32 * NB)
            link(dve.tensor_copy(absR[:, :], dg_i))
            link(dve.tensor_copy(sg_f, sg_i))
            for b in range(NB):
                ins = dve.tensor_scalar(relR[:, b * P:(b + 1) * P], absR[:, b * P:(b + 1) * P], wcol[:, b:b + 1], None, ALU.subtract)
            ins.then_inc(sem("rows_made"), 1)
            dve.wait_ge(sem("lo_ps"), 1)
            dve.tensor_copy(loC, ps[:, 4 * 512:4 * 512 + HT])
            dve.wait_ge(sem("key_ps"), 1)
            dve.tensor_copy(keyC, ps[:, 6 * 512:6 * 512 + HT]).then_inc(sem("hist_cols"), 1)
            dve.wait_ge(sem("rel_ps"), 1)
            link(dve.tensor_copy(relC[:, :], ps[:, 0:NSP]))
            dve.wait_ge(sem("src_ps"), 1)
            dve.tensor_copy(srcC[:, :], ps[:, 1024:1024 + NSP]).then_inc(sem("srcC_made"), 1)
            dve.wait_ge(sem("srcC_made"), 1)
            dve.tensor_copy(relB, relR[:, :]).then_inc(sem("relB_made"), 1)

            dve.wait_ge(sem("iotas"), 6)
            dve.wait_ge(sem("hist_cols"), 1)
            link(dve.tensor_copy(iota8, iota8_i))
            link(dve.memset(rows[:, 11 * NSP:11 * NSP + 512], 0.0))
            link(dve.memset(koh[0], 0.0))
            dve.sem_inc(sem("hist_z"), 1)
            dve.wait_ge(sem("hist_zero"), 1)
            with dve.Fori(0, HT // (2 * G)) as it:
                for b in range(2):
                    c = it * 2 + b
                    dve.wait_ge(sem("hist_ps"), reuse(c, 2))
                    for o, k, n in ((loh[b], loC, P), (koh[b], keyC, NK)):
                        ins = dve.tensor_tensor(o.rearrange("p (n g) -> p n g", g=G), k[:, ds(c * G, G)].unsqueeze(1).broadcast_to([P, n, G]),
                                                iota8[:, 0:n * G].rearrange("p (n g) -> p n g", g=G), ALU.is_equal)
                    ins.then_inc(sem("oneh"), 1)

            dve.wait_ge(sem("x_in"), 80)
            with dve.Fori(0, NW) as t:
                dve.bn_stats(stats[:, ds(t * 6, 6)], nodes[:, ds(t * D, D)]).then_inc(sem("bn"), 1)
            dve.wait_ge(sem("bn"), NW)
            for t in range(NW):
                dve.bn_aggr(mv[:, t * 2:(t + 1) * 2], stats[:, t * 6:(t + 1) * 6]).then_inc(sem("bn"), 1)
            dve.wait_ge(sem("bn"), 2 * NW)
            dve.tensor_scalar(rstd[:, :], mv[:, :].rearrange("p (t c) -> p c t", c=2)[:, 1, :], EPS, None, ALU.add).then_inc(sem("var_eps"), 1)
            dve.wait_ge(sem("std"), 1)
            link(dve.reciprocal(rstd[:, :], rstd[:, :]))
            with dve.Fori(0, NW) as t:
                dve.tensor_scalar(nodes[:, ds(t * D, D)], nodes[:, ds(t * D, D)], mv[:, ds(t * 2, 1)], rstd[:, ds(t, 1)],
                                  ALU.subtract, ALU.mult).then_inc(sem("xn_made"), 1)

            dve.wait_ge(sem("hist_ps"), done(HT // G - 1))
            link(dve.tensor_copy(r4[:, :], bank(4, 0, NK)))
            r4v = r4[:, :].rearrange("p (w k) -> p w k", k=NTYPE)
            link(dve.tensor_reduce(count, r4v, AX_X, ALU.add))
            link(dve.tensor_scalar(count, count, 1.0, None, ALU.max))
            link(dve.reciprocal(count, count))
            dve.tensor_tensor(r4v, r4v, count.unsqueeze(2).broadcast_to([P, NW, NTYPE]), ALU.mult).then_inc(sem("r4_made"), 1)
            dve.memset(gramS, 0.0).then_inc(sem("gram0"), 1)

            dve.wait_ge(sem("w_in"), 176)
            dve.wait_ge(sem("xn_stored"), 1)

            def front(t, k):
                dve.wait_ge(sem("es_ps"), done(t))
                dve.tensor_tensor(xp[k], bank(k, P, P + D), xs[k], ALU.add).then_inc(sem("xp_made"), 1)

            def evacuate(t, k):
                dve.wait_ge(sem("mkv_ps"), done(t))
                dve.wait_ge(sem("gram_ps"), reuse(t, 2))
                dve.tensor_tensor(mkv[k], bank(6), b_mix[:, D:3 * D], ALU.add).then_inc(sem("mkv_sb"), 1)
                dve.wait_ge(sem("qk_ps"), done(t))
                dve.tensor_tensor(nodes[:, ds(t * D, D)], bank(4, 0, D), b_gnn[:, 0:D], ALU.add)
                dve.wait_ge(sem("stored"), reuse(t, 2))
                dve.tensor_tensor(kS[k], bank(4, D, 2 * D), b_gnn[:, D:2 * D], ALU.add).then_inc(sem("qk_sb"), 1)
                dve.wait_ge(sem("vs_ps"), done(t))
                dve.tensor_tensor(vsS[k], bank(5), b_gnn[:, 2 * D:4 * D], ALU.add).then_inc(sem("vs_sb"), 1)
            front(0, 0)
            with dve.Fori(0, NW // 2) as it:
                front(it * 2 + 1, 1)
                evacuate(it * 2, 0)
                front(it * 2 + 2, 0)
                evacuate(it * 2 + 1, 1)
            evacuate(NW - 1, 0)
            dve.wait_ge(sem("gram_ps"), done(NW - 1))
            dve.tensor_copy(gramK[:, :], bank(7, 0, 2 * P)).then_inc(sem("gram_sb"), 1)
            dve.wait_ge(sem("stored"), done(NW - 1))

            dve.wait_ge(sem("gram_sb"), 1)
            for i in range(2):
                for h in range(2):
                    r = slice(C * h, C * (h + 1))
                    ins = dve.tensor_copy(a_sm[r, i * C:(i + 1) * C], gramK[r, i * P + C * h:i * P + C * (h + 1)])
            link(ins)
            a3 = a_sm.rearrange("p (i c) -> p i c", i=2)
            link(dve.tensor_reduce(a_v[0], a3, AX_X, ALU.max))
            dve.tensor_scalar(a_v[1], a_v[0], -1.0 / C ** 0.5, None, ALU.mult).then_inc(sem("a_neg"), 1)
            link(dve.memset(a_bd, 0.0))
            dve.wait_ge(sem("a_exp"), 2)
            link(dve.reciprocal(a_v[3], a_v[2]))
            for i in range(2):
                for h in range(2):
                    r = slice(C * h, C * (h + 1))
                    ins = dve.tensor_scalar(a_bd[r, i * P + C * h:i * P + C * (h + 1)], a_sm[r, i * C:(i + 1) * C], a_v[3][r, i:i + 1], None, ALU.mult)
            ins.then_inc(sem("a_made"), 1)
            dve.wait_ge(sem("a_turn"), 1)
            dve.tensor_copy(a_wT, bank(2))
            dve.tensor_copy(a_bT, bank(3, 0, 2 * P))
            dve.tensor_copy(m_col[:, 0:2 * NF + NM], bank(3, 2 * P, 2 * P + 2 * NF + NM))
            dve.wait_ge(sem("aT_ps"), 1)
            dve.tensor_copy(a_T, bank(0, 0, 2 * P)).then_inc(sem("aT_sb"), 1)
            dve.wait_ge(sem("fold_ps"), 1)
            dve.tensor_copy(w_qf, bank(1).rearrange("p (a d) -> p a d", a=2))
            dve.tensor_copy(b_mix[:, 0:D], bank(0, D, 2 * D)).then_inc(sem("fold_sb"), 1)
            dve.wait_ge(sem("fold_sb"), 1)
            dve.sem_inc(sem("att_used"), 1)

            def chained(name, base):
                state = [0]

                def add(ins):
                    state[0] += 1
                    ins.then_inc(sem(name), 1)
                    dve.wait_ge(sem(name), base + state[0])
                return add, state

            def halves(t, n):
                return [(t[:, c * 2 * D:min(n, 2 * c + 2) * D], c, (min(n, 2 * c + 2) - 2 * c) * D) for c in range(-(-n // 2))]

            def mix_out(g, b, n):
                dve.wait_ge(sem("fc2_ps"), done(g))
                dve.tensor_tensor(m_x1[:, 0:n * D], ps[:, 6 * 512:6 * 512 + n * D], m_s[b][:, 0:n * D], ALU.add).then_inc(sem("m_out"), 1)

            def mix(g, b, p, n, go, before):
                if p == 0 and before:
                    mix_out(g - 1, 1 - b, before)
                three = lambda t: t[:, 0:n * D].rearrange("p (t d) -> p t d", d=D)
                brow = lambda a: b_mix[:, a * D:(a + 1) * D].unsqueeze(1).broadcast_to([P, n, D])
                if p == 1:
                    dve.wait_ge(sem("x1_ps"), done(g))
                    dve.wait_ge(sem("res_stored"), reuse(g, 1))
                    go(dve.tensor_tensor(m_x1[:, 0:n * D], ps[:, 6 * 512:6 * 512 + n * D], m_xn[b][:, 0:n * D], ALU.add))
                    go(dve.tensor_tensor(three(m_x1), three(m_x1), brow(0), ALU.add))
                    for t in range(n):
                        ins = dve.bn_stats(m_st[:, t * 6:(t + 1) * 6], m_x1[:, t * D:(t + 1) * D])
                    go(ins)
                    dve.memset(spare[:, 1:2], 0.0)
                    for t in range(n):
                        ins = dve.bn_aggr(m_mv[:, t * 2:(t + 1) * 2], m_st[:, t * 6:(t + 1) * 6])
                    go(ins)
                    dve.tensor_scalar(m_rs[:, 0:n], m_mv[:, 0:2 * n].rearrange("p (t c) -> p c t", c=2)[:, 1, :], EPS, None, ALU.add).then_inc(sem("m_var"), 1)
                if p == 2:
                    dve.wait_ge(sem("m_std"), done(g))
                    go(dve.reciprocal(m_rs[:, 0:n], m_rs[:, 0:n]))
                    for t in range(n):
                        ins = dve.tensor_scalar(m_xn[b][:, t * D:(t + 1) * D], m_x1[:, t * D:(t + 1) * D], m_mv[:, 2 * t:2 * t + 1], m_rs[:, t:t + 1], ALU.subtract, ALU.mult)
                    ins.then_inc(sem("m_z"), 1)
                    dve.wait_ge(sem(f"mix_rows{b}"), (g - b) * 24 + 48)
                    go(dve.tensor_tensor(m_s[b][:, 0:n * D], m_s[b][:, 0:n * D], m_x[b][:, 0:n * D], ALU.add))
                if p == 3:
                    dve.wait_ge(sem("m_hT_ps"), done(g))
                    for i in range(NF):
                        ins = dve.tensor_scalar(m_hT[:, i * TG * P:i * TG * P + n * P], bank(4 + i, 0, n * P), m_col[:, i:i + 1], m_col[:, NF + i:NF + i + 1], ALU.mult, ALU.add)
                    ins.then_inc(sem("m_hT_sb"), 1)
                if p == 4:
                    go(dve.tensor_tensor(m_s[b][:, 0:n * D], m_s[b][:, 0:n * D], m_x1[:, 0:n * D], ALU.add))
                if p == 5:
                    go(dve.tensor_tensor(three(m_s[b]), three(m_s[b]), brow(1), ALU.add))

            def one_hots(j, b, m):
                dve.wait_ge(sem(f"relq_in{b}"), m * 16 + 16)
                dve.tensor_scalar(oh[b], relq[b], iota_p[:, 0:1], None, ALU.is_equal).then_inc(sem("oh_made"), 1)

            def scores(j, b, m):
                for h in range(2):
                    dve.wait_ge(sem(f"kv_in{2 * b + h}"), m * (16 * HG) + 16 * HG)
                    dve.wait_ge(sem("qg_ps"), done(j * 2 + h))
                    dve.tensor_tensor(kv[2 * b + h][:, :, 0:D], kv[2 * b + h][:, :, 0:D],
                                      ps[:, 1024 * h:1024 * (h + 1)].rearrange("p (g d) -> p g d", g=4), ALU.mult).then_inc(sem("prod_made"), 1)
                for h in range(2):
                    dve.wait_ge(sem("prod_made"), done(j * 2 + h))
                    dve.tensor_reduce(alpha[:, ds((j * 2 + h) * (4 * H), 4 * H)].rearrange("p (g h) -> p g h", g=HG),
                                      kv[2 * b + h][:, :, 0:D].rearrange("p g (h c) -> p g h c", c=C), AX_X, ALU.add).then_inc(sem("kv_used"), 1)

            def pass1(g, b, n, before=TG):
                go, state = chained("mchain", g * 8)
                for p in range(PIECES):
                    if g is not NG or p < PIECES - 1:
                        one_hots(g * PIECES + (p + 1), (p + 1) % 2, g * (PIECES // 2) + (p + 1) // 2)
                    scores(g * PIECES + p, p % 2, g * (PIECES // 2) + p // 2)
                    mix(g, b, p, n, go, before)
                assert state[0] == 8
            one_hots(0, 0, 0)
            pass1(0, 0, TG, 0)
            with dve.Fori(0, NG // 2 - 1) as it:
                for b in range(2):
                    pass1(it * 2 + (b + 1), 1 - b, TG)
            dve.memset(m_x[0][:, 0:D], 0.0).then_inc(sem("m_x_zero"), 1)
            pass1(NG - 1, 1, TG)
            pass1(NG, 0, 1)
            mix_out(NG, 0, 1)
            dve.memset(alpha[:, NGR * G * H:NSP * H], 0.0).then_inc(sem("alpha_pad"), 1)

            dve.wait_ge(sem("res_out"), 16 * (NG + 1))
            link(dve.tensor_scalar(slot_n(10), relR[:, :], 0.0, None, ALU.is_lt))
            link(dve.scalar_tensor_tensor(out=slot_n(10), in0=relR[:, :], scalar=float(P - 1), in1=slot_n(10), op0=ALU.is_gt, op1=ALU.add))
            link(dve.tensor_scalar(slot_n(10), slot_n(10), BIG_NEG, None, ALU.mult))
            inv = slot_n(10)
            fresh = slot_n(11)
            ab = absR[:, :].rearrange("p (b e) -> p b e", b=NB)
            fr = fresh.rearrange("p (b e) -> p b e", b=NB)
            link(dve.tensor_tensor(fr[:, :, 1:P], ab[:, :, 1:P], ab[:, :, 0:P - 1], ALU.not_equal))
            link(dve.memset(fr[:, :, 0:1], 1.0))
            link(dve.tensor_scalar(penR.rearrange("p (h x) -> p h x", h=H), fresh.unsqueeze(1).broadcast_to([P, H, NSP]), BIG_NEG, None, ALU.mult))
            link(dve.memset(rows[:, 4 * RW:4 * RW + 1], BIG_NEG))
            for h in range(H):
                dve.wait_ge(sem("row_turn"), h + 1)
                link(dve.scalar_tensor_tensor(out=atR[:, h * NSP:(h + 1) * NSP], in0=ps[:, 1024 * h:1024 * h + NSP], scalar=1.0 / C ** 0.5,
                                              in1=inv, op0=ALU.mult, op1=ALU.add))

            def scans():
                dve.tensor_tensor_scan(fwR, penR, atR, BIG_NEG, ALU.add, ALU.max).then_inc(sem("scan"), 1)
                link(dve.tensor_tensor_scan(bwR[:, ::-1], penN[:, ::-1], atR[:, ::-1], BIG_NEG, ALU.add, ALU.max))
            scans()
            av = atR.rearrange("p (h b e) -> p b h e", h=H, b=NB)
            fv = fwR.rearrange("p (h b e) -> p b h e", h=H, b=NB)
            bv_ = bwR.rearrange("p (h b e) -> p b h e", h=H, b=NB)
            ev = [e.rearrange("p (b h) -> p b h", b=NB) for e in ends]
            sv = [e.rearrange("p (b h) -> p b h", b=NB) for e in saved]
            dve.tensor_copy(ev[0], fv[:, :, :, P - 1])
            dve.tensor_copy(ev[1], bv_[:, :, :, 0])
            dve.tensor_copy(sv[0], av[:, :, :, 0])
            dve.tensor_copy(sv[1], av[:, :, :, P - 1])
            dve.tensor_copy(ev[2], ab[:, :, 0:1].broadcast_to([P, NB, H]))
            dve.tensor_copy(ev[3], ab[:, :, P - 1:P].broadcast_to([P, NB, H])).then_inc(sem("ends_made"), 1)
            dve.wait_ge(sem("ends_turn"), 1)
            lm, fm, d0, de, cont, chain, fsc, bsc = [line(i) for i in range(8)]
            for i in range(4):
                link(dve.tensor_copy(line(i), ps[0:H, 1024 * i:1024 * i + NSP]))
            Z = NSP - 1
            link(dve.memset(cont, 0.0))
            link(dve.tensor_tensor(cont[:, 1:NSP], d0[:, 1:NSP], de[:, 0:Z], ALU.is_equal))
            link(dve.tensor_tensor(d0, d0, de, ALU.is_equal))
            link(dve.tensor_tensor(chain, d0, cont, ALU.mult))
            link(dve.tensor_scalar(chain, chain, -BIG_NEG, BIG_NEG, ALU.mult, ALU.add))
            link(dve.tensor_tensor_scan(fsc, chain, lm, BIG_NEG, ALU.add, ALU.max))
            link(dve.memset(chain, 0.0))
            link(dve.tensor_tensor(chain[:, 0:Z], d0[:, 0:Z], cont[:, 1:NSP], ALU.mult))
            link(dve.tensor_scalar(chain, chain, -BIG_NEG, BIG_NEG, ALU.mult, ALU.add))
            link(dve.tensor_tensor_scan(bsc[:, ::-1], chain[:, ::-1], fm[:, ::-1], BIG_NEG, ALU.add, ALU.max))
            link(dve.tensor_scalar(cont, cont, -BIG_NEG, BIG_NEG, ALU.mult, ALU.add))
            dve.memset(carry[0], BIG_NEG)
            link(dve.memset(carry[1], BIG_NEG))
            dve.tensor_tensor(carry[0][:, 1:NSP], fsc[:, 0:Z], cont[:, 1:NSP], ALU.add)
            dve.tensor_tensor(carry[1][:, 0:Z], bsc[:, 1:NSP], cont[:, 1:NSP], ALU.add).then_inc(sem("carry_made"), 1)
            dve.wait_ge(sem("carry_turn"), 1)
            for i, e in ((0, 0), (1, P - 1)):
                link(dve.tensor_tensor(av[:, :, :, e], sv[i], bank(i, 0, NB * H).rearrange("p (b h) -> p b h", b=NB), ALU.max))
            dve.sem_inc(sem("carry_in"), 1)
            scans()
            link(dve.tensor_tensor(fwR, fwR, bwR, ALU.max))
            for i, e in ((0, 0), (1, P - 1)):
                link(dve.tensor_copy(av[:, :, :, e], sv[i]))
            dve.tensor_tensor(atR, atR, fwR, ALU.subtract).then_inc(sem("shifted"), 1)
            dve.memset(nodes[:, :], 0.0).then_inc(sem("acc_zero"), 1)
            dve.memset(zeros, 0.0)
            link(dve.tensor_copy(base_f, wrow[0:1, :].rearrange("p (i g) -> p i g", g=HG)[:, :, 0]))
            link(dve.tensor_scalar(base_f, base_f, float(NW - HG), None, ALU.min))
            link(dve.tensor_copy(base_w, base_f))
            dve.tensor_tensor(slot_w.rearrange("p (i g) -> p i g", g=HG), wrow[0:1, :].rearrange("p (i g) -> p i g", g=HG),
                              base_f.unsqueeze(2).broadcast_to([1, NSP // HG, HG]), ALU.subtract).then_inc(sem("slots_made"), 1)
            dve.wait_ge(sem("slots_made"), 1)
            for h in range(H):
                dve.wait_ge(sem("col_turn"), h + 1)
                ins = dve.tensor_copy(alpha[:, :].rearrange("p (s h) -> p h s", h=H)[:, h, :], ps[:, 1024 * h:1024 * h + NSP])
            ins.then_inc(sem("ex_cols"), 1)
            dve.wait_ge(sem("ex_cols"), 1)
            dve.wait_ge(sem("acc_zero"), 1)

            def weigh(i, b, m):
                dve.tensor_tensor(ohh[b].rearrange("p (g n) -> p g n", g=HG), relC[:, ds(i * HG, HG)].unsqueeze(2).broadcast_to([P, HG, P]),
                                  iota_f[:, :].unsqueeze(1).broadcast_to([P, HG, P]), ALU.is_equal)
                dve.wait_ge(sem(f"kv_in{b}"), m * (16 * HG) + (NHF // KV * 16 * HG + 16 * HG))
                v4 = kv[b][:, :, 0:D].rearrange("p g (h c) -> p g h c", h=H)
                dve.tensor_tensor(v4, v4, alpha[:, ds(i * (HG * H), HG * H)].rearrange("p (g h) -> p g h", g=HG).unsqueeze(3).broadcast_to([P, HG, H, C]),
                                  ALU.mult).then_inc(sem("oh2_made"), 1)

            def add_up(i, b):
                _, base = nc.values_load_multi_w_load_instructions(base_w[0:1, ds(i, 1)], engines=(dve.engine,), min_val=0, max_val=NW - HG)
                dve.wait_ge(sem("agg_ps"), done(i))
                dve.sem_inc(sem("kv_used"), 1)
                dve.wait_ge(sem("acc_made"), done(i - 1))
                acc = nodes[:, ds(base[0] * AC, HG * AC)].rearrange("p (s a) -> p s a", s=HG)
                dve.tensor_tensor(acc, acc, ps[:, 2048 * (b % 2):2048 * (b % 2 + 1)].rearrange("p (s a) -> p s a", s=HG)[:, :, 0:AC], ALU.add).then_inc(sem("acc_made"), 1)
            weigh(0, 0, 0)
            with dve.Fori(0, NHF // KV - 1) as it:
                for b in range(KV):
                    weigh(it * KV + (b + 1), (b + 1) % KV, it + (b + 1) // KV)
                    add_up(it * KV + b, b)
            for b in range(KV):
                i = NHF - KV + b
                if b < KV - 1:
                    weigh(i + 1, b + 1, NHF // KV - 1)
                add_up(i, b)
            dve.wait_ge(sem("acc_made"), done(NHF - 1))

            dve.wait_ge(sem("par_turn"), 1)
            for l in range(2):
                link(dve.tensor_copy(e_par[l], bank(2, l * 80, (l + 1) * 80)))
                ins = dve.tensor_scalar(e_sc[l], e_par[l][:, 64:80], 0.001, None, ALU.add)
            ins.then_inc(sem("e_var"), 1)
            dve.wait_ge(sem("e_std"), 1)
            for l in range(2):
                pg, pb, pbe, pm = [e_par[l][:, 16 * i:16 * (i + 1)] for i in range(4)]
                link(dve.reciprocal(e_sc[l], e_sc[l]))
                link(dve.tensor_tensor(e_sc[l], e_sc[l], pg, ALU.mult))
                link(dve.tensor_tensor(e_sh[l], pb, pm, ALU.subtract))
                link(dve.tensor_tensor(e_sh[l], e_sh[l], e_sc[l], ALU.mult))
                link(dve.tensor_tensor(e_sh[l], e_sh[l], pbe, ALU.add))
            dve.sem_inc(sem("e_ready"), 1)

            def first_part(g, b, m, n, q, go):
                y = f_y[b]
                av = nodes[:, ds(g * (TG * AC), n * AC)].rearrange("p (t a) -> p t a", a=AC)
                l3 = f_lg[:, 0:n * NE].rearrange("p (t e) -> p t e", e=NE)
                if q == 0:
                    go(dve.tensor_scalar(f_rc[:, 0:n * H].rearrange("p (t h) -> p t h", h=H), av[:, :, D:AC], 1e-16, None, ALU.add))
                    go(dve.reciprocal(f_rc[:, 0:n * H], f_rc[:, 0:n * H]))
                    dve.wait_ge(sem("y_stored"), reuse(g, 2))
                    go(dve.tensor_tensor(y[:, 0:n * D].rearrange("p (t h c) -> p t h c", t=n, h=H), av[:, :, 0:D].rearrange("p t (h c) -> p t h c", h=H),
                                         f_rc[:, 0:n * H].rearrange("p (t h) -> p t h", h=H).unsqueeze(3).broadcast_to([P, n, H, C]), ALU.mult))
                    dve.wait_ge(sem(f"res_in{b}"), m * 16 + 16)
                    go(dve.tensor_tensor(y[:, 0:n * D], y[:, 0:n * D], f_res[b][:, 0:n * D], ALU.add))
                    for t in range(n):
                        ins = dve.bn_stats(f_st[:, t * 6:(t + 1) * 6], y[:, t * D:(t + 1) * D])
                    go(ins)
                    dve.memset(spare[:, 1:2], 0.0)
                    for t in range(n):
                        ins = dve.bn_aggr(f_mv[:, t * 2:(t + 1) * 2], f_st[:, t * 6:(t + 1) * 6])
                    go(ins)
                    dve.tensor_scalar(f_rs[:, 0:n], f_mv[:, 0:2 * n].rearrange("p (t c) -> p c t", c=2)[:, 1, :], EPS, None, ALU.add).then_inc(sem("f_var"), 1)
                if q == 1:
                    dve.wait_ge(sem("f_std"), done(g))
                    go(dve.reciprocal(f_rs[:, 0:n], f_rs[:, 0:n]))
                    for t in range(n):
                        ins = dve.tensor_scalar(f_z[:, t * D:(t + 1) * D], y[:, t * D:(t + 1) * D], f_mv[:, 2 * t:2 * t + 1], f_rs[:, t:t + 1], ALU.subtract, ALU.mult)
                    ins.then_inc(sem("f_z_made"), 1)
                if q == 3:
                    dve.wait_ge(sem("lg_ps"), done(g))
                    go(dve.tensor_tensor(l3, bank(6, 0, n * NE).rearrange("p (t e) -> p t e", e=NE), e_br.unsqueeze(1).broadcast_to([P, n, NE]), ALU.add))
                    go(dve.tensor_reduce(f_m[:, 0:n], l3, AX_X, ALU.max))
                    dve.tensor_tensor(l3, l3, f_m[:, 0:n].unsqueeze(2).broadcast_to([P, n, NE]), ALU.subtract).then_inc(sem("f_sub"), 1)
                if q == 4:
                    dve.wait_ge(sem("f_exp"), done(g))
                    go(dve.tensor_reduce(f_m[:, 0:n], l3, AX_X, ALU.add))
                    go(dve.reciprocal(f_m[:, 0:n], f_m[:, 0:n]))
                    dve.tensor_tensor(f_w[b][:, 0:n * NE].rearrange("p (t e) -> p t e", e=NE), l3, f_m[:, 0:n].unsqueeze(2).broadcast_to([P, n, NE]), ALU.mult).then_inc(sem("f_w_made"), 1)
                if q == 6:
                    dve.wait_ge(sem("bo_ps"), done(g))
                    dve.tensor_tensor(y[:, 0:n * D], ps[:, 6 * 512:6 * 512 + n * D], y[:, 0:n * D], ALU.add).then_inc(sem("y_init"), 1)

            def experts(g, b, m, n, nxt):
                go, state = chained("fchain", (g + 1) * 11)
                dve.wait_ge(sem("y_init"), done(g))
                for e in range(NE):
                    dve.wait_ge(sem("l3_ps"), done(g * NE + e))
                    dve.wait_ge(sem("y_made"), done(g * NE + (e - 1)))
                    for t in range(n):
                        yt = f_y[b][:, t * D:(t + 1) * D]
                        ins = dve.scalar_tensor_tensor(out=yt, in0=bank(4 + t // 2, t % 2 * D, (t % 2 + 1) * D), scalar=f_w[b][:, t * NE + e:t * NE + e + 1],
                                                       in1=yt, op0=ALU.mult, op1=ALU.add)
                    ins.then_inc(sem("y_made"), 1)
                    if nxt:
                        first_part(g + 1, 1 - b, m + b, nxt, e, go)
                assert state[0] in (0, 11)
            go, _ = chained("fchain", 0)
            for q in range(NE):
                first_part(0, 0, 0, TG, q, go)
            with dve.Fori(0, NG // 2 - 1) as it:
                for b in range(2):
                    experts(it * 2 + b, b, it, TG, TG)
            experts(NG - 2, 0, NG // 2 - 1, TG, TG)
            experts(NG - 1, 1, NG // 2 - 1, TG, 1)
            experts(NG, 0, NG // 2, 1, 0)


_INS = ['x', 'src', 'dst', 'edge_type_4', 'L0_gnn_edge_emb', 'L0_gnn_Wq', 'L0_gnn_bq', 'L0_gnn_Wk', 'L0_gnn_bk', 'L0_gnn_Wv',
        'L0_gnn_bv', 'L0_gnn_Ws', 'L0_gnn_bs', 'L0_mix_w_qkv', 'L0_mix_b_qkv', 'L0_mix_norm_g', 'L0_mix_norm_b', 'L0_mix_w_fc1',
        'L0_mix_b_fc1', 'L0_mix_w_fc2', 'L0_mix_b_fc2', 'L0_ffn_Wr', 'L0_ffn_br', 'L0_ffn_W1', 'L0_ffn_b1', 'L0_ffn_g1',
        'L0_ffn_be1', 'L0_ffn_m1', 'L0_ffn_v1', 'L0_ffn_W2', 'L0_ffn_b2', 'L0_ffn_g2', 'L0_ffn_be2', 'L0_ffn_m2', 'L0_ffn_v2',
        'L0_ffn_Wo', 'L0_ffn_bo']
_OUTS = [((6250, 256), 'float32')]


def kernel(**inputs):
    import numpy as _np
    import concourse.bacc as _bacc
    from concourse import mybir as _mybir
    from concourse.bass_utils import run_bass_kernel_spmd as _run

    nc = _bacc.Bacc("TRN2", target_bir_lowering=False, num_devices=1)
    arrays, args = {}, []
    for name in _INS:
        a = _np.ascontiguousarray(inputs[name])
        arrays[f"in_{name}_dram"] = a
        args.append(nc.dram_tensor(f"in_{name}_dram", a.shape, _mybir.dt.from_np(a.dtype), kind="ExternalInput").ap())
    for i, (shape, dtype) in enumerate(_OUTS):
        dt = _mybir.dt.from_np(_np.dtype(dtype))
        args.append(nc.dram_tensor(f"out_{i}_dram", shape, dt, kind="ExternalOutput").ap())
    gps_layer_kernel(nc, *args)
    r = _run(nc, [arrays], core_ids=[0])
    got = tuple(r.results[0][f"out_{i}_dram"] for i in range(len(_OUTS)))
    return got[0]
```

```python
from contextlib import ExitStack

import concourse.bass as bass
from concourse import mybir

ALU = mybir.AluOpType
ACT = mybir.ActivationFunctionType
AX_X = mybir.AxisListType.X
F32 = mybir.dt.float32
BF16 = mybir.dt.bfloat16
F32R = mybir.dt.float32r
I32 = mybir.dt.int32
U32 = mybir.dt.uint32

P = 128
BIG_NEG = -1.0e30
FAR = 1 << 20


def ds(start, size):
    return bass.ds(start, size)


def gps_layer_kernel(nc, x, src, dst, etype, edge_emb, Wq, bq, Wk, bk, Wv, bv, Ws, bs,
                     w_qkv, b_qkv, norm_g, norm_b, w_fc1, b_fc1, w_fc2, b_fc2,
                     Wr, br, W1, b1, g1, be1, m1, v1, W2, b2, g2, be2, m2, v2, Wo, bo, out):
    N, D = x.shape
    E = src.shape[0]
    NTYPE = edge_emb.shape[0]
    H, C = 4, 64
    NW = -(-N // P)
    TAIL = N - (NW - 1) * P
    ET = -(-E // P)
    G = 8
    NS = -(-(ET + NW) // G) * G
    NB = -(-NS // P)
    NSP = NB * P
    NGR = NS // G
    AC = D + H
    HT = -(-ET // (2 * G)) * 2 * G
    NK = NW * NTYPE
    EPS = 1e-5
    MH = w_fc1.shape[1]
    NE = W1.shape[0]
    FE = E // P
    FB = FE // P
    FR = FE - FB * P
    EREST = E - FE * P
    TG = 4
    T2 = 2
    NG2 = (NW - 1) // T2
    WT = T2 * D
    NG = (NW - 1) // TG
    NM = MH // P
    NF = D // P
    PIECES = NGR // (NG + 1)
    assert NGR % 4 == 0 and NW % 7 == 0 and NW == NG * TG + 1 and NG % 2 == 0 and PIECES * (NG + 1) == NGR and PIECES == 8 and NE == 8 and NG2 % 2 == 0
    HG = G // 2
    NHF = 2 * NGR
    KV = 4
    HI = HT // (2 * G)
    HI1, HI2 = 9, (NW - 1) // 2
    CREDIT = 2

    def done(g):
        return g + (1 + CREDIT)

    def reuse(g, ring):
        return g + (1 + CREDIT - ring)

    srcS = nc.dram_tensor("edges_src", [(ET + 1) * P], I32, kind="Internal").ap()
    dstS = nc.dram_tensor("edges_dst", [(ET + 1) * P], I32, kind="Internal").ap()
    srcT = nc.dram_tensor("sorted_src", [ET * P], I32, kind="Internal").ap()
    dstT = nc.dram_tensor("sorted_dst", [ET * P], I32, kind="Internal").ap()
    nextD = nc.dram_tensor("next_place", [NW * P], F32, kind="Internal").ap()
    downD = nc.dram_tensor("descents", [P], F32, kind="Internal").ap()
    relD = nc.dram_tensor("rel_rows", [NSP, P], BF16, kind="Internal").ap()
    xnD = nc.dram_tensor("xn_rows", [NW * P, D], F32, kind="Internal").ap()
    kD = nc.dram_tensor("k_rows", [NW * P, D], F32, kind="Internal").ap()
    vD = nc.dram_tensor("v_rows", [NW * P, D], F32, kind="Internal").ap()
    resD = nc.dram_tensor("res_rows", [NW * P, D], F32, kind="Internal").ap()

    with ExitStack() as ctx:
        def sb(name, shape, dt):
            return ctx.enter_context(nc.sbuf_tensor(name, shape, dt))

        sems = {}

        def sem(name):
            if name not in sems:
                sems[name] = ctx.enter_context(nc.semaphore(name))
            return sems[name]

        nodes = sb("nodes", [P, NW * AC], F32)
        wrow = sb("wrow", [1, NSP], U32)
        emb = sb("emb", [NTYPE, D], F32)
        ident = sb("ident", [P, P], F32)
        iota_f = sb("iota_f", [P, P], F32)
        iota_p = sb("iota_p", [P, 1], F32)
        ones = sb("ones", [P, 1], F32)
        r4 = sb("r4", [P, NK], F32)
        stats = sb("stats", [P, NW * 6], F32)
        mv = sb("mv", [P, NW * 2], F32)
        rstd = sb("rstd", [P, NW], F32)
        tiny = sb("tiny", [P, 160], F32)

        gramK = sb("gramK", [P, 2 * P], F32)
        ends_all = sb("ends_all", [P, 6 * NB * H], F32)

        spare = sb("spare", [P, 2], F32)
        m_col = sb("m_col", [P, 16], F32)
        m_st = sb("m_st", [P, TG * 6], F32)
        m_mv = sb("m_mv", [P, TG * 2], F32)
        m_rs = sb("m_rs", [P, TG], F32)

        early = ExitStack()
        RN, WN = 16 * NSP + 8, 9280
        rows = early.enter_context(nc.sbuf_tensor("rows", [P, RN], F32))
        sizes = (NSP * H, NSP, NSP, NSP, NSP, 8 * D, 6 * D, MH // P * D, 4 * D, 3 * D)
        edge_w = early.enter_context(nc.sbuf_tensor("edge_w", [P, sum(sizes)], F32))

        def part(i):
            return edge_w[:, sum(sizes[:i]):sum(sizes[:i + 1])]
        alpha = part(0)
        srcC = part(1).bitcast(U32)
        relC, relR, absR = part(2), part(3), part(4)
        w_gnn = part(5).rearrange("p (k n) -> p k n", k=2)
        w_mix = part(6).rearrange("p (k n) -> p k n", k=2)
        w_f2 = part(7).rearrange("p (k n) -> p k n", n=D)
        w_qf = w_mix[:, :, 0:D]
        b_gnn = part(8)
        b_mix = part(9)
        work = early.enter_context(nc.sbuf_tensor("work", [P, WN], F32))
        early.close()
        WE = NE * NF * D
        e_lower = sb("e_lower", [P, 3 * WE], F32R)
        e_rest = sb("e_rest", [P, RN - 3 * WE], F32)
        e_upper = sb("e_upper", [P, 3 * WE], F32R)
        e_tail = sb("e_tail", [P, sum(sizes) - 3 * WE], F32)
        f_split = sb("f_split", [P, 12 * WT], F32R)
        f_more = sb("f_more", [P, WN - 12 * WT], F32)

        ps = ctx.enter_context(nc.psum_tensor("ps", [P, 8 * 512], F32))

        def bank(i, a=0, b=512):
            return ps[:, 512 * i + a:512 * i + b]

        def slot(i, n=1):
            return rows[:, i * NSP:(i + n) * NSP]

        iota_s = slot(0)
        cmp = slot(1)
        hs_i = slot(2).bitcast(I32)
        hy_i = slot(3).bitcast(I32)
        lo_i = slot(4).bitcast(I32)
        hi_i = slot(5).bitcast(I32)
        key_f = slot(6)
        lo_f = slot(7)
        sg_i = slot(8).bitcast(I32)
        dg_i = slot(9).bitcast(I32)
        sg_f = slot(10)
        iota8_i = rows[:, 11 * NSP:11 * NSP + NK * G].bitcast(I32)
        loh = [rows[:, 11 * NSP + 512 * b:11 * NSP + 512 * (b + 1)].bitcast(BF16) for b in range(2)]
        iota8 = rows[:, 13 * NSP:13 * NSP + NK * G // 2].bitcast(BF16)
        koh = [rows[:, 14 * NSP + NK * G // 2 * b:14 * NSP + NK * G // 2 * (b + 1)].bitcast(BF16) for b in range(2)]
        loC = work[:, 5000:5000 + HT // 2].bitcast(BF16)
        keyC = work[:, 5500:5500 + HT // 2].bitcast(BF16)
        relB = slot(10)[:, 0:NSP // 2].bitcast(BF16)
        assert NK * G <= 2 * NSP and NK * G // 2 <= NSP
        OC = next(c for c in range(1000, 1, -1) if (E - 1) % c == 0)
        OR = (E - 1) // OC
        assert OR < P and 3 * OC + P <= WN
        o_this = work[0:OR, 0:OC].bitcast(I32)
        o_next = work[0:OR, OC:2 * OC].bitcast(I32)
        o_gt = work[0:OR, 2 * OC:3 * OC]
        o_row = work[0:1, 3 * OC:3 * OC + P]
        o_sum = tiny[:, 57:58]
        o_flag = tiny[0:1, 58:59].bitcast(U32)
        t_row = work[:, 0:P].bitcast(I32)
        t_rowf = work[:, P:2 * P]
        t_col = work[:, 2 * P:2 * P + 2].bitcast(I32)
        t_colf = work[:, 2 * P + 2:2 * P + 3]
        t_next = work[:, 2 * P + 3:2 * P + 4]
        t_place = work[:, 2 * P + 4:2 * P + 5]
        t_place_u = work[:, 2 * P + 5:2 * P + 6].bitcast(U32)
        t_dst_u = work[:, 2 * P + 6:2 * P + 7].bitcast(U32)
        t_cnt = work[:, 3 * P:5 * P].rearrange("p (q e) -> p q e", q=2)
        t_low = work[:, 5 * P:6 * P]
        t_table = work[0:NW, 6 * P:7 * P]
        t_base = [work[0:NW, 7 * P + P * i:8 * P + P * i] for i in range(2)]
        last_i = tiny[:, 0:8].bitcast(I32)
        last_w = tiny[:, 8:16].bitcast(I32)
        stepkey = tiny[:, 16:24]
        tcol = tiny[:, 24:32]
        icol = tiny[:, 32:40]
        wcol = tiny[:, 40:48]
        tcol_u = tiny[:, 48:56].bitcast(U32)
        count = tiny[:, 64:64 + NW]

        MA = 2 * D // P

        def w_f1(i, m):
            return w_gnn[:, i, m * P:(m + 1) * P] if m < MA else w_mix[:, i, D + (m - MA) * P:D + (m - MA + 1) * P]

        xs = [work[:, 260 * k:260 * k + D + 1] for k in range(2)]
        xT = [work[:, 520 + 256 * k:520 + 256 * (k + 1)] for k in range(2)]
        kS = [work[:, 1544 + 256 * k:1544 + 256 * (k + 1)] for k in range(2)]
        r4T = work[0:NTYPE, WN - NW * P:WN]
        zero_g = work[:, 2320:2320 + D + 1]
        g_G = work[:, 2600:2600 + 2 * (D + 1)].rearrange("p (i e) -> p i e", i=2)
        g_U = work[:, 3200:3200 + 2 * D].rearrange("p (i e) -> p i e", i=2)
        g_s = work[0:1, 3800:3800 + D]
        g_t = work[0:1, 4100:4100 + D]

        kv = [work[:, HG * AC * b:HG * AC * (b + 1)].rearrange("p (g a) -> p g a", a=AC) for b in range(KV)]
        oh = [work[:, 2 * G * AC + G * P * b:2 * G * AC + G * P * (b + 1)] for b in range(2)]
        relq = [work[:, 2 * G * AC + 2 * G * P + G * P // 2 * b:2 * G * AC + 2 * G * P + G * P // 2 * (b + 1)].bitcast(BF16) for b in range(2)]
        ohh = [work[:, 2 * G * AC + HG * P * b:2 * G * AC + HG * P * (b + 1)] for b in range(4)]
        idx = [tiny[:, 128 + G * b:128 + G * (b + 1)].bitcast(U32) for b in range(4)]
        assert 2 * G * AC + 3 * G * P <= WN

        RW = H * NSP
        atR = rows[:, 0:RW]
        fwR = rows[:, RW:2 * RW]
        bwR = rows[:, 2 * RW:3 * RW]
        penR = rows[:, 3 * RW:4 * RW]
        penN = rows[:, 3 * RW + 1:4 * RW + 1]
        ends = [ends_all[:, i * NB * H:(i + 1) * NB * H] for i in range(4)]
        saved = [ends_all[:, (4 + i) * NB * H:(5 + i) * NB * H] for i in range(2)]

        base_w = absR[0:1, 0:NSP // HG].bitcast(U32)
        base_f = absR[0:1, NSP // 2:NSP // 2 + NSP // HG]
        slot_w = relR[0:1, :].bitcast(U32)
        zeros = absR[:, NSP - AC // 2:NSP].bitcast(BF16)
        assert NSP // 2 + NSP // HG <= NSP - AC // 2

        def line(i):
            return nodes[0:H, i * NSP:(i + 1) * NSP]
        carry = [line(8), line(9)]

        def slot_n(i):
            return nodes[:, i * NSP:(i + 1) * NSP]

        def cut(t, at, n):
            return t[:, at:at + n]
        W4 = TG * D
        m_xn = [cut(rows, W4 * b, W4) for b in range(2)]
        m_x = [cut(rows, W4 * (2 + b), W4) for b in range(2)]
        m_x1 = cut(rows, W4 * 4, W4)
        m_T = cut(rows, W4 * 5, W4)
        m_pT = cut(rows, W4 * 6, W4)
        m_hT = cut(rows, W4 * 7, W4)
        m_v = cut(rows, W4 * 8, W4)
        m_gT = cut(rows, W4 * 9, NM * TG * P)
        m_at = W4 * 9 + NM * TG * P
        m_rT = rows[0:NTYPE, m_at:m_at + TG * P]
        m_r4 = cut(rows, m_at + TG * P, TG * NTYPE)
        assert m_at + TG * P + TG * NTYPE <= 16 * NSP
        a_sm = cut(work, 0, 2 * C)
        a_bd = cut(work, 128, 2 * P)
        a_T = cut(work, 384, 2 * P)
        a_wT = cut(work, 640, 4 * P)
        a_bT = cut(work, 1152, 2 * P)
        a_row = cut(work, 1408, P)
        a_v = [cut(work, 1536 + 2 * i, 2) for i in range(4)]

        e_w = [rows[:, WE * i:WE * (i + 1)] for i in range(3)]
        e_parts = [[t[:, WE * i:WE * (i + 1)].rearrange("p (e k n) -> p e k n", e=NE, k=NF) for t in (e_upper, e_lower)] for i in range(3)]
        e_bo = e_rest[0:NE, 0:D]
        e_wr = e_rest[:, D:D + NF * NE].rearrange("p (k n) -> p k n", k=NF)
        e_br = cut(e_rest, D + 16, NE)
        e_prow = [cut(e_rest, D + 32 + P * i, P) for i in range(2)]
        e_par = [cut(e_rest, D + 32 + 2 * P + 80 * i, 80) for i in range(2)]
        e_sc = [cut(e_rest, D + 448 + 16 * i, 16) for i in range(2)]
        e_sh = [cut(e_rest, D + 480 + 16 * i, 16) for i in range(2)]
        f_wT = e_rest[0:NE, D + 512:D + 512 + T2 * P]
        assert D + 512 + T2 * P <= RN - 3 * WE

        def split_pair(a):
            return [cut(f_split, WT * (a + i), WT) for i in range(2)]
        f_T = [split_pair(2 * b) for b in range(2)]
        f_h = [[split_pair(4 + 4 * l + 2 * b) for b in range(2)] for l in range(2)]
        f_whole = [cut(f_more, WT * l, WT) for l in range(2)]
        f_y = [cut(f_more, WT * (2 + b), WT) for b in range(2)]
        f_z = cut(f_more, WT * 4, WT)
        assert 17 * WT <= WN and 3 * WE + 3 * WT <= sum(sizes)
        f_res = [cut(e_tail, WT * b, WT) for b in range(2)]
        f_zT = cut(e_tail, 2 * WT, WT)

        def spread(t, n):
            return t if n == T2 else t.rearrange("p (m a) -> p m a", m=NF)[:, :, 0:n * P]
        f_lg = cut(ends_all, 0, T2 * NE)
        f_w = [cut(ends_all, 32 + 32 * b, T2 * NE) for b in range(2)]
        f_rc = cut(ends_all, 96, T2 * H)
        f_m = cut(ends_all, 112, T2)
        f_st, f_mv, f_rs = m_st, m_mv, m_rs

        block = ctx.enter_context(nc.Block())

        @block.sync
        def _(sp):
            sp.wait_ge(sem("pads"), 3)
            for t, o in ((src, hs_i), (etype, hy_i)):
                sp.dma_start(o[:, 0:FB * P].rearrange("p (b e) -> p b e", b=FB),
                             t[0:FB * P * P].rearrange("(b p e) -> p b e", b=FB, p=P)).then_inc(sem("hist_in"), 16)
                sp.dma_start(o[0:FR, FB * P:(FB + 1) * P],
                             t[FB * P * P:FE * P].rearrange("(p e) -> p e", p=FR)).then_inc(sem("hist_in"), 16)
                sp.dma_start(o[FR:FR + 1, FB * P:FB * P + EREST],
                             t[FE * P:E].rearrange("(p e) -> p e", p=1)).then_inc(sem("hist_in"), 16)
            sp.dma_start(o_this, dst[0:E - 1].rearrange("(a b) -> a b", b=OC)).then_inc(sem("order_in"), 16)
            sp.dma_start(o_next, dst[1:E].rearrange("(a b) -> a b", b=OC)).then_inc(sem("order_in"), 16)
            sp.dma_start(srcS[0:E].rearrange("(a b) -> a b", a=160), src.rearrange("(a b) -> a b", a=160)).then_inc(sem("edges"), 16)
            sp.dma_start(dstS[0:E].rearrange("(a b) -> a b", a=160), dst.rearrange("(a b) -> a b", a=160)).then_inc(sem("edges"), 16)
            sp.wait_ge(sem("pads"), 1)
            one = lambda t, a, b: t[a:b].rearrange("(a b) -> a b", a=1)
            sp.dma_start(one(srcS, E, (ET + 1) * P), iota8_i[0:1, 0:(ET + 1) * P - E]).then_inc(sem("edges"), 16)
            sp.dma_start(one(dstS, E, ET * P), iota8_i[0:1, 256:256 + ET * P - E]).then_inc(sem("edges"), 16)
            sp.dma_start(one(dstS, ET * P, (ET + 1) * P), iota8_i[0:1, 384:384 + P]).then_inc(sem("edges"), 16)
            sp.wait_ge(sem("order_seen"), 1)
            sp.dma_start(downD[0:OR].rearrange("(a b) -> a b", b=1), o_sum[0:OR, :]).then_inc(sem("order_out"), 16)
            sp.wait_ge(sem("order_out"), 16)
            sp.dma_start(o_row[:, 0:OR], downD[0:OR].rearrange("(a b) -> a b", a=1)).then_inc(sem("order_row"), 16)
            sp.wait_ge(sem("edges_sorted"), 1)
            sp.wait_ge(sem("pads"), 4)
            lastd = dstS[0:ET * P].rearrange("(t e) -> t e", e=P)
            for b in range(NB):
                n = min(P, ET - b * P)
                sp.dma_start(last_i[0:n, b:b + 1], lastd[b * P:b * P + n, P - 1:P], allow_slow_non_contiguous=True).then_inc(sem("last_in"), 16)
            for i, w in enumerate((Wq, Wk, Wv, Ws)):
                sp.dma_start(w_gnn[:, :, i * D:(i + 1) * D], w.rearrange("(k p) n -> p k n", p=P)).then_inc(sem("w_in"), 16)
            sp.dma_start(w_mix[:, :, :], w_qkv.rearrange("(k p) n -> p k n", p=P)).then_inc(sem("w_in"), 16)
            for i, w in enumerate((bq, bk, bv, bs)):
                sp.dma_start(b_gnn[:, i * D:(i + 1) * D], w.rearrange("(a n) -> a n", a=1).partition_broadcast(P)).then_inc(sem("w_in"), 16)
            sp.dma_start(b_mix[:, :], b_qkv.rearrange("(a n) -> a n", a=1).partition_broadcast(P)).then_inc(sem("w_in"), 16)
            sp.dma_start(emb[:, :], edge_emb).then_inc(sem("w_in"), 16)
            sp.wait_ge(sem("relB_made"), 1)
            sp.dma_start(relD.rearrange("(b p) e -> p b e", p=P), relB.rearrange("p (b e) -> p b e", b=NB)).then_inc(sem("rel_out"), 16)
            sp.wait_ge(sem("xn_made"), NW)
            sp.dma_start(xnD.rearrange("(t p) d -> p t d", p=P), nodes[:, 0:NW * D].rearrange("p (t d) -> p t d", d=D)).then_inc(sem("xn_out"), 16)
            sp.wait_ge(sem("xn_out"), 16)
            sp.sem_inc(sem("xn_stored"), 1)
            sp.sem_inc(sem("stored"), CREDIT)

            def store(t, k):
                sp.wait_ge(sem("qk_sb"), done(t))
                sp.dma_start(kD[ds(t * P, P), :], kS[k]).then_inc(sem("proj_out"), 16)
                sp.wait_ge(sem("proj_out"), t * 16 + 16)
                sp.sem_inc(sem("stored"), 1)
            with sp.Fori(0, NW // 2) as it:
                for k in range(2):
                    store(it * 2 + k, k)
            store(NW - 1, 0)
            sp.wait_ge(sem("att_sb"), 4)
            for i, (w, n) in enumerate(((norm_g, NF), (norm_b, NF), (b_fc1, NM))):
                sp.dma_start(a_row[NF * i:NF * i + n, :], w.rearrange("(k p) -> k p", p=P)).then_inc(sem("mix_in"), 16)
            sp.dma_start(b_gnn[:, 0:D], b_fc2.rearrange("(a n) -> a n", a=1).partition_broadcast(P)).then_inc(sem("mix_in"), 16)
            f1 = w_fc1.rearrange("(k p) n -> p k n", p=P)
            sp.dma_start(w_gnn[:, :, 0:MA * P], f1[:, :, 0:MA * P]).then_inc(sem("mix_in"), 16)
            sp.dma_start(w_f2[:, :, :], w_fc2.rearrange("(k p) n -> p k n", p=P)).then_inc(sem("mix_in"), 16)

            def rel_load(j, b):
                sp.wait_ge(sem("oh_made"), reuse(j, 2))
                sp.dma_start(relq[b], relD[ds(j * G, G), :].rearrange("(a g) e -> a (g e)", a=1).partition_broadcast(P)).then_inc(sem(f"relq_in{b}"), 16)

            def tiles(t, g, n):
                return t[ds(g * (TG * P), n * P), :].rearrange("(t p) d -> p t d", p=P)

            def mix_load(g, b, n):
                sp.dma_start(m_xn[b][:, 0:n * D].rearrange("p (t d) -> p t d", d=D), tiles(xnD, g, n)).then_inc(sem(f"mix_rows{b}"), 16)
                if n == TG:
                    sp.dma_start(m_x[b].rearrange("p (t d) -> p t d", d=D), tiles(x, g, n)).then_inc(sem(f"mix_rows{b}"), 16)
                else:
                    sp.dma_start(m_x[b][0:TAIL, 0:D], x[(NW - 1) * P:N, :]).then_inc(sem(f"mix_rows{b}"), 16)

            def mix_store(g, n):
                sp.wait_ge(sem("m_out"), done(g))
                sp.dma_start(tiles(resD, g, n), m_x1[:, 0:n * D].rearrange("p (t d) -> p t d", d=D)).then_inc(sem("res_out"), 16)
                sp.wait_ge(sem("res_out"), g * 16 + 16)
                sp.sem_inc(sem("res_stored"), 1)

            def v_store(g, n):
                sp.wait_ge(sem("v_sb"), done(g))
                sp.dma_start(tiles(vD, g, n), m_v[:, 0:n * D].rearrange("p (t d) -> p t d", d=D)).then_inc(sem("v_out"), 16)

            def pass1(g, b, n, nxt, before):
                for p in range(PIECES):
                    if not (isinstance(g, int) and g == NG) or p < PIECES - 2:
                        rel_load(g * PIECES + (p + 2), p % 2)
                    if p == 0 and before:
                        mix_store(g - 1, before)
                    if p == 1 and nxt:
                        if nxt == 1:
                            sp.wait_ge(sem("m_x_zero"), 1)
                        sp.wait_ge(sem("m_out"), reuse(g + 1, 2))
                        mix_load(g + 1, 1 - b, nxt)
                    if p == 4:
                        v_store(g, n)
            sp.sem_inc(sem("res_stored"), CREDIT)
            sp.wait_ge(sem("rel_out"), 16)
            sp.wait_ge(sem("att_used"), 1)
            sp.dma_start(w_mix[:, :, D:D + MH - MA * P], f1[:, :, MA * P:MH]).then_inc(sem("fc1_in"), 16)
            rel_load(0, 0)
            rel_load(1, 1)
            mix_load(0, 0, TG)
            pass1(0, 0, TG, TG, 0)
            with sp.Fori(0, NG // 2 - 1) as it:
                for b in range(2):
                    pass1(it * 2 + (b + 1), 1 - b, TG, TG, TG)
            pass1(NG - 1, 1, TG, 1, TG)
            pass1(NG, 0, 1, 0, TG)
            mix_store(NG, 1)

            sp.wait_ge(sem("ex_cols"), 1)
            for i, w in enumerate((W1, W2, Wo)):
                sp.dma_start(e_w[i].rearrange("p (e n) -> p e n", n=D), w.rearrange("e (k p) n -> p (e k) n", p=P)).then_inc(sem("exp_in"), 16)
            sp.dma_start(e_bo, bo).then_inc(sem("exp_in"), 16)
            sp.dma_start(e_wr, Wr.rearrange("(k p) n -> p k n", p=P)).then_inc(sem("exp_in"), 16)
            sp.dma_start(e_br, br.rearrange("(a n) -> a n", a=1).partition_broadcast(P)).then_inc(sem("exp_in"), 16)
            for l, ws in enumerate(((g1, b1, be1, m1, v1), (g2, b2, be2, m2, v2))):
                for i, w in enumerate(ws):
                    sp.dma_start(e_prow[l][16 * i:16 * (i + 1), :], w.rearrange("e (k p) -> (e k) p", p=P)).then_inc(sem("exp_in"), 16)

            def tiles2(t, g, n):
                return t[ds(g * (T2 * P), n * P), :].rearrange("(t p) d -> p t d", p=P)

            def res_load(g, b, n):
                sp.dma_start(f_res[b][:, 0:n * D].rearrange("p (t d) -> p t d", d=D), tiles2(resD, g, n)).then_inc(sem(f"res_in{b}"), 16)

            def out_store(g, b, n):
                sp.wait_ge(sem("y_made"), done(g * NE + (NE - 1)))
                if n == T2:
                    sp.dma_start(tiles2(out, g, n), f_y[b].rearrange("p (t d) -> p t d", d=D)).then_inc(sem("out_sent"), 16)
                else:
                    sp.dma_start(out[(NW - 1) * P:N, :], f_y[b][0:TAIL, 0:D]).then_inc(sem("out_sent"), 16)
                sp.wait_ge(sem("out_sent"), g * 16 + 16)
                sp.sem_inc(sem("y_stored"), 1)
            sp.sem_inc(sem("y_stored"), CREDIT)
            sp.wait_ge(sem("acc_made"), done(NHF - 1))
            sp.wait_ge(sem("res_stored"), done(NG))
            res_load(0, 0, T2)
            res_load(1, 1, T2)

            def experts(g, b, n, later):
                if later:
                    sp.wait_ge(sem("y_init"), done(g))
                    res_load(g + 2, b, later)
                out_store(g, b, n)
            with sp.Fori(0, NG2 // 2 - 1) as it:
                for b in range(2):
                    experts(it * 2 + b, b, T2, T2)
            experts(NG2 - 2, 0, T2, 1)
            experts(NG2 - 1, 1, T2, 0)
            experts(NG2, 0, 1, 0)
            sp.wait_ge(sem("out_sent"), 16 * (NG2 + 1))

        @block.gpsimd
        def _(pool):
            pool.iota(iota_s, pattern=[[1, NSP]], base=0, channel_multiplier=0, allow_small_or_imprecise_dtypes=True).then_inc(sem("iotas"), 1)
            pool.iota(iota_f[:, :], pattern=[[1, P]], base=0, channel_multiplier=0, allow_small_or_imprecise_dtypes=True).then_inc(sem("iotas"), 1)
            pool.iota(iota_p[:, :], pattern=[[0, 1]], base=0, channel_multiplier=1, allow_small_or_imprecise_dtypes=True).then_inc(sem("iotas"), 1)
            pool.iota(icol[:, 0:NB], pattern=[[P, NB]], base=0, channel_multiplier=1, allow_small_or_imprecise_dtypes=True).then_inc(sem("iotas"), 1)
            pool.memset(ident[:, :], 0.0).then_inc(sem("ident"), 1)
            pool.wait_ge(sem("ident"), 1)
            pool.affine_select(out=ident[:, :], in_=ident[:, :], compare_op=ALU.not_equal, fill=1.0,
                               base=0, pattern=[[-1, P]], channel_multiplier=1).then_inc(sem("ident"), 1)
            pool.memset(ones[:, :], 1.0).then_inc(sem("iotas"), 1)
            pool.wait_ge(sem("edges"), 80)
            pool.iota(iota8_i, pattern=[[1, NK], [0, G]], base=0, channel_multiplier=0).then_inc(sem("iotas"), 1)

            def settled(ins):
                ins.then_inc(sem("sort_step"), 1)
                pool.wait_ge(sem("sort_step"), 1)
                pool.sem_clear(sem("sort_step"))

            sent = [0, "table_moves"]

            def moved(ins):
                sent[0] = sent[0] + 1
                ins.then_inc(sem(sent[1]), 16)
                pool.wait_ge(sem(sent[1]), sent[0] * 16)
                pool.sem_inc(sem("sort_seen"), 1)

            def offset(t):
                return bass.IndirectOffsetOnAxis(ap=t, axis=0)

            def tally(t):
                e = dstS[ds(t * P, P)]
                moved(pool.dma_start(t_row, e.rearrange("(a b) -> a b", a=1).partition_broadcast(P)))
                moved(pool.dma_start(t_col[:, 0:1], e.rearrange("(a b) -> a b", b=1)))
                pool.tensor_copy(t_rowf, t_row)
                pool.tensor_copy(t_dst_u, t_col[:, 0:1])
                settled(pool.tensor_copy(t_colf, t_col[:, 0:1]))
                settled(pool.tensor_scalar(t_cnt[:, 0, :], t_rowf, t_colf, None, ALU.is_equal))
                settled(pool.tensor_tensor(t_cnt[:, 1, :], t_cnt[:, 0, :], t_low, ALU.mult))
                n = P // 2
                while n:
                    settled(pool.tensor_tensor(t_cnt[:, :, 0:n], t_cnt[:, :, 0:n], t_cnt[:, :, n:2 * n], ALU.add))
                    n //= 2
                moved(pool.indirect_dma_start(out=t_next, out_offset=None, in_=table1, in_offset=offset(t_dst_u)))

            def advance():
                settled(pool.tensor_tensor(t_next, t_next, t_cnt[:, 0, 0:1], ALU.add))
                moved(pool.indirect_dma_start(out=table1, out_offset=offset(t_dst_u), in_=t_next, in_offset=None))

            table1 = nextD.rearrange("(a b) -> a b", b=1)
            table2 = nextD.rearrange("(a b) -> a b", b=P)
            pool.wait_ge(sem("order_flag"), 1)
            _, unsorted = nc.values_load_multi_w_load_instructions(o_flag, engines=(pool.engine,), min_val=0, max_val=1)
            with pool.If(unsorted[0]):
                settled(pool.tensor_scalar(t_low, iota_f[:, :], iota_p[:, 0:1], None, ALU.is_lt))
                settled(pool.memset(t_table, 0.0))
                moved(pool.dma_start(table2, t_table))
                base_moves = sent[:]
                with pool.Fori(0, ET) as t:
                    sent[:] = [t * 4, "count_moves"]
                    tally(t)
                    advance()
                sent[:] = base_moves
                moved(pool.dma_start(t_table, table2))
                settled(pool.tensor_copy(t_base[0], t_table))
                src_, n = 0, 1
                while n < P:
                    settled(pool.tensor_copy(t_base[1 - src_], t_base[src_]))
                    settled(pool.tensor_tensor(t_base[1 - src_][:, n:P], t_base[src_][:, n:P], t_base[src_][:, 0:P - n], ALU.add))
                    src_, n = 1 - src_, 2 * n
                incl = t_base[src_]
                settled(pool.tensor_tensor(t_base[1 - src_], incl, t_table, ALU.subtract))
                tot = [work[0:1, 9 * P + P * i:10 * P + P * i] for i in range(3)]
                settled(pool.memset(tot[0], 0.0))
                moved(pool.dma_start(srcT[0:NW].rearrange("(a b) -> a b", b=1).bitcast(F32), incl[:, P - 1:P]))
                moved(pool.dma_start(tot[0][:, 0:NW], srcT[0:NW].rearrange("(a b) -> a b", a=1).bitcast(F32)))
                settled(pool.tensor_copy(tot[1], tot[0]))
                q, n = 1, 1
                while n < NW:
                    settled(pool.tensor_copy(tot[3 - q], tot[q]))
                    settled(pool.tensor_tensor(tot[3 - q][:, n:P], tot[q][:, n:P], tot[q][:, 0:P - n], ALU.add))
                    q, n = 3 - q, 2 * n
                settled(pool.tensor_tensor(tot[q], tot[q], tot[0], ALU.subtract))
                moved(pool.dma_start(srcT[0:NW].rearrange("(a b) -> a b", a=1).bitcast(F32), tot[q][:, 0:NW]))
                moved(pool.dma_start(t_colf[0:NW, :], srcT[0:NW].rearrange("(a b) -> a b", b=1).bitcast(F32)))
                settled(pool.tensor_scalar(t_base[1 - src_], t_base[1 - src_], t_colf[0:NW, :], None, ALU.add))
                moved(pool.dma_start(table2, t_base[1 - src_]))
                base_moves = sent[:]
                with pool.Fori(0, ET) as t:
                    sent[:] = [t * 4, "place_moves"]
                    tally(t)
                    sent[:] = [t * 3, "edge_moves"]
                    moved(pool.dma_start(t_col[:, 1:2], srcS[ds(t * P, P)].rearrange("(a b) -> a b", b=1)))
                    settled(pool.tensor_tensor(t_place, t_next, t_cnt[:, 1, 0:1], ALU.add))
                    settled(pool.tensor_copy(t_place_u, t_place))
                    for i, o in ((0, dstT), (1, srcT)):
                        moved(pool.indirect_dma_start(out=o.rearrange("(a b) -> a b", b=1), out_offset=offset(t_place_u), in_=t_col[:, i:i + 1], in_offset=None))
                    sent[:] = [t * 4 + 3, "place_moves"]
                    advance()
                sent[:] = base_moves
                for a, o in ((dstT, dstS), (srcT, srcS)):
                    moved(pool.dma_start(o[0:ET * P].rearrange("(a b) -> a b", b=P), a.rearrange("(a b) -> a b", b=P)))
            pool.sem_inc(sem("edges_sorted"), 1)
            pool.wait_ge(sem("steps"), 1)
            for b in range(NB):
                for t, o in ((srcS, sg_i), (dstS, dg_i)):
                    pool.indirect_dma_start(out=o[:, b * P:(b + 1) * P], out_offset=None, in_=t.rearrange("(t e) -> t e", e=P),
                                            in_offset=bass.IndirectOffsetOnAxis(ap=tcol_u[:, b:b + 1], axis=0)).then_inc(sem("rows_in"), 16)

            def gather(j, b, table):
                pool.wait_ge(sem("idx_made"), j + 1)
                pool.sem_inc(sem("gathers_begun"), 1)
                for h in range(2):
                    pool.wait_ge(sem("kv_used"), j * 2 + (h + 1))
                    pool.sem_inc(sem("gathers_begun"), 1)
                    for g in range(HG):
                        c = 2 * (b % 2) + h
                        pool.indirect_dma_start(out=kv[c][:, g, 0:D], out_offset=None, in_=table,
                                                in_offset=bass.IndirectOffsetOnAxis(ap=idx[b][:, HG * h + g:HG * h + g + 1], axis=0)).then_inc(sem(f"kv_in{c}"), 16)

            pool.sem_inc(sem("kv_used"), KV)
            pool.wait_ge(sem("proj_out"), NW * 16)
            pool.wait_ge(sem("att_used"), 1)
            with pool.Fori(0, NGR // 4) as it:
                for b in range(4):
                    gather(it * 4 + b, b, kD)
            pool.wait_ge(sem("v_out"), (NG + 1) * 16)
            for b in range(4):
                gather(NGR + b, b, vD)
                if b == 1:
                    pool.wait_ge(sem("seg_dve"), 3)
                    pool.memset(nodes[:, :], 0.0).then_inc(sem("acc_zero"), 1)
            with pool.Fori(1, NGR // 4) as it:
                for b in range(4):
                    gather(it * 4 + (b + NGR), b, vD)

        @block.scalar
        def _(act):
            act.wait_ge(sem("pads"), 2)
            act.wait_ge(sem("hist_in"), 96)
            for c in range(4):
                n = (NW - 1) // 4
                act.dma_start(nodes[:, c * n * D:(c + 1) * n * D].rearrange("p (t d) -> p t d", d=D),
                              x[c * n * P:(c + 1) * n * P, :].rearrange("(t p) d -> p t d", p=P)).then_inc(sem("x_in"), 16)
            act.dma_start(nodes[0:TAIL, (NW - 1) * D:NW * D], x[(NW - 1) * P:N, :]).then_inc(sem("x_in"), 16)
            for q in ("a_in", "xT_sb"):
                act.sem_inc(sem(q), CREDIT)
            act.wait_ge(sem("var_eps"), 1)
            act.activation(rstd[:, :], rstd[:, :], ACT.Sqrt).then_inc(sem("std"), 1)
            act.wait_ge(sem("xn_made"), NW)
            act.wait_ge(sem("gram0"), 1)
            act.sem_inc(sem("xs_in"), CREDIT)

            def take_x(t, k):
                act.wait_ge(sem("gram_ps"), reuse(t, 2))
                act.activation(xs[k][:, 0:D], nodes[:, ds(t * D, D)], ACT.Copy).then_inc(sem("xs_in"), 1)
            with act.Fori(0, NW // 2) as it:
                for k in range(2):
                    take_x(it * 2 + k, k)
            take_x(NW - 1, 0)
            act.wait_ge(sem("r4_made"), 1)

            for c in range(0, NW, 8):
                n = min(8, NW - c) * P
                act.wait_ge(sem("r4T_ps"), c // 8 + 1)
                act.activation(r4T[:, c * P:c * P + n], ps[0:NTYPE, 1024 * (c // 8 % 2):1024 * (c // 8 % 2) + n], ACT.Copy).then_inc(sem("r4T_sb"), 1)

            def take(t, k):
                act.wait_ge(sem("xT_ps"), reuse(t, 2))
                act.activation(xs[k][:, 0:D], nodes[:, ds(t * D, D)], ACT.Copy).then_inc(sem("a_in"), 1)

            def turned(t, k):
                act.wait_ge(sem("xT_ps"), done(t))
                act.wait_ge(sem("qk_ps"), reuse(t, 2))
                act.activation(xT[k], bank(2 + k, 0, D), ACT.Copy).then_inc(sem("xT_sb"), 1)
            take(0, 0)
            with act.Fori(0, NW // 2) as it:
                for k in range(2):
                    take(it * 2 + (k + 1), 1 - k)
                    turned(it * 2 + k, k)
            turned(NW - 1, 0)
            for q in ("m_T_sb", "m_r4_sb", "m_rT_sb"):
                act.sem_inc(sem(q), CREDIT)
            act.sem_inc(sem("m_std"), CREDIT)
            act.sem_inc(sem("gelu"), CREDIT)
            act.wait_ge(sem("a_neg"), 1)
            for i in range(2):
                act.activation(a_sm[:, i * C:(i + 1) * C], a_sm[:, i * C:(i + 1) * C], ACT.Exp, bias=a_v[1][:, i:i + 1],
                               scale=1.0 / C ** 0.5, accum_out=a_v[2][:, i:i + 1]).then_inc(sem("a_exp"), 1)

            def mix(g, p, n):
                if p == 0:
                    act.wait_ge(sem("m_T_ps"), done(g))
                    for i in range(NF):
                        ins = act.activation(m_T[:, i * TG * P:i * TG * P + n * P], bank(4 + i, 0, n * P), ACT.Copy)
                    ins.then_inc(sem("m_T_sb"), 1)
                    act.activation(m_r4[:, 0:n * NTYPE], r4[:, ds(g * (TG * NTYPE), n * NTYPE)], ACT.Copy).then_inc(sem("m_r4_sb"), 1)
                if p == 1:
                    act.wait_ge(sem("m_rT_ps"), done(g))
                    act.activation(m_rT[:, 0:n * P], bank(4, 0, n * P)[0:NTYPE, :], ACT.Copy).then_inc(sem("m_rT_sb"), 1)
                    act.wait_ge(sem("m_var"), done(g))
                    act.activation(m_rs[:, 0:n], m_rs[:, 0:n], ACT.Sqrt).then_inc(sem("m_std"), 1)
                if p in (4, 5):
                    for i in range(NM // 2):
                        m = NM // 2 * (p - 4) + i
                        act.wait_ge(sem("fc1_ps"), done(g * NM + m))
                        act.activation(m_gT[:, m * TG * P:m * TG * P + n * P], bank(4 + m % 2, 0, n * P), ACT.Gelu,
                                       bias=m_col[:, 2 * NF + m:2 * NF + m + 1]).then_inc(sem("gelu"), 1)

            def pass1(g, n):
                for p in range(PIECES):
                    mix(g, p, n)
            with act.Fori(0, NG // 2) as it:
                for b in range(2):
                    pass1(it * 2 + b, TG)
            pass1(NG, 1)

            act.wait_ge(sem("seg_dve"), 4)
            act.activation(atR, atR, ACT.Exp).then_inc(sem("ex_made"), 1)
            act.sem_inc(sem("ex_in"), CREDIT)
            act.wait_ge(sem("ex_cols"), 1)
            with act.Fori(0, NHF // KV) as it:
                for b in range(KV):
                    i = it * KV + b
                    act.wait_ge(sem("kv_used"), i + (NHF + 1))
                    act.activation(kv[b][:, :, D:AC], alpha[:, ds(i * (HG * H), HG * H)].rearrange("p (g h) -> p g h", g=HG), ACT.Copy).then_inc(sem("ex_in"), 1)

            for q in ("f_std", "f_T_sb", "f_exp", "f_wT_sb", "h1_sb", "h2_sb", "h1_up"):
                act.sem_inc(sem(q), CREDIT)
            act.wait_ge(sem("exp_in"), 256)
            act.wait_ge(sem("acc_made"), done(NHF - 1))
            act.wait_ge(sem("fc2_ps"), done(NG))
            act.wait_ge(sem("e_var"), 1)
            for l in range(2):
                ins = act.activation(e_sc[l], e_sc[l], ACT.Sqrt)
            ins.then_inc(sem("e_std"), 1)

            def first_part(g, b, n, q):
                if q == 1:
                    act.wait_ge(sem("f_var"), done(g))
                    act.activation(f_rs[:, 0:n], f_rs[:, 0:n], ACT.Sqrt).then_inc(sem("f_std"), 1)
                if q == 3:
                    act.wait_ge(sem("f_T_ps"), done(g))
                    for i in range(NF):
                        o = slice(i * T2 * P, i * T2 * P + n * P)
                        act.activation(f_T[b][0][:, o], bank(6, i * T2 * P, i * T2 * P + n * P), ACT.Copy)
                        ins = act.activation(f_zT[:, o], bank(6, i * T2 * P, i * T2 * P + n * P), ACT.Copy)
                    ins.then_inc(sem("f_T_sb"), 1)
                if q == 5:
                    act.wait_ge(sem("f_sub"), done(g))
                    act.activation(f_lg[:, 0:n * NE], f_lg[:, 0:n * NE], ACT.Exp).then_inc(sem("f_exp"), 1)
                if q == 6:
                    act.wait_ge(sem("f_wT_ps"), done(g))
                    act.activation(f_wT[:, 0:n * P], bank(7, P, P + n * P)[0:NE, :], ACT.Copy).then_inc(sem("f_wT_sb"), 1)

            def layer(l, u, e, n):
                s_ps, s_sb, s_lo, s_next = (("l1_ps", "h1_sb", "h1_lo", "l2_ps"), ("l2_ps", "h2_sb", "h2_lo", "l3_ps"))[l]
                act.wait_ge(sem(s_ps), done(u))
                act.wait_ge(sem(s_lo), reuse(u, 1))
                act.wait_ge(sem(s_next), reuse(u, 2))
                for m in range(NF):
                    ins = act.activation(f_whole[l][:, m * T2 * P:m * T2 * P + n * P], bank(2 * l + e % 2, m * T2 * P, m * T2 * P + n * P), ACT.Relu,
                                         bias=e_sh[l][:, e * NF + m:e * NF + m + 1], scale=e_sc[l][:, e * NF + m:e * NF + m + 1])
                ins.then_inc(sem(s_sb), 1)
                if l == 0:
                    act.wait_ge(sem(s_sb), done(u))
                    act.activation(spread(f_h[l][e % 2][0], n), spread(f_whole[l], n), ACT.Copy).then_inc(sem("h1_up"), 1)

            def experts(g, b, n, nxt):
                for e in range(NE):
                    u = g * NE + e
                    if e + 2 < NE or nxt:
                        layer(0, u + 2, (e + 2) % NE, n if e + 2 < NE else nxt)
                    if e + 1 < NE or nxt:
                        layer(1, u + 1, (e + 1) % NE, n if e + 1 < NE else nxt)
                    if nxt:
                        first_part(g + 1, 1 - b, nxt, e)
            for q in range(NE):
                first_part(0, 0, T2, q)
                if q < 3:
                    act.activation(e_upper[:, WE * q:WE * (q + 1)], e_w[q], ACT.Copy).then_inc(sem("e_upper"), 1)
            layer(0, 0, 0, T2)
            layer(0, 1, 1, T2)
            layer(1, 0, 0, T2)
            with act.Fori(0, NG2 // 2 - 1) as it:
                for b in range(2):
                    experts(it * 2 + b, b, T2, T2)
            experts(NG2 - 2, 0, T2, T2)
            experts(NG2 - 1, 1, T2, 1)
            experts(NG2, 0, 1, 0)

        @block.tensor
        def _(pe):
            for s in ("xT_ps", "qk_ps", "gram_ps", "m_rT_ps", "m_pT_ps", "v_ps", "hist_ps", "qg_ps", "agg_ps", "m_T_ps", "x1_ps", "m_hT_ps", "fc1_ps",
                      "fc2_ps", "f_T_ps", "lg_ps", "f_wT_ps", "bo_ps", "l1_ps", "l2_ps", "l3_ps"):
                pe.sem_inc(sem(s), CREDIT)
            pe.wait_ge(sem("iotas"), 5)
            pe.wait_ge(sem("ident"), 2)

            def turn(rowsrc, first):
                for b in range(NB):
                    last = pe.transpose(bank(first + b // 4, (b % 4) * P, (b % 4 + 1) * P), rowsrc[:, b * P:(b + 1) * P], ident[:, :])
                return last
            pe.wait_ge(sem("hist_rows"), 1)
            turn(lo_f, 4).then_inc(sem("hist_T"), 1)
            turn(key_f, 6).then_inc(sem("hist_T"), 1)
            pe.wait_ge(sem("hist_z"), 1)
            pe.matmul(bank(4, 0, NK), loh[0][:, 0:P], koh[0][:, 0:NK], start=True, stop=False, skip_group_check=True)
            pe.matmul(bank(4, 0, NK), loh[0][:, 0:P], koh[0][:, 0:NK], start=False, stop=False, skip_group_check=True).then_inc(sem("hist_zero"), 1)

            def tally(c, b):
                pe.wait_ge(sem("oneh"), done(c))
                lo = loh[b].rearrange("p (n g) -> p g n", g=G)
                ky = koh[b].rearrange("p (n g) -> p g n", g=G)
                for g in range(G):
                    last = pe.matmul(bank(4, 0, NK), lo[:, g, :], ky[:, g, :], start=False, stop=False, skip_group_check=True)
                last.then_inc(sem("hist_ps"), 1)

            def gram(t, k):
                pe.wait_ge(sem("xs_in"), done(t))
                for i in range(2):
                    last = pe.matmul(bank(6 + i, 0, D + 1), xs[k][:, i * P:(i + 1) * P], xs[k], start=False, stop=False, skip_group_check=True)
                last.then_inc(sem("gram_ps"), 1)
            with pe.Fori(0, HI1) as it:
                for b in range(2):
                    tally(it * 2 + b, b)
            pe.wait_ge(sem("cmp_made"), 1)
            for b in range(NB):
                pe.matmul(bank(0, b, b + 1), cmp[:, b * P:(b + 1) * P], ones[:, :], start=True, stop=True)
            for h in range(2):
                w = NSP // 2
                last = pe.matmul(bank(1 + h, 0, w)[0:1, :], ones[:, :], cmp[:, h * w:(h + 1) * w], start=True, stop=True)
            last.then_inc(sem("tcol_ps"), 1)
            pe.wait_ge(sem("rows_made"), 1)
            pe.wait_ge(sem("tcol_sb"), 1)
            turn(relR, 0).then_inc(sem("step_T"), 1)
            turn(sg_f, 2).then_inc(sem("step_T"), 1)
            pe.wait_ge(sem("gram0"), 1)
            for i in range(2):
                pe.matmul(bank(6 + i, 0, D + 1), zero_g[:, 0:P], zero_g, start=True, stop=False, skip_group_check=True)
            with pe.Fori(0, HI2) as it:
                for b in range(2):
                    tally(it * 2 + (2 * HI1 + b), b)
                    gram(it * 2 + b, b)
            gram(NW - 1, 0)
            with pe.Fori(0, HI - HI1 - HI2) as it:
                for b in range(2):
                    tally(it * 2 + (2 * (HI1 + HI2) + b), b)

            pe.wait_ge(sem("w_in"), 176)
            pe.wait_ge(sem("xn_made"), NW)
            pe.wait_ge(sem("r4_made"), 1)
            pe.wait_ge(sem("srcC_made"), 1)

            for c in range(0, NW, 8):
                if c >= 16:
                    pe.wait_ge(sem("r4T_sb"), c // 8 - 1)
                for t in range(c, min(NW, c + 8)):
                    last = pe.transpose(ps[0:NTYPE, 1024 * (c // 8 % 2) + (t - c) * P:1024 * (c // 8 % 2) + (t - c + 1) * P], r4[:, t * NTYPE:(t + 1) * NTYPE], ident[:, :])
                last.then_inc(sem("r4T_ps"), 1)
            pe.wait_ge(sem("r4T_sb"), -(-NW // 8))

            def turn_x(t, k):
                pe.wait_ge(sem("a_in"), done(t))
                pe.wait_ge(sem("xT_sb"), reuse(t, 2))
                for i in range(2):
                    o = bank(2 + k, i * P, (i + 1) * P)
                    pe.matmul(o, xs[k][:, i * P:(i + 1) * P], ident[:, :], start=True, stop=False)
                    last = pe.matmul(o, emb[:, i * P:(i + 1) * P], r4T[:, ds(t * P, P)], start=False, stop=True)
                last.then_inc(sem("xT_ps"), 1)

            def project(t, k):
                pe.wait_ge(sem("xT_sb"), done(t))
                pe.wait_ge(sem("qk_sb"), reuse(t, 2))
                for i in range(2):
                    last = pe.matmul(bank(4 + k), xT[k][:, i * P:(i + 1) * P], w_gnn[:, i, 0:2 * D], start=(i == 0), stop=(i == 1))
                last.then_inc(sem("qk_ps"), 1)
            turn_x(0, 0)
            with pe.Fori(0, NW // 2) as it:
                for k in range(2):
                    turn_x(it * 2 + (k + 1), 1 - k)
                    project(it * 2 + k, k)
            project(NW - 1, 0)

            pe.wait_ge(sem("att_sb"), 1)
            for i in range(2):
                last = pe.transpose(bank(6, i * P, (i + 1) * P)[0:1, :], g_G[:, i, D:D + 1], ident[:, :])
            last.then_inc(sem("att_ps"), 1)
            for i in range(2):
                last = pe.matmul(bank(7, 0, D)[0:1, :], g_G[:, i, D:D + 1], w_mix[:, i, 2 * D:3 * D], start=(i == 0), stop=(i == 1))
            last.then_inc(sem("att_ps"), 1)
            pe.wait_ge(sem("att_sb"), 2)
            pe.wait_ge(sem("qk_sb"), done(NW - 1))
            for i in range(2):
                for j in range(2):
                    pe.matmul(bank(4, i * D, (i + 1) * D), g_G[:, j, i * P:(i + 1) * P], w_mix[:, j, 2 * D:3 * D], start=(j == 0), stop=False)
                last = pe.matmul(bank(4, i * D, (i + 1) * D), g_s[:, i * P:(i + 1) * P], b_mix[0:1, 2 * D:3 * D], start=False, stop=True)
            last.then_inc(sem("att_ps"), 1)
            pe.wait_ge(sem("att_sb"), 3)
            for i in range(2):
                for a in range(2):
                    pe.matmul(bank(5, i * P, (i + 1) * P), w_mix[:, a, D + i * P:D + (i + 1) * P], g_U[:, a, i * P:(i + 1) * P], start=(a == 0), stop=False)
                last = pe.matmul(bank(5, i * P, (i + 1) * P), b_mix[0:1, D + i * P:D + (i + 1) * P], g_t[:, i * P:(i + 1) * P], start=False, stop=True)
            last.then_inc(sem("att_ps"), 1)
            pe.wait_ge(sem("att_sb"), 4)
            for a in range(2):
                for i in range(2):
                    last = pe.transpose(bank(2, (2 * i + a) * P, (2 * i + a + 1) * P), w_mix[:, a, i * P:(i + 1) * P], ident[:, :])
            for i in range(2):
                last = pe.transpose(bank(3, i * P, (i + 1) * P), b_mix[:, i * P:(i + 1) * P], ident[:, :])
            pe.wait_ge(sem("mix_in"), 96)
            n_ = 2 * NF + NM
            pe.transpose(bank(3, 2 * P, 2 * P + n_), a_row[0:n_, :], ident[0:n_, 0:n_]).then_inc(sem("att_ps"), 1)
            pe.wait_ge(sem("att_sb"), 5)
            for i in range(2):
                last = pe.transpose(bank(0, i * P, (i + 1) * P), a_bd[:, i * P:(i + 1) * P], ident[:, :])
            last.then_inc(sem("att_ps"), 1)
            pe.wait_ge(sem("att_sb"), 6)
            for i in range(2):
                for a in range(2):
                    pe.matmul(bank(1, a * D + i * P, a * D + (i + 1) * P), a_wT[:, (2 * i + a) * P:(2 * i + a + 1) * P], a_T[:, i * P:(i + 1) * P], start=True, stop=True)
                last = pe.matmul(bank(0, D + i * P, D + (i + 1) * P), a_bT[:, i * P:(i + 1) * P], a_T[:, i * P:(i + 1) * P], start=True, stop=True)
            last.then_inc(sem("att_ps"), 1)
            pe.wait_ge(sem("att_sb"), 7)
            pe.wait_ge(sem("qk_sb"), done(NW - 1))

            def mix(g, b, p, n):
                if p == 0:
                    pe.wait_ge(sem(f"mix_rows{b}"), (g - b) * 16 + 32)
                    pe.wait_ge(sem("gelu"), done(g * NM - 1))
                    for t in range(n):
                        for i in range(NF):
                            last = pe.transpose(bank(4 + i, t * P, (t + 1) * P), m_xn[b][:, t * D + i * P:t * D + (i + 1) * P], ident[:, :])
                    last.then_inc(sem("m_T_ps"), 1)
                if p == 1:
                    pe.wait_ge(sem("m_T_sb"), done(g))
                    pe.wait_ge(sem("m_r4_sb"), done(g))
                    for t in range(n):
                        last = pe.transpose(bank(4, t * P, (t + 1) * P)[0:NTYPE, :], m_r4[:, t * NTYPE:(t + 1) * NTYPE], ident[:, :])
                    last.then_inc(sem("m_rT_ps"), 1)
                    pe.wait_ge(sem("m_out"), reuse(g, 1))
                    for t in range(n):
                        for i in range(NF):
                            last = pe.matmul(bank(6 + t // 2, t % 2 * D, (t % 2 + 1) * D), m_T[:, i * TG * P + t * P:i * TG * P + (t + 1) * P], w_qf[:, i, :], start=(i == 0), stop=(i == 1))
                    last.then_inc(sem("x1_ps"), 1)
                    pe.wait_ge(sem("m_rT_sb"), done(g))
                    for i in range(NF):
                        last = pe.matmul(bank(4 + i, 0, n * P), emb[:, i * P:(i + 1) * P], m_rT[:, 0:n * P], start=True, stop=True)
                    last.then_inc(sem("m_pT_ps"), 1)
                if p == 2:
                    pe.wait_ge(sem("m_pT_sb"), done(g))
                    pe.wait_ge(sem("m_var"), done(g))
                    for t in range(n):
                        for i in range(NF):
                            last = pe.matmul(bank(6 + t // 2, t % 2 * D, (t % 2 + 1) * D), m_pT[:, i * TG * P + t * P:i * TG * P + (t + 1) * P],
                                             w_gnn[:, i, 2 * D:3 * D], start=(i == 0), stop=(i == 1))
                    last.then_inc(sem("v_ps"), 1)
                if p == 3:
                    pe.wait_ge(sem("m_z"), done(g))
                    for t in range(n):
                        for i in range(NF):
                            last = pe.transpose(bank(4 + i, t * P, (t + 1) * P), m_xn[b][:, t * D + i * P:t * D + (i + 1) * P], ident[:, :])
                    last.then_inc(sem("m_hT_ps"), 1)
                    pe.wait_ge(sem("v_sb"), done(g))
                    for t in range(n):
                        for i in range(NF):
                            pe.matmul(bank(6 + t // 2, t % 2 * D, (t % 2 + 1) * D), m_pT[:, i * TG * P + t * P:i * TG * P + (t + 1) * P],
                                      w_gnn[:, i, 3 * D:4 * D], start=(i == 0 and t % 2 == 0), stop=False, skip_group_check=True)
                if p in (4, 5):
                    pe.wait_ge(sem("fc1_in"), 16)
                    pe.wait_ge(sem("m_hT_sb"), done(g))
                    for k in range(NM // 2):
                        m = NM // 2 * (p - 4) + k
                        if m >= 2:
                            pe.wait_ge(sem("gelu"), done(g * NM + (m - 2)))
                        for i in range(NF):
                            last = pe.matmul(bank(4 + m % 2, 0, n * P), w_f1(i, m), m_hT[:, i * TG * P:i * TG * P + n * P], start=(i == 0), stop=(i == 1))
                        last.then_inc(sem("fc1_ps"), 1)
                if p in (6, 7):
                    pe.wait_ge(sem("gelu"), done(g * NM + (NM - 1)))
                    last = None
                    for t in range(2 * (p - 6), min(n, 2 * (p - 6) + 2)):
                        for m in range(NM):
                            last = pe.matmul(bank(6 + t // 2, t % 2 * D, (t % 2 + 1) * D), m_gT[:, m * TG * P + t * P:m * TG * P + (t + 1) * P], w_f2[:, m, :],
                                             start=False, stop=(m == NM - 1), skip_group_check=True)
                    if p == 7 and last is not None or n == 1 and p == 6:
                        last.then_inc(sem("fc2_ps"), 1)

            def edges(j, b):
                _, win = nc.values_load_multi_w_load_instructions(wrow[0:1, ds(j * G, G)], engines=(pe.engine,), min_val=0, max_val=NW - 1)
                pe.wait_ge(sem("oh_made"), done(j))
                for h in range(2):
                    pe.wait_ge(sem("prod_made"), reuse(j * 2 + h, 2))
                    for g in range(4):
                        s = 4 * h + g
                        last = pe.matmul(ps[:, 1024 * h + 256 * g:1024 * h + 256 * (g + 1)], oh[b][:, s * P:(s + 1) * P],
                                         nodes[:, ds(win[s] * D, D)], start=True, stop=True)
                    last.then_inc(sem("qg_ps"), 1)

            def pass1(g, b, n):
                for p in range(PIECES):
                    mix(g, b, p, n)
                    if not (isinstance(g, int) and g == NG) or p < PIECES - 1:
                        edges(g * PIECES + (p + 1), (p + 1) % 2)
            edges(0, 0)
            with pe.Fori(0, NG // 2) as it:
                for b in range(2):
                    pass1(it * 2 + b, b, TG)
            pass1(NG, 0, 1)

            pe.wait_ge(sem("kv_used"), NHF + KV)
            pe.wait_ge(sem("alpha_pad"), 1)
            al = alpha[:, :].rearrange("p (s h) -> p h s", h=H)
            for h in range(H):
                for b in range(NB):
                    last = pe.transpose(ps[:, 1024 * h + b * P:1024 * h + (b + 1) * P], al[:, h, b * P:(b + 1) * P], ident[:, :])
                last.then_inc(sem("row_turn"), 1)
            pe.wait_ge(sem("seg_dve"), 1)
            for i in range(4):
                for b in range(NB):
                    last = pe.transpose(ps[0:H, 1024 * i + b * P:1024 * i + (b + 1) * P], ends[i][:, b * H:(b + 1) * H], ident[:, :])
            last.then_inc(sem("seg_ps"), 1)
            pe.wait_ge(sem("seg_dve"), 2)
            for i in range(2):
                for b in range(NB):
                    last = pe.transpose(bank(i, b * H, (b + 1) * H), carry[i][:, b * P:(b + 1) * P], ident[0:H, 0:H])
            last.then_inc(sem("seg_ps"), 1)
            pe.wait_ge(sem("ex_made"), 1)
            pe.wait_ge(sem("seg_dve"), 3)
            for h in range(H):
                for b in range(NB):
                    n = h * NB + b
                    last = pe.transpose(ps[:, 1024 * h + b * P:1024 * h + (b + 1) * P], atR[:, n * P:(n + 1) * P], ident[:, :])
                last.then_inc(sem("col_turn"), 1)

            pe.wait_ge(sem("ex_cols"), 1)
            pe.wait_ge(sem("slots_made"), 1)
            with pe.Fori(0, NHF // KV) as it:
                for b in range(KV):
                    i = it * KV + b
                    _, place = nc.values_load_multi_w_load_instructions(slot_w[0:1, ds(i * HG, HG)], engines=(pe.engine,), min_val=0, max_val=HG - 1)
                    pe.wait_ge(sem("acc_made"), reuse(i, 2))
                    for g in range(HG):
                        pe.matmul(bank(4 * (b % 2) + g, 0, AC), zeros[:, 0:P], zeros, start=True, stop=False, skip_group_check=True)
                    pe.wait_ge(sem("oh2_made"), done(i))
                    pe.wait_ge(sem("ex_in"), done(i))
                    for g in range(HG):
                        last = pe.matmul(ps[:, ds(place[g] * 512 + 2048 * (b % 2), AC)], ohh[b][:, g * P:(g + 1) * P], kv[b][:, g, :],
                                         start=False, stop=False, skip_group_check=True)
                    last.then_inc(sem("agg_ps"), 1)

            pe.wait_ge(sem("exp_in"), 256)
            pe.wait_ge(sem("acc_made"), done(NHF - 1))
            for l in range(2):
                last = pe.transpose(bank(2, l * 80, (l + 1) * 80), e_prow[l][0:80, :], ident[0:80, 0:80])
            last.then_inc(sem("par_turn"), 1)

            def first_part(g, b, n, q):
                if q == 3:
                    pe.wait_ge(sem("f_z_made"), done(g))
                    pe.wait_ge(sem("y_init"), reuse(g, 1))
                    for t in range(n):
                        for i in range(NF):
                            last = pe.transpose(bank(6, i * T2 * P + t * P, i * T2 * P + (t + 1) * P), f_z[:, t * D + i * P:t * D + (i + 1) * P], ident[:, :])
                    last.then_inc(sem("f_T_ps"), 1)
                if q == 4:
                    pe.wait_ge(sem("f_T_sb"), done(g))
                    for t in range(n):
                        for i in range(NF):
                            last = pe.matmul(bank(7, t * NE, (t + 1) * NE), f_zT[:, i * T2 * P + t * P:i * T2 * P + (t + 1) * P], e_wr[:, i, :], start=(i == 0), stop=(i == 1))
                    last.then_inc(sem("lg_ps"), 1)
                if q == 6:
                    pe.wait_ge(sem("f_w_made"), done(g))
                    for t in range(n):
                        last = pe.transpose(bank(7, P + t * P, P + (t + 1) * P)[0:NE, :], f_w[b][:, t * NE:(t + 1) * NE], ident[:, :])
                    last.then_inc(sem("f_wT_ps"), 1)
                if q == 7:
                    pe.wait_ge(sem("f_wT_sb"), done(g))
                    for t in range(n):
                        last = pe.matmul(bank(6, t * D, (t + 1) * D), f_wT[:, t * P:(t + 1) * P], e_bo, start=True, stop=True)
                    last.then_inc(sem("bo_ps"), 1)

            PASSES = ((0, 0), (0, 1), (1, 0))

            def layer(l, u, e, b, g, n):
                s_ps, s_sb, src_ = (("l1_ps", "h1_sb", f_T[b]), ("l2_ps", "h2_sb", f_h[0][e % 2]))[l]
                if l == 1:
                    pe.wait_ge(sem("h1_lo"), done(u))
                elif e == 0:
                    pe.wait_ge(sem("f_T_lo"), done(g))
                pe.wait_ge(sem(s_sb), reuse(u, 2))
                for m in range(NF):
                    for i in range(NF):
                        for w, a in PASSES:
                            last = pe.matmul(bank(2 * l + e % 2, m * T2 * P, m * T2 * P + n * P), e_parts[l][w][:, e, i, m * P:(m + 1) * P],
                                             src_[a][:, i * T2 * P:i * T2 * P + n * P], start=(i == 0 and w + a == 0), stop=(i == NF - 1 and w == 1))
                last.then_inc(sem(s_ps), 1)

            def last_layer(u, e, n):
                pe.wait_ge(sem("h2_lo"), done(u))
                pe.wait_ge(sem("y_made"), reuse(u, 2))
                for t in range(n):
                    for i in range(NF):
                        for w, a in PASSES:
                            last = pe.matmul(bank(4 + e % 2, t * D, (t + 1) * D), f_h[1][e % 2][a][:, i * T2 * P + t * P:i * T2 * P + (t + 1) * P],
                                             e_parts[2][w][:, e, i, :], start=(i == 0 and w + a == 0), stop=(i == NF - 1 and w == 1))
                last.then_inc(sem("l3_ps"), 1)

            def experts(g, b, n, nxt):
                for e in range(NE):
                    u = g * NE + e
                    if e + 2 < NE:
                        layer(0, u + 2, e + 2, b, g, n)
                    elif nxt:
                        layer(0, u + 2, e + 2 - NE, 1 - b, g + 1, nxt)
                    if e + 1 < NE or nxt:
                        layer(1, u + 1, (e + 1) % NE, b, g, n if e + 1 < NE else nxt)
                    last_layer(u, e, n)
                    if nxt:
                        first_part(g + 1, 1 - b, nxt, e)
            for q in range(NE):
                first_part(0, 0, T2, q)
            pe.wait_ge(sem("e_ready"), 4)
            layer(0, 0, 0, 0, 0, T2)
            layer(0, 1, 1, 0, 0, T2)
            layer(1, 0, 0, 0, 0, T2)
            with pe.Fori(0, NG2 // 2 - 1) as it:
                for b in range(2):
                    experts(it * 2 + b, b, T2, T2)
            experts(NG2 - 2, 0, T2, T2)
            experts(NG2 - 1, 1, T2, 1)
            experts(NG2, 0, 1, 0)

        @block.vector
        def _(dve):
            for s in ("oneh", "qk_sb", "m_pT_sb", "v_sb", "oh_made", "prod_made", "oh2_made", "acc_made",
                      "m_var", "m_z", "m_hT_sb", "m_out", "f_var", "f_z_made", "f_sub", "f_w_made", "y_init", "y_made", "f_T_lo", "h1_lo", "h2_lo", "h2_up"):
                dve.sem_inc(sem(s), CREDIT)
            link_n = [0]

            def link(ins):
                link_n[0] += 1
                ins.then_inc(sem("link"), 1)
                dve.wait_ge(sem("link"), link_n[0])

            dve.memset(iota8_i[0:1, 0:256], 0)
            dve.memset(iota8_i[0:1, 256:384], NW * P - 1)
            dve.memset(iota8_i[0:1, 384:512], FAR).then_inc(sem("pads"), 1)
            dve.memset(nodes[:, (NW - 1) * D:NW * D], 0.0).then_inc(sem("pads"), 1)
            dve.memset(hs_i, P * 63)
            dve.memset(hy_i, 0).then_inc(sem("pads"), 1)
            dve.memset(last_i, FAR).then_inc(sem("pads"), 1)

            dve.wait_ge(sem("hist_in"), 96)
            link(dve.tensor_scalar(hi_i, hs_i, 7, None, ALU.logical_shift_right))
            link(dve.tensor_scalar(lo_i, hs_i, P - 1, None, ALU.bitwise_and))
            link(dve.tensor_copy(lo_f, lo_i))
            link(dve.tensor_copy(key_f, hi_i))
            dve.scalar_tensor_tensor(out=key_f, in0=key_f, scalar=float(NTYPE), in1=hy_i, op0=ALU.mult, op1=ALU.add).then_inc(sem("hist_rows"), 1)

            dve.wait_ge(sem("order_in"), 32)
            link(dve.tensor_tensor(o_gt, o_this, o_next, ALU.is_gt))
            dve.tensor_reduce(o_sum[0:OR, :], o_gt, AX_X, ALU.add).then_inc(sem("order_seen"), 1)
            dve.wait_ge(sem("order_row"), 16)
            link(dve.tensor_reduce(o_row[:, P - 1:P], o_row[:, 0:OR], AX_X, ALU.max))
            dve.tensor_scalar(o_flag, o_row[:, P - 1:P], 1.0, None, ALU.min).then_inc(sem("order_flag"), 1)

            dve.wait_ge(sem("hist_T"), 1)
            dve.tensor_copy(loC, ps[:, 4 * 512:4 * 512 + HT])
            dve.wait_ge(sem("hist_T"), 2)
            dve.tensor_copy(keyC, ps[:, 6 * 512:6 * 512 + HT]).then_inc(sem("hist_cols"), 1)
            dve.wait_ge(sem("iotas"), 6)
            dve.wait_ge(sem("hist_cols"), 1)
            link(dve.tensor_copy(iota8, iota8_i))
            link(dve.memset(rows[:, 11 * NSP:11 * NSP + 512], 0.0))
            link(dve.memset(koh[0], 0.0))
            dve.sem_inc(sem("hist_z"), 1)
            dve.wait_ge(sem("hist_zero"), 1)
            def one_hot_keys(c, b):
                dve.wait_ge(sem("hist_ps"), reuse(c, 2))
                for o, k, n in ((loh[b], loC, P), (koh[b], keyC, NK)):
                    ins = dve.tensor_tensor(o.rearrange("p (n g) -> p n g", g=G), k[:, ds(c * G, G)].unsqueeze(1).broadcast_to([P, n, G]),
                                            iota8[:, 0:n * G].rearrange("p (n g) -> p n g", g=G), ALU.is_equal)
                ins.then_inc(sem("oneh"), 1)

            def histogram(first, n):
                with dve.Fori(0, n) as it:
                    for b in range(2):
                        one_hot_keys(it * 2 + (first * 2 + b), b)
            histogram(0, HI1)

            dve.wait_ge(sem("x_in"), 80)
            with dve.Fori(0, NW // 7) as it:
                for u in range(7):
                    t = it * 7 + u
                    dve.bn_stats(stats[:, ds(t * 6, 6)], nodes[:, ds(t * D, D)]).then_inc(sem("bn"), 1)
            dve.wait_ge(sem("bn"), NW)
            for t in range(NW):
                dve.bn_aggr(mv[:, t * 2:(t + 1) * 2], stats[:, t * 6:(t + 1) * 6]).then_inc(sem("bn"), 1)
            dve.wait_ge(sem("bn"), 2 * NW)
            dve.tensor_scalar(rstd[:, :], mv[:, :].rearrange("p (t c) -> p c t", c=2)[:, 1, :], EPS, None, ALU.add).then_inc(sem("var_eps"), 1)
            dve.wait_ge(sem("last_in"), 16 * NB)
            dve.wait_ge(sem("iotas"), 5)
            link(dve.tensor_scalar(last_w[:, 0:NB], last_i[:, 0:NB], 7, None, ALU.logical_shift_right))
            link(dve.tensor_copy(stepkey[:, 0:NB], last_w[:, 0:NB]))
            link(dve.tensor_tensor(stepkey[:, 0:NB], stepkey[:, 0:NB], icol[:, 0:NB], ALU.add))
            link(dve.tensor_scalar(cmp, iota_s, stepkey[:, 0:1], None, ALU.is_gt))
            for b in range(1, NB):
                ins = dve.scalar_tensor_tensor(out=cmp, in0=iota_s, scalar=stepkey[:, b:b + 1], in1=cmp, op0=ALU.is_gt, op1=ALU.add)
                if b < NB - 1:
                    link(ins)
            ins.then_inc(sem("cmp_made"), 1)
            dve.wait_ge(sem("std"), 1)
            link(dve.reciprocal(rstd[:, :], rstd[:, :]))
            dve.wait_ge(sem("tcol_ps"), 1)
            link(dve.tensor_copy(tcol[:, 0:NB], bank(0, 0, NB)))
            dve.tensor_copy(tcol_u[:, 0:NB], tcol[:, 0:NB]).then_inc(sem("steps"), 1)
            link(dve.tensor_tensor(wcol[:, 0:NB], icol[:, 0:NB], tcol[:, 0:NB], ALU.subtract))
            link(dve.tensor_scalar(wcol[:, 0:NB], wcol[:, 0:NB], float(NW - 1), float(P), ALU.min, ALU.mult))
            w2 = NSP // 2
            for h in range(2):
                dve.tensor_tensor(cmp[0:1, h * w2:(h + 1) * w2], iota_s[0:1, h * w2:(h + 1) * w2], bank(1 + h, 0, w2)[0:1, :], ALU.subtract).then_inc(sem("t_row"), 1)
            dve.wait_ge(sem("t_row"), 2)
            link(dve.tensor_scalar(wrow[:, :], cmp[0:1, :], float(NW - 1), None, ALU.min))
            dve.sem_inc(sem("tcol_sb"), 1)

            with dve.Fori(0, NW // 7) as it:
                for u in range(7):
                    t = it * 7 + u
                    dve.tensor_scalar(nodes[:, ds(t * D, D)], nodes[:, ds(t * D, D)], mv[:, ds(t * 2, 1)], rstd[:, ds(t, 1)],
                                      ALU.subtract, ALU.mult).then_inc(sem("xn_made"), 1)

            dve.wait_ge(sem("rows_in"), 32 * NB)
            link(dve.tensor_copy(absR[:, :], dg_i))
            link(dve.tensor_copy(sg_f, sg_i))
            for b in range(NB):
                ins = dve.tensor_scalar(relR[:, b * P:(b + 1) * P], absR[:, b * P:(b + 1) * P], wcol[:, b:b + 1], None, ALU.subtract)
            ins.then_inc(sem("rows_made"), 1)
            dve.wait_ge(sem("step_T"), 1)
            link(dve.tensor_copy(relC[:, :], ps[:, 0:NSP]))
            dve.wait_ge(sem("step_T"), 2)
            dve.tensor_copy(srcC[:, :], ps[:, 1024:1024 + NSP]).then_inc(sem("srcC_made"), 1)
            dve.wait_ge(sem("srcC_made"), 1)
            dve.tensor_copy(relB, relR[:, :]).then_inc(sem("relB_made"), 1)

            for k in range(2):
                dve.memset(xs[k][:, D:D + 1], 1.0)
            dve.memset(zero_g, 0.0).then_inc(sem("gram0"), 1)
            histogram(HI1, HI - HI1)

            dve.wait_ge(sem("hist_ps"), done(HT // G - 1))
            link(dve.tensor_copy(r4[:, :], bank(4, 0, NK)))
            r4v = r4[:, :].rearrange("p (w k) -> p w k", k=NTYPE)
            link(dve.tensor_reduce(count, r4v, AX_X, ALU.add))
            link(dve.tensor_scalar(count, count, 1.0, None, ALU.max))
            link(dve.reciprocal(count, count))
            dve.tensor_tensor(r4v, r4v, count.unsqueeze(2).broadcast_to([P, NW, NTYPE]), ALU.mult).then_inc(sem("r4_made"), 1)

            dve.wait_ge(sem("w_in"), 176)
            dve.wait_ge(sem("xn_stored"), 1)

            def evacuate(t, k):
                dve.wait_ge(sem("qk_ps"), done(t))
                dve.tensor_tensor(nodes[:, ds(t * D, D)], bank(4 + k, 0, D), b_gnn[:, 0:D], ALU.add)
                dve.wait_ge(sem("stored"), reuse(t, 2))
                dve.tensor_tensor(kS[k], bank(4 + k, D, 2 * D), b_gnn[:, D:2 * D], ALU.add).then_inc(sem("qk_sb"), 1)
            with dve.Fori(0, NW // 2) as it:
                for k in range(2):
                    evacuate(it * 2 + k, k)
            evacuate(NW - 1, 0)

            dve.wait_ge(sem("gram_ps"), done(NW - 1))
            dve.tensor_copy(g_G[:, 0, :], bank(6, 0, D + 1))
            dve.tensor_copy(g_G[:, 1, :], bank(7, 0, D + 1)).then_inc(sem("att_sb"), 1)
            dve.wait_ge(sem("att_ps"), 1)
            dve.tensor_copy(g_s, bank(6, 0, D)[0:1, :]).then_inc(sem("att_sb"), 1)
            dve.wait_ge(sem("att_ps"), 2)
            dve.scalar_tensor_tensor(out=g_t, in0=b_mix[0:1, 2 * D:3 * D], scalar=float(N), in1=bank(7, 0, D)[0:1, :], op0=ALU.mult, op1=ALU.add)
            dve.wait_ge(sem("att_ps"), 3)
            dve.tensor_copy(g_U, bank(4).rearrange("p (i e) -> p i e", i=2)).then_inc(sem("att_sb"), 1)
            dve.wait_ge(sem("att_ps"), 4)
            dve.tensor_copy(gramK[:, :], bank(5, 0, 2 * P)).then_inc(sem("att_sb"), 1)
            dve.wait_ge(sem("stored"), done(NW - 1))

            dve.wait_ge(sem("att_sb"), 4)
            for i in range(2):
                for h in range(2):
                    r = slice(C * h, C * (h + 1))
                    ins = dve.tensor_copy(a_sm[r, i * C:(i + 1) * C], gramK[r, i * P + C * h:i * P + C * (h + 1)])
            link(ins)
            a3 = a_sm.rearrange("p (i c) -> p i c", i=2)
            link(dve.tensor_reduce(a_v[0], a3, AX_X, ALU.max))
            dve.tensor_scalar(a_v[1], a_v[0], -1.0 / C ** 0.5, None, ALU.mult).then_inc(sem("a_neg"), 1)
            link(dve.memset(a_bd, 0.0))
            dve.wait_ge(sem("a_exp"), 2)
            link(dve.reciprocal(a_v[3], a_v[2]))
            for i in range(2):
                for h in range(2):
                    r = slice(C * h, C * (h + 1))
                    ins = dve.tensor_scalar(a_bd[r, i * P + C * h:i * P + C * (h + 1)], a_sm[r, i * C:(i + 1) * C], a_v[3][r, i:i + 1], None, ALU.mult)
            ins.then_inc(sem("att_sb"), 1)
            dve.wait_ge(sem("att_ps"), 5)
            dve.tensor_copy(a_wT, bank(2))
            dve.tensor_copy(a_bT, bank(3, 0, 2 * P))
            dve.tensor_copy(m_col[:, 0:2 * NF + NM], bank(3, 2 * P, 2 * P + 2 * NF + NM))
            dve.wait_ge(sem("att_ps"), 6)
            dve.tensor_copy(a_T, bank(0, 0, 2 * P)).then_inc(sem("att_sb"), 1)
            dve.wait_ge(sem("att_ps"), 7)
            dve.tensor_copy(w_qf, bank(1).rearrange("p (a d) -> p a d", a=2))
            dve.tensor_copy(b_mix[:, 0:D], bank(0, D, 2 * D)).then_inc(sem("att_sb"), 1)
            dve.wait_ge(sem("att_sb"), 7)
            dve.sem_inc(sem("att_used"), 1)
            dve.wait_ge(sem("mix_in"), 96)
            link(dve.tensor_tensor(b_gnn[:, 0:D], b_gnn[:, 0:D], b_gnn[:, 3 * D:4 * D], ALU.add))

            def chained(name, base):
                state = [0]

                def add(ins):
                    state[0] += 1
                    ins.then_inc(sem(name), 1)
                    dve.wait_ge(sem(name), base + state[0])
                return add, state

            def mix_out(g, b, n):
                dve.wait_ge(sem("fc2_ps"), done(g))
                dve.tensor_tensor(m_x1[:, 0:n * D], ps[:, 6 * 512:6 * 512 + n * D], m_x[b][:, 0:n * D], ALU.add).then_inc(sem("m_out"), 1)

            def mix(g, b, p, n, go, before):
                if p == 0 and before:
                    mix_out(g - 1, 1 - b, before)
                    if isinstance(g, int) and g == NG - 1:
                        dve.wait_ge(sem("m_out"), done(g - 1))
                        dve.memset(m_x[1 - b][:, 0:D], 0.0).then_inc(sem("m_x_zero"), 1)
                three = lambda t: t[:, 0:n * D].rearrange("p (t d) -> p t d", d=D)
                brow = lambda row: row.unsqueeze(1).broadcast_to([P, n, D])
                if p == 1:
                    dve.wait_ge(sem("x1_ps"), done(g))
                    dve.wait_ge(sem("res_stored"), reuse(g, 1))
                    go(dve.tensor_tensor(m_x1[:, 0:n * D], ps[:, 6 * 512:6 * 512 + n * D], m_xn[b][:, 0:n * D], ALU.add))
                    go(dve.tensor_tensor(three(m_x1), three(m_x1), brow(b_mix[:, 0:D]), ALU.add))
                    for t in range(n):
                        ins = dve.bn_stats(m_st[:, t * 6:(t + 1) * 6], m_x1[:, t * D:(t + 1) * D])
                    go(ins)
                    dve.memset(spare[:, 1:2], 0.0)
                    for t in range(n):
                        ins = dve.bn_aggr(m_mv[:, t * 2:(t + 1) * 2], m_st[:, t * 6:(t + 1) * 6])
                    go(ins)
                    dve.tensor_scalar(m_rs[:, 0:n], m_mv[:, 0:2 * n].rearrange("p (t c) -> p c t", c=2)[:, 1, :], EPS, None, ALU.add).then_inc(sem("m_var"), 1)
                    dve.wait_ge(sem("m_pT_ps"), done(g))
                    for i in range(NF):
                        ins = dve.tensor_tensor(m_pT[:, i * TG * P:i * TG * P + n * P], bank(4 + i, 0, n * P), m_T[:, i * TG * P:i * TG * P + n * P], ALU.add)
                    ins.then_inc(sem("m_pT_sb"), 1)
                if p == 2:
                    dve.wait_ge(sem("m_std"), done(g))
                    go(dve.reciprocal(m_rs[:, 0:n], m_rs[:, 0:n]))
                    for t in range(n):
                        ins = dve.tensor_scalar(m_xn[b][:, t * D:(t + 1) * D], m_x1[:, t * D:(t + 1) * D], m_mv[:, 2 * t:2 * t + 1], m_rs[:, t:t + 1], ALU.subtract, ALU.mult)
                    ins.then_inc(sem("m_z"), 1)
                    dve.wait_ge(sem(f"mix_rows{b}"), (g - b) * 16 + 32)
                    go(dve.tensor_tensor(m_x[b][:, 0:n * D], m_x[b][:, 0:n * D], m_x1[:, 0:n * D], ALU.add))
                    if before:
                        dve.wait_ge(sem("v_out"), g * 16)
                    dve.wait_ge(sem("v_ps"), done(g))
                    dve.tensor_tensor(three(m_v), ps[:, 6 * 512:6 * 512 + n * D].rearrange("p (t d) -> p t d", d=D), brow(b_gnn[:, 2 * D:3 * D]),
                                      ALU.add).then_inc(sem("v_sb"), 1)
                if p == 3:
                    dve.wait_ge(sem("m_hT_ps"), done(g))
                    for i in range(NF):
                        ins = dve.tensor_scalar(m_hT[:, i * TG * P:i * TG * P + n * P], bank(4 + i, 0, n * P), m_col[:, i:i + 1], m_col[:, NF + i:NF + i + 1], ALU.mult, ALU.add)
                    ins.then_inc(sem("m_hT_sb"), 1)
                if p == 4:
                    go(dve.tensor_tensor(three(m_x[b]), three(m_x[b]), brow(b_gnn[:, 0:D]), ALU.add))

            def take_idx(m, b):
                dve.tensor_copy(idx[b], srcC[:, ds(m * G, G)]).then_inc(sem("idx_made"), 1)
            take_idx(0, 0)
            take_idx(1, 1)

            def one_hots(j, b, m):
                dve.wait_ge(sem(f"relq_in{b}"), m * 16 + 16)
                dve.tensor_scalar(oh[b], relq[b], iota_p[:, 0:1], None, ALU.is_equal).then_inc(sem("oh_made"), 1)

            def scores(j, b, m):
                for h in range(2):
                    dve.wait_ge(sem(f"kv_in{2 * b + h}"), m * (16 * HG) + 16 * HG)
                    dve.wait_ge(sem("qg_ps"), done(j * 2 + h))
                    dve.tensor_tensor(kv[2 * b + h][:, :, 0:D], kv[2 * b + h][:, :, 0:D],
                                      ps[:, 1024 * h:1024 * (h + 1)].rearrange("p (g d) -> p g d", g=4), ALU.mult).then_inc(sem("prod_made"), 1)
                for h in range(2):
                    dve.wait_ge(sem("prod_made"), done(j * 2 + h))
                    dve.tensor_reduce(alpha[:, ds((j * 2 + h) * (4 * H), 4 * H)].rearrange("p (g h) -> p g h", g=HG),
                                      kv[2 * b + h][:, :, 0:D].rearrange("p g (h c) -> p g h c", c=C), AX_X, ALU.add).then_inc(sem("kv_used"), 1)

            def pass1(g, b, n, before=TG):
                go, state = chained("mchain", g * 7)
                for p in range(PIECES):
                    if not (isinstance(g, int) and g == NG) or p < PIECES - 1:
                        one_hots(g * PIECES + (p + 1), (p + 1) % 2, g * (PIECES // 2) + (p + 1) // 2)
                    if isinstance(g, int) and g == NG and p >= PIECES - 2:
                        take_idx(p + 2 - PIECES, (p + 2) % 4)
                    else:
                        take_idx(g * PIECES + (p + 2), (p + 2) % 4)
                    scores(g * PIECES + p, p % 2, g * (PIECES // 2) + p // 2)
                    mix(g, b, p, n, go, before)
                assert state[0] == 7
            one_hots(0, 0, 0)
            pass1(0, 0, TG, 0)
            with dve.Fori(0, NG // 2 - 1) as it:
                for b in range(2):
                    pass1(it * 2 + (b + 1), 1 - b, TG)
            pass1(NG - 1, 1, TG)
            pass1(NG, 0, 1)
            mix_out(NG, 0, 1)
            dve.memset(alpha[:, NGR * G * H:NSP * H], 0.0).then_inc(sem("alpha_pad"), 1)

            dve.wait_ge(sem("res_out"), 16 * (NG + 1))
            link(dve.tensor_scalar(slot_n(10), relR[:, :], 0.0, None, ALU.is_lt))
            link(dve.scalar_tensor_tensor(out=slot_n(10), in0=relR[:, :], scalar=float(P - 1), in1=slot_n(10), op0=ALU.is_gt, op1=ALU.add))
            link(dve.tensor_scalar(slot_n(10), slot_n(10), BIG_NEG, None, ALU.mult))
            inv = slot_n(10)
            fresh = slot_n(11)
            ab = absR[:, :].rearrange("p (b e) -> p b e", b=NB)
            fr = fresh.rearrange("p (b e) -> p b e", b=NB)
            link(dve.tensor_tensor(fr[:, :, 1:P], ab[:, :, 1:P], ab[:, :, 0:P - 1], ALU.not_equal))
            link(dve.memset(fr[:, :, 0:1], 1.0))
            link(dve.tensor_scalar(penR.rearrange("p (h x) -> p h x", h=H), fresh.unsqueeze(1).broadcast_to([P, H, NSP]), BIG_NEG, None, ALU.mult))
            link(dve.memset(rows[:, 4 * RW:4 * RW + 1], BIG_NEG))
            for h in range(H):
                dve.wait_ge(sem("row_turn"), h + 1)
                link(dve.scalar_tensor_tensor(out=atR[:, h * NSP:(h + 1) * NSP], in0=ps[:, 1024 * h:1024 * h + NSP], scalar=1.0 / C ** 0.5,
                                              in1=inv, op0=ALU.mult, op1=ALU.add))

            def scans():
                link(dve.tensor_tensor_scan(fwR, penR, atR, BIG_NEG, ALU.add, ALU.max))
                link(dve.tensor_tensor_scan(bwR[:, ::-1], penN[:, ::-1], atR[:, ::-1], BIG_NEG, ALU.add, ALU.max))
            scans()
            av = atR.rearrange("p (h b e) -> p b h e", h=H, b=NB)
            fv = fwR.rearrange("p (h b e) -> p b h e", h=H, b=NB)
            bv_ = bwR.rearrange("p (h b e) -> p b h e", h=H, b=NB)
            ev = [e.rearrange("p (b h) -> p b h", b=NB) for e in ends]
            sv = [e.rearrange("p (b h) -> p b h", b=NB) for e in saved]
            dve.tensor_copy(ev[0], fv[:, :, :, P - 1])
            dve.tensor_copy(ev[1], bv_[:, :, :, 0])
            dve.tensor_copy(sv[0], av[:, :, :, 0])
            dve.tensor_copy(sv[1], av[:, :, :, P - 1])
            dve.tensor_copy(ev[2], ab[:, :, 0:1].broadcast_to([P, NB, H]))
            dve.tensor_copy(ev[3], ab[:, :, P - 1:P].broadcast_to([P, NB, H])).then_inc(sem("seg_dve"), 1)
            dve.wait_ge(sem("seg_ps"), 1)
            lm, fm, d0, de, cont, chain, fsc, bsc = [line(i) for i in range(8)]
            for i in range(4):
                link(dve.tensor_copy(line(i), ps[0:H, 1024 * i:1024 * i + NSP]))
            Z = NSP - 1
            link(dve.memset(cont, 0.0))
            link(dve.tensor_tensor(cont[:, 1:NSP], d0[:, 1:NSP], de[:, 0:Z], ALU.is_equal))
            link(dve.tensor_tensor(d0, d0, de, ALU.is_equal))
            link(dve.tensor_tensor(chain, d0, cont, ALU.mult))
            link(dve.tensor_scalar(chain, chain, -BIG_NEG, BIG_NEG, ALU.mult, ALU.add))
            link(dve.tensor_tensor_scan(fsc, chain, lm, BIG_NEG, ALU.add, ALU.max))
            link(dve.memset(chain, 0.0))
            link(dve.tensor_tensor(chain[:, 0:Z], d0[:, 0:Z], cont[:, 1:NSP], ALU.mult))
            link(dve.tensor_scalar(chain, chain, -BIG_NEG, BIG_NEG, ALU.mult, ALU.add))
            link(dve.tensor_tensor_scan(bsc[:, ::-1], chain[:, ::-1], fm[:, ::-1], BIG_NEG, ALU.add, ALU.max))
            link(dve.tensor_scalar(cont, cont, -BIG_NEG, BIG_NEG, ALU.mult, ALU.add))
            dve.memset(carry[0], BIG_NEG)
            link(dve.memset(carry[1], BIG_NEG))
            dve.tensor_tensor(carry[0][:, 1:NSP], fsc[:, 0:Z], cont[:, 1:NSP], ALU.add)
            dve.tensor_tensor(carry[1][:, 0:Z], bsc[:, 1:NSP], cont[:, 1:NSP], ALU.add).then_inc(sem("seg_dve"), 1)
            dve.wait_ge(sem("seg_ps"), 2)
            for i, e in ((0, 0), (1, P - 1)):
                link(dve.tensor_tensor(av[:, :, :, e], sv[i], bank(i, 0, NB * H).rearrange("p (b h) -> p b h", b=NB), ALU.max))
            dve.sem_inc(sem("seg_dve"), 1)
            scans()
            link(dve.tensor_tensor(fwR, fwR, bwR, ALU.max))
            for i, e in ((0, 0), (1, P - 1)):
                link(dve.tensor_copy(av[:, :, :, e], sv[i]))
            dve.tensor_tensor(atR, atR, fwR, ALU.subtract).then_inc(sem("seg_dve"), 1)
            dve.memset(zeros, 0.0)
            link(dve.tensor_copy(base_f, wrow[0:1, :].rearrange("p (i g) -> p i g", g=HG)[:, :, 0]))
            link(dve.tensor_scalar(base_f, base_f, float(NW - HG), None, ALU.min))
            link(dve.tensor_copy(base_w, base_f))
            dve.tensor_tensor(slot_w.rearrange("p (i g) -> p i g", g=HG), wrow[0:1, :].rearrange("p (i g) -> p i g", g=HG),
                              base_f.unsqueeze(2).broadcast_to([1, NSP // HG, HG]), ALU.subtract).then_inc(sem("slots_made"), 1)
            dve.wait_ge(sem("slots_made"), 1)
            for h in range(H):
                dve.wait_ge(sem("col_turn"), h + 1)
                ins = dve.tensor_copy(alpha[:, :].rearrange("p (s h) -> p h s", h=H)[:, h, :], ps[:, 1024 * h:1024 * h + NSP])
            ins.then_inc(sem("ex_cols"), 1)
            dve.wait_ge(sem("ex_cols"), 1)
            dve.wait_ge(sem("acc_zero"), 1)

            def weigh(i, b, m):
                dve.tensor_tensor(ohh[b].rearrange("p (g n) -> p g n", g=HG), relC[:, ds(i * HG, HG)].unsqueeze(2).broadcast_to([P, HG, P]),
                                  iota_f[:, :].unsqueeze(1).broadcast_to([P, HG, P]), ALU.is_equal)
                dve.wait_ge(sem(f"kv_in{b}"), m * (16 * HG) + (NHF // KV * 16 * HG + 16 * HG))
                v4 = kv[b][:, :, 0:D].rearrange("p g (h c) -> p g h c", h=H)
                dve.tensor_tensor(v4, v4, alpha[:, ds(i * (HG * H), HG * H)].rearrange("p (g h) -> p g h", g=HG).unsqueeze(3).broadcast_to([P, HG, H, C]),
                                  ALU.mult).then_inc(sem("oh2_made"), 1)

            def add_up(i, b):
                _, base = nc.values_load_multi_w_load_instructions(base_w[0:1, ds(i, 1)], engines=(dve.engine,), min_val=0, max_val=NW - HG)
                dve.wait_ge(sem("agg_ps"), done(i))
                dve.sem_inc(sem("kv_used"), 1)
                dve.wait_ge(sem("acc_made"), done(i - 1))
                acc = nodes[:, ds(base[0] * AC, HG * AC)].rearrange("p (s a) -> p s a", s=HG)
                dve.tensor_tensor(acc, acc, ps[:, 2048 * (b % 2):2048 * (b % 2 + 1)].rearrange("p (s a) -> p s a", s=HG)[:, :, 0:AC], ALU.add).then_inc(sem("acc_made"), 1)
            U = 2 * KV
            weigh(0, 0, 0)
            with dve.Fori(0, NHF // U - 1) as it:
                for c in range(U):
                    if c % 2 == 0:
                        take_idx(it * (U // 2) + (c // 2 + 2), (c // 2 + 2) % 4)
                    weigh(it * U + (c + 1), (c + 1) % KV, it * (U // KV) + (c + 1) // KV)
                    add_up(it * U + c, c % KV)
            for c in range(U):
                i = NHF - U + c
                if c in (0, 2):
                    take_idx(i // 2 + 2, (c // 2 + 2) % 4)
                if c < U - 1:
                    weigh(i + 1, (c + 1) % KV, (i + 1) // KV)
                add_up(i, c % KV)
            dve.wait_ge(sem("acc_made"), done(NHF - 1))

            dve.wait_ge(sem("par_turn"), 1)
            for l in range(2):
                link(dve.tensor_copy(e_par[l], bank(2, l * 80, (l + 1) * 80)))
                ins = dve.tensor_scalar(e_sc[l], e_par[l][:, 64:80], 0.001, None, ALU.add)
            ins.then_inc(sem("e_var"), 1)
            dve.wait_ge(sem("e_std"), 1)
            for l in range(2):
                pg, pb, pbe, pm = [e_par[l][:, 16 * i:16 * (i + 1)] for i in range(4)]
                link(dve.reciprocal(e_sc[l], e_sc[l]))
                link(dve.tensor_tensor(e_sc[l], e_sc[l], pg, ALU.mult))
                link(dve.tensor_tensor(e_sh[l], pb, pm, ALU.subtract))
                link(dve.tensor_tensor(e_sh[l], e_sh[l], e_sc[l], ALU.mult))
                link(dve.tensor_tensor(e_sh[l], e_sh[l], pbe, ALU.add))
            dve.sem_inc(sem("e_ready"), 1)

            def first_part(g, b, m, n, q, go):
                y = f_y[b]
                av = nodes[:, ds(g * (T2 * AC), n * AC)].rearrange("p (t a) -> p t a", a=AC)
                l3 = f_lg[:, 0:n * NE].rearrange("p (t e) -> p t e", e=NE)
                if q == 0:
                    go(dve.tensor_scalar(f_rc[:, 0:n * H].rearrange("p (t h) -> p t h", h=H), av[:, :, D:AC], 1e-16, None, ALU.add))
                    go(dve.reciprocal(f_rc[:, 0:n * H], f_rc[:, 0:n * H]))
                    dve.wait_ge(sem("y_stored"), reuse(g, 2))
                    go(dve.tensor_tensor(y[:, 0:n * D].rearrange("p (t h c) -> p t h c", t=n, h=H), av[:, :, 0:D].rearrange("p t (h c) -> p t h c", h=H),
                                         f_rc[:, 0:n * H].rearrange("p (t h) -> p t h", h=H).unsqueeze(3).broadcast_to([P, n, H, C]), ALU.mult))
                    dve.wait_ge(sem(f"res_in{b}"), m * 16 + 16)
                    go(dve.tensor_tensor(y[:, 0:n * D], y[:, 0:n * D], f_res[b][:, 0:n * D], ALU.add))
                    for t in range(n):
                        ins = dve.bn_stats(f_st[:, t * 6:(t + 1) * 6], y[:, t * D:(t + 1) * D])
                    go(ins)
                    dve.memset(spare[:, 1:2], 0.0)
                    for t in range(n):
                        ins = dve.bn_aggr(f_mv[:, t * 2:(t + 1) * 2], f_st[:, t * 6:(t + 1) * 6])
                    go(ins)
                    dve.tensor_scalar(f_rs[:, 0:n], f_mv[:, 0:2 * n].rearrange("p (t c) -> p c t", c=2)[:, 1, :], EPS, None, ALU.add).then_inc(sem("f_var"), 1)
                if q == 2:
                    dve.wait_ge(sem("f_std"), done(g))
                    go(dve.reciprocal(f_rs[:, 0:n], f_rs[:, 0:n]))
                    for t in range(n):
                        ins = dve.tensor_scalar(f_z[:, t * D:(t + 1) * D], y[:, t * D:(t + 1) * D], f_mv[:, 2 * t:2 * t + 1], f_rs[:, t:t + 1], ALU.subtract, ALU.mult)
                    ins.then_inc(sem("f_z_made"), 1)
                if q == 3:
                    dve.wait_ge(sem("f_T_sb"), done(g))
                    for i in range(NF):
                        o = slice(i * T2 * P, i * T2 * P + n * P)
                        ins = dve.tensor_tensor(f_T[b][1][:, o], f_zT[:, o], f_T[b][0][:, o].bitcast(F32), ALU.subtract)
                    ins.then_inc(sem("f_T_lo"), 1)
                if q == 4:
                    dve.wait_ge(sem("lg_ps"), done(g))
                    go(dve.tensor_tensor(l3, bank(7, 0, n * NE).rearrange("p (t e) -> p t e", e=NE), e_br.unsqueeze(1).broadcast_to([P, n, NE]), ALU.add))
                    go(dve.tensor_reduce(f_m[:, 0:n], l3, AX_X, ALU.max))
                    dve.tensor_tensor(l3, l3, f_m[:, 0:n].unsqueeze(2).broadcast_to([P, n, NE]), ALU.subtract).then_inc(sem("f_sub"), 1)
                if q == 5:
                    dve.wait_ge(sem("f_exp"), done(g))
                    go(dve.tensor_reduce(f_m[:, 0:n], l3, AX_X, ALU.add))
                    go(dve.reciprocal(f_m[:, 0:n], f_m[:, 0:n]))
                    dve.tensor_tensor(f_w[b][:, 0:n * NE].rearrange("p (t e) -> p t e", e=NE), l3, f_m[:, 0:n].unsqueeze(2).broadcast_to([P, n, NE]), ALU.mult).then_inc(sem("f_w_made"), 1)
                if q == 7:
                    dve.wait_ge(sem("bo_ps"), done(g))
                    dve.tensor_tensor(y[:, 0:n * D], ps[:, 6 * 512:6 * 512 + n * D], y[:, 0:n * D], ALU.add).then_inc(sem("y_init"), 1)

            def lower(l, u, e, n):
                up, lo = [spread(t, n) for t in f_h[l][e % 2]]
                whole = spread(f_whole[l], n)
                if l == 0:
                    dve.wait_ge(sem("h1_up"), done(u))
                else:
                    dve.wait_ge(sem("h2_sb"), done(u))
                    dve.tensor_copy(up, whole).then_inc(sem("h2_up"), 1)
                    dve.wait_ge(sem("h2_up"), done(u))
                dve.tensor_tensor(lo, whole, up.bitcast(F32), ALU.subtract).then_inc(sem(("h1_lo", "h2_lo")[l]), 1)

            def experts(g, b, m, n, nxt):
                go, state = chained("fchain", (g + 1) * 11)
                for e in range(NE):
                    u = g * NE + e
                    if e + 2 < NE or nxt:
                        lower(0, u + 2, (e + 2) % NE, n if e + 2 < NE else nxt)
                    if e + 1 < NE or nxt:
                        lower(1, u + 1, (e + 1) % NE, n if e + 1 < NE else nxt)
                    if e == 0:
                        dve.wait_ge(sem("y_init"), done(g))
                    dve.wait_ge(sem("l3_ps"), done(u))
                    dve.wait_ge(sem("y_made"), done(u - 1))
                    for t in range(n):
                        yt = f_y[b][:, t * D:(t + 1) * D]
                        ins = dve.scalar_tensor_tensor(out=yt, in0=bank(4 + e % 2, t * D, (t + 1) * D), scalar=f_w[b][:, t * NE + e:t * NE + e + 1],
                                                       in1=yt, op0=ALU.mult, op1=ALU.add)
                    ins.then_inc(sem("y_made"), 1)
                    if nxt:
                        first_part(g + 1, 1 - b, m + b, nxt, e, go)
                assert state[0] in (0, 11)
            go, _ = chained("fchain", 0)
            for q in range(NE):
                first_part(0, 0, 0, T2, q, go)
                if q in (2, 3, 5):
                    l = (2, 3, 5).index(q)
                    dve.wait_ge(sem("e_upper"), l + 1)
                    link(dve.tensor_tensor(e_lower[:, WE * l:WE * (l + 1)], e_w[l], e_upper[:, WE * l:WE * (l + 1)].bitcast(F32), ALU.subtract))
                    dve.sem_inc(sem("e_ready"), 1)
            lower(0, 0, 0, T2)
            lower(0, 1, 1, T2)
            lower(1, 0, 0, T2)
            with dve.Fori(0, NG2 // 2 - 1) as it:
                for b in range(2):
                    experts(it * 2 + b, b, it, T2, T2)
            experts(NG2 - 2, 0, NG2 // 2 - 1, T2, T2)
            experts(NG2 - 1, 1, NG2 // 2 - 1, T2, 1)
            experts(NG2, 0, NG2 // 2, 1, 0)


_INS = ['x', 'src', 'dst', 'edge_type_4', 'L0_gnn_edge_emb', 'L0_gnn_Wq', 'L0_gnn_bq', 'L0_gnn_Wk', 'L0_gnn_bk', 'L0_gnn_Wv',
        'L0_gnn_bv', 'L0_gnn_Ws', 'L0_gnn_bs', 'L0_mix_w_qkv', 'L0_mix_b_qkv', 'L0_mix_norm_g', 'L0_mix_norm_b', 'L0_mix_w_fc1',
        'L0_mix_b_fc1', 'L0_mix_w_fc2', 'L0_mix_b_fc2', 'L0_ffn_Wr', 'L0_ffn_br', 'L0_ffn_W1', 'L0_ffn_b1', 'L0_ffn_g1',
        'L0_ffn_be1', 'L0_ffn_m1', 'L0_ffn_v1', 'L0_ffn_W2', 'L0_ffn_b2', 'L0_ffn_g2', 'L0_ffn_be2', 'L0_ffn_m2', 'L0_ffn_v2',
        'L0_ffn_Wo', 'L0_ffn_bo']
_OUTS = [((6250, 256), 'float32')]


def kernel(**inputs):
    import numpy as _np
    import concourse.bacc as _bacc
    from concourse import mybir as _mybir
    from concourse.bass_utils import run_bass_kernel_spmd as _run

    nc = _bacc.Bacc("TRN2", target_bir_lowering=False, num_devices=1)
    arrays, args = {}, []
    for name in _INS:
        a = _np.ascontiguousarray(inputs[name])
        arrays[f"in_{name}_dram"] = a
        args.append(nc.dram_tensor(f"in_{name}_dram", a.shape, _mybir.dt.from_np(a.dtype), kind="ExternalInput").ap())
    for i, (shape, dtype) in enumerate(_OUTS):
        dt = _mybir.dt.from_np(_np.dtype(dtype))
        args.append(nc.dram_tensor(f"out_{i}_dram", shape, dt, kind="ExternalOutput").ap())
    gps_layer_kernel(nc, *args)
    r = _run(nc, [arrays], core_ids=[0])
    got = tuple(r.results[0][f"out_{i}_dram"] for i in range(len(_OUTS)))
    return got[0]
```
